# Optimizing a Trainium2 kernel written in Bass

```python
import numpy as np
import jax
import jax.numpy as jnp

def _softmax(x, axis=-1):
    return jax.nn.softmax(x, axis=axis)

def _gelu(x):
    return jax.nn.gelu(x, approximate=True)

def _silu(x):
    return jax.nn.silu(x)

def _sigmoid(x):
    return jax.nn.sigmoid(x)

def _layernorm(x, axis=-1, eps=1e-05):
    m = jnp.mean(x, axis=axis, keepdims=True)
    v = jnp.var(x, axis=axis, keepdims=True)
    return (x - m) / jnp.sqrt(v + eps)

def _scatter_add(tgt, idx, src, axis=0):
    return tgt.at[idx].add(src)

def _segment_sum(src, seg, n):
    return jax.ops.segment_sum(src, seg, n)
kernel_name = 'mk_hybrid_d1_jaxref_r8_fd0317'

def setup_inputs(seed: int=0):
    np.random.seed(seed)
    _w = jnp.asarray

    def _L0_attn_a_setup():
        import jax, jax.numpy as jnp
        import numpy as np
        HIDDEN = 512
        NH = 32
        NKV = 8
        HD = 128
        GS = 128
        BASE = 10000.0
        B, S = (2, 256)

        def _dequant(codes, scales):
            w = codes.astype(jnp.float32) - 8.0
            return w * jnp.repeat(scales, GS, axis=0)

        def _rope(x):
            s, d = (x.shape[2], x.shape[3])
            pos = jnp.arange(s, dtype=jnp.float32)
            inv_freq = 1.0 / BASE ** (jnp.arange(0, d, 2, dtype=jnp.float32) / d)
            f = pos[:, None] * inv_freq[None, :]
            cos = jnp.cos(f)[None, None]
            sin = jnp.sin(f)[None, None]
            xe = x[..., ::2]
            xo = x[..., 1::2]
            re = xe * cos - xo * sin
            ro = xo * cos + xe * sin
            return jnp.stack([re, ro], axis=-1).reshape(x.shape)
        key = jax.random.key(seed)
        ks = jax.random.split(key, 9)

        def codes(k, i, o):
            return jax.random.randint(k, (i, o), 0, 16, dtype=jnp.int32)

        def scales(k, i, o):
            return jax.random.uniform(k, (i // GS, o), dtype=jnp.float32) * 0.02
        return {'hidden_states': jax.random.normal(ks[0], (B, S, HIDDEN), jnp.float32), 'q_codes': codes(ks[1], HIDDEN, NH * HD), 'q_scales': scales(ks[2], HIDDEN, NH * HD), 'k_codes': codes(ks[3], HIDDEN, NKV * HD), 'k_scales': scales(ks[4], HIDDEN, NKV * HD), 'v_codes': codes(ks[5], HIDDEN, NKV * HD), 'v_scales': scales(ks[6], HIDDEN, NKV * HD), 'o_codes': codes(ks[7], NH * HD, HIDDEN), 'o_scales': scales(ks[8], NH * HD, HIDDEN)}
    _L0_attn_a_in = _L0_attn_a_setup()

    def _L0_attn_b_setup():
        import math
        import jax, jax.numpy as jnp
        import numpy as np
        D_MODEL = 512
        N_HEADS = 32
        N_KV_HEADS = 8
        D_HEAD = D_MODEL // N_HEADS
        GROUP = N_HEADS // N_KV_HEADS
        ROPE = dict(rope_theta=500000.0, factor=32.0, hi_freq_factor=4.0, lo_freq_factor=1.0, original_context_length=1024)

        def _rope_cos_sin(head_dim, pos, dtype):
            idx = jnp.arange(0, head_dim, 2, dtype=jnp.float32) / head_dim
            freq = 1.0 / (2.0 * math.pi) * ROPE['rope_theta'] ** (-idx)
            factor, lo, hi = (ROPE['factor'], ROPE['lo_freq_factor'], ROPE['hi_freq_factor'])
            L0 = ROPE['original_context_length']
            freq_low, freq_high = (lo / L0, hi / L0)
            freq_scaled = jnp.where(freq < freq_low, freq / factor, freq)
            smooth = jnp.clip((L0 * freq - lo) / (hi - lo), 0.0, 1.0)
            freq_smooth = (1.0 - smooth) * (freq / factor) + smooth * freq
            is_mid = (freq >= freq_low) & (freq <= freq_high)
            freq = jnp.where(is_mid, freq_smooth, freq_scaled)
            phase = 2.0 * math.pi * pos.astype(jnp.float32)[:, None] * freq[None, :]
            emb = jnp.concatenate([phase, phase], axis=-1)
            return (jnp.cos(emb).astype(dtype), jnp.sin(emb).astype(dtype))

        def _rotate_half(x):
            h = x.shape[-1] // 2
            return jnp.concatenate([-x[..., h:], x[..., :h]], axis=-1)
        key = jax.random.key(seed)
        ks = jax.random.split(key, 5)
        B, T = (1, 256)
        s = 0.02
        return {'resid': jax.random.normal(ks[0], (B, T, D_MODEL), jnp.float32), 'Wq': jax.random.normal(ks[1], (D_MODEL, D_MODEL), jnp.float32) * s, 'Wk': jax.random.normal(ks[2], (D_MODEL, N_KV_HEADS * D_HEAD), jnp.float32) * s, 'Wv': jax.random.normal(ks[3], (D_MODEL, N_KV_HEADS * D_HEAD), jnp.float32) * s, 'Wo': jax.random.normal(ks[4], (D_MODEL, D_MODEL), jnp.float32) * s}
    _L0_attn_b_in = _L0_attn_b_setup()

    def _L0_ffn_setup():
        import jax, jax.numpy as jnp
        import numpy as np
        N_EXPERTS = 8
        TOP_K = 2
        D_MODEL = 512
        RANK = 64
        key = jax.random.key(seed)
        k0, k1, k2, k3 = jax.random.split(key, 4)
        inputs = jax.random.normal(k0, (4, 256, D_MODEL), dtype=jnp.float32)
        gate_w = jax.random.normal(k1, (N_EXPERTS, D_MODEL), dtype=jnp.float32) * 0.02
        lora_A = jax.random.normal(k2, (N_EXPERTS, RANK, D_MODEL), dtype=jnp.float32) * 0.02
        lora_B = jax.random.normal(k3, (N_EXPERTS, D_MODEL, RANK), dtype=jnp.float32) * 0.02
        return {'inputs': inputs, 'gate_w': gate_w, 'lora_A': lora_A, 'lora_B': lora_B}
    _L0_ffn_in = _L0_ffn_setup()
    _d = {'L0_attn_a_hidden_states': _L0_attn_a_in['hidden_states'], 'L0_attn_a_q_codes': _L0_attn_a_in['q_codes'], 'L0_attn_a_q_scales': _L0_attn_a_in['q_scales'], 'L0_attn_a_k_codes': _L0_attn_a_in['k_codes'], 'L0_attn_a_k_scales': _L0_attn_a_in['k_scales'], 'L0_attn_a_v_codes': _L0_attn_a_in['v_codes'], 'L0_attn_a_v_scales': _L0_attn_a_in['v_scales'], 'L0_attn_a_o_codes': _L0_attn_a_in['o_codes'], 'L0_attn_a_o_scales': _L0_attn_a_in['o_scales'], 'L0_attn_b_Wq': _L0_attn_b_in['Wq'], 'L0_attn_b_Wk': _L0_attn_b_in['Wk'], 'L0_attn_b_Wv': _L0_attn_b_in['Wv'], 'L0_attn_b_Wo': _L0_attn_b_in['Wo'], 'L0_ffn_gate_w': _L0_ffn_in['gate_w'], 'L0_ffn_lora_A': _L0_ffn_in['lora_A'], 'L0_ffn_lora_B': _L0_ffn_in['lora_B']}
    _x0 = _d['L0_attn_a_hidden_states']
    _d['L0_attn_a_hidden_states'] = jax.random.normal(jax.random.fold_in(jax.random.key(seed), 1), (2, 512, 512), dtype=_x0.dtype)
    del _x0
    return _d

def reference(L0_attn_a_hidden_states, L0_attn_a_q_codes, L0_attn_a_q_scales, L0_attn_a_k_codes, L0_attn_a_k_scales, L0_attn_a_v_codes, L0_attn_a_v_scales, L0_attn_a_o_codes, L0_attn_a_o_scales, L0_attn_b_Wq, L0_attn_b_Wk, L0_attn_b_Wv, L0_attn_b_Wo, L0_ffn_gate_w, L0_ffn_lora_A, L0_ffn_lora_B):

    def _L0_attn_a_ref(hidden_states, q_codes, q_scales, k_codes, k_scales, v_codes, v_scales, o_codes, o_scales):
        import jax, jax.numpy as jnp
        import numpy as np
        HIDDEN = 512
        NH = 32
        NKV = 8
        HD = 128
        GS = 128
        BASE = 10000.0
        B, S = (2, 256)

        def _dequant(codes, scales):
            w = codes.astype(jnp.float32) - 8.0
            return w * jnp.repeat(scales, GS, axis=0)

        def _rope(x):
            s, d = (x.shape[2], x.shape[3])
            pos = jnp.arange(s, dtype=jnp.float32)
            inv_freq = 1.0 / BASE ** (jnp.arange(0, d, 2, dtype=jnp.float32) / d)
            f = pos[:, None] * inv_freq[None, :]
            cos = jnp.cos(f)[None, None]
            sin = jnp.sin(f)[None, None]
            xe = x[..., ::2]
            xo = x[..., 1::2]
            re = xe * cos - xo * sin
            ro = xo * cos + xe * sin
            return jnp.stack([re, ro], axis=-1).reshape(x.shape)
        b, s, _ = hidden_states.shape
        q = hidden_states @ _dequant(q_codes, q_scales)
        k = hidden_states @ _dequant(k_codes, k_scales)
        v = hidden_states @ _dequant(v_codes, v_scales)
        q = q.reshape(b, s, NH, HD).transpose(0, 2, 1, 3)
        k = k.reshape(b, s, NKV, HD).transpose(0, 2, 1, 3)
        v = v.reshape(b, s, NKV, HD).transpose(0, 2, 1, 3)
        q = _rope(q)
        k = _rope(k)
        rf = NH // NKV
        k = jnp.repeat(k, rf, axis=1)
        v = jnp.repeat(v, rf, axis=1)
        scale = HD ** (-0.5)
        causal = jnp.tril(jnp.ones((s, s), dtype=bool))
        mask = jnp.where(causal, 0.0, -jnp.inf).astype(q.dtype)
        scores = jnp.einsum('bhqd,bhkd->bhqk', q, k) * scale + mask[None, None]
        attn = jax.nn.softmax(scores, axis=-1)
        out = jnp.einsum('bhqk,bhkd->bhqd', attn, v)
        out = out.transpose(0, 2, 1, 3).reshape(b, s, NH * HD)
        return out @ _dequant(o_codes, o_scales)

    def _L0_attn_b_ref(resid, Wq, Wk, Wv, Wo):
        import math
        import jax, jax.numpy as jnp
        import numpy as np
        D_MODEL = 512
        N_HEADS = 32
        N_KV_HEADS = 8
        D_HEAD = D_MODEL // N_HEADS
        GROUP = N_HEADS // N_KV_HEADS
        ROPE = dict(rope_theta=500000.0, factor=32.0, hi_freq_factor=4.0, lo_freq_factor=1.0, original_context_length=1024)

        def _rope_cos_sin(head_dim, pos, dtype):
            idx = jnp.arange(0, head_dim, 2, dtype=jnp.float32) / head_dim
            freq = 1.0 / (2.0 * math.pi) * ROPE['rope_theta'] ** (-idx)
            factor, lo, hi = (ROPE['factor'], ROPE['lo_freq_factor'], ROPE['hi_freq_factor'])
            L0 = ROPE['original_context_length']
            freq_low, freq_high = (lo / L0, hi / L0)
            freq_scaled = jnp.where(freq < freq_low, freq / factor, freq)
            smooth = jnp.clip((L0 * freq - lo) / (hi - lo), 0.0, 1.0)
            freq_smooth = (1.0 - smooth) * (freq / factor) + smooth * freq
            is_mid = (freq >= freq_low) & (freq <= freq_high)
            freq = jnp.where(is_mid, freq_smooth, freq_scaled)
            phase = 2.0 * math.pi * pos.astype(jnp.float32)[:, None] * freq[None, :]
            emb = jnp.concatenate([phase, phase], axis=-1)
            return (jnp.cos(emb).astype(dtype), jnp.sin(emb).astype(dtype))

        def _rotate_half(x):
            h = x.shape[-1] // 2
            return jnp.concatenate([-x[..., h:], x[..., :h]], axis=-1)
        B, T, _ = resid.shape
        q = (resid @ Wq).reshape(B, T, N_HEADS, D_HEAD).transpose(0, 2, 1, 3)
        k = (resid @ Wk).reshape(B, T, N_KV_HEADS, D_HEAD).transpose(0, 2, 1, 3)
        v = (resid @ Wv).reshape(B, T, N_KV_HEADS, D_HEAD).transpose(0, 2, 1, 3)
        cos, sin = _rope_cos_sin(D_HEAD, jnp.arange(T), resid.dtype)
        cos = cos[None, None]
        sin = sin[None, None]
        q = q * cos + _rotate_half(q) * sin
        k = k * cos + _rotate_half(k) * sin
        qg = q.reshape(B, N_KV_HEADS, GROUP, T, D_HEAD)
        att = jnp.einsum('bhgqd,bhkd->bhgqk', qg.astype(jnp.float32), k.astype(jnp.float32)) / math.sqrt(D_HEAD)
        causal = jnp.tril(jnp.ones((T, T), dtype=bool))
        att = jnp.where(causal[None, None, None], att, -jnp.inf)
        probs = jax.nn.softmax(att, axis=-1).astype(resid.dtype)
        ctx = jnp.einsum('bhgqk,bhkd->bhgqd', probs, v)
        out = ctx.reshape(B, N_HEADS, T, D_HEAD).transpose(0, 2, 1, 3).reshape(B, T, D_MODEL)
        return out @ Wo

    def _L0_ffn_ref(inputs, gate_w, lora_A, lora_B):
        import jax, jax.numpy as jnp
        import numpy as np
        N_EXPERTS = 8
        TOP_K = 2
        D_MODEL = 512
        RANK = 64
        x = inputs.reshape(-1, inputs.shape[-1])
        T = x.shape[0]
        gate_probs = jax.nn.softmax(x @ gate_w.T, axis=-1)
        weights, sel = jax.lax.top_k(gate_probs, TOP_K)
        weights = weights / jnp.sum(weights, axis=-1, keepdims=True)
        w_full = jnp.zeros((T, N_EXPERTS), dtype=x.dtype).at[jnp.arange(T)[:, None], sel].add(weights)
        out = jnp.zeros((T, D_MODEL), dtype=x.dtype)
        for e in range(N_EXPERTS):
            y = x @ lora_A[e].T @ lora_B[e].T
            out = out + w_full[:, e:e + 1] * y
        return out.reshape(inputs.shape[:-1] + (D_MODEL,))
    x = L0_attn_a_hidden_states
    x = x + _L0_attn_a_ref(_layernorm(x, axis=-1), L0_attn_a_q_codes, L0_attn_a_q_scales, L0_attn_a_k_codes, L0_attn_a_k_scales, L0_attn_a_v_codes, L0_attn_a_v_scales, L0_attn_a_o_codes, L0_attn_a_o_scales)
    x = x + _L0_ffn_ref(_layernorm(x, axis=-1), L0_ffn_gate_w, L0_ffn_lora_A, L0_ffn_lora_B)
    x = x + _L0_attn_b_ref(_layernorm(x, axis=-1), L0_attn_b_Wq, L0_attn_b_Wk, L0_attn_b_Wv, L0_attn_b_Wo)
    x = x + _L0_ffn_ref(_layernorm(x, axis=-1), L0_ffn_gate_w, L0_ffn_lora_A, L0_ffn_lora_B)
    return x

_drawn_inputs = setup_inputs


def setup_inputs(seed=0):
    import zlib

    import numpy as np

    out = dict(_drawn_inputs(seed))
    spreads = {}
    factors = {'L0_attn_b_Wq': 8.0, 'L0_attn_b_Wk': 8.0}
    for name, (base, spread) in spreads.items():
        noise = np.random.default_rng([zlib.crc32(name.encode()), seed]).standard_normal(out[name].shape)
        drawn = base * np.exp(spread * noise) if base else spread * noise
        out[name] = jnp.asarray(drawn.astype(out[name].dtype))
    for name, factor in factors.items():
        out[name] = (out[name] * factor).astype(out[name].dtype)
    return out
```

```python
from contextlib import ExitStack

import numpy as np

import concourse.bass as bass
from concourse import mybir

F32 = mybir.dt.float32
F16 = mybir.dt.float16
BF16 = mybir.dt.bfloat16
I32 = mybir.dt.int32
U32 = mybir.dt.uint32
ALU = mybir.AluOpType
ACT = mybir.ActivationFunctionType
AX = mybir.AxisListType.X

P = 128
B, S, D = 2, 512, 512
TOK = B * S
NT = TOK // P
ST = S // P
KT = D // P
EPS = 1e-5

A_HEADS, KV_HEADS, A_HD = 32, 8, 128
GROUP = A_HEADS // KV_HEADS
B_HEADS, B_HD = 32, 16
B_ST = 4 * B_HD
EXPERTS, RANK = 8, 64

X_UP = 2.0 ** 10
W_UP = 2.0 ** 10
PROJ_DN = 2.0 ** -18
PROJ_DN_B = 2.0 ** -15
P_UP = 2.0 ** 15
MASKED = -1e30

S_OFF = [0, P, 3 * P, 6 * P]
TRI = 10 * P
S_BANK = [(0, 0), (1, 0), (0, P), (2, 0)]
S_ORDER = (0, 2, 1, 3)
O_BANK = [7, 6, 7, 6, 7, 5, 7, 5]
T_OFF = {0: 0, 1: S, 3: S + 3 * P, 2: 2 * S}

WEIGHTS = ("lora_a", "lora_b", "b_q", "b_kv", "b_o", "gate")
W_COLS = {"lora_a": KT * EXPERTS * RANK, "lora_b": KT * D, "b_q": KT * D, "b_kv": KT * 2 * KV_HEADS * B_HD,
          "b_o": KT * D, "gate": KT * EXPERTS}
QUANT = ("q", "k", "v", "o")
QUANT_COLS = {"q": P, "k": P // 4, "v": P // 4, "o": P}


def build(nc, t_in, out):
    ctx = ExitStack()
    with ctx:
        def sb(name, shape, dt):
            return ctx.enter_context(nc.sbuf_tensor(name, shape, dt))

        def sem(name):
            return ctx.enter_context(nc.semaphore(name))

        bank = [ctx.enter_context(nc.psum_tensor(f"bank{i}", [P, 512], F32)) for i in range(8)]

        x = sb("x", [P, NT, D], F32)
        xt_hi = sb("xt_hi", [P, KT, TOK], F16)
        xt_lo = sb("xt_lo", [P, KT, TOK], F16)
        xn = sb("xn", [P, 2, D], F32)
        ident = sb("ident", [P, P], F32)
        ident_h = sb("ident_h", [P, P], F16)
        ident_b = sb("ident_b", [P, P], BF16)
        mask_f = sb("mask_f", [P, P], F32)
        mask_b = sb("mask_b", [P, P], BF16)
        cos_b = sb("cos_b", [P, ST, B_HD // 2], F32)
        sin_b = sb("sin_b", [P, ST, B_HD // 2], F32)
        iota_e = sb("iota_e", [P, EXPERTS], F32)
        minus_half = sb("minus_half", [P, 1], F32)
        bn = sb("bn", [P, NT, 6], F32)
        mv = sb("mv", [P, NT, 2], F32)
        rstd = sb("rstd", [P, NT], F32)
        w_hi = {n: sb(f"{n}_hi", [P, W_COLS[n]], F16) for n in WEIGHTS}
        w_lo = {n: sb(f"{n}_lo", [P, W_COLS[n]], F16) for n in WEIGHTS}
        amax_w = sb("amax_w", [P, 8], F32)
        pow_w = sb("pow_w", [P, 8], F32)
        inv_w = sb("inv_w", [P, 8], F32)
        amax_q = sb("amax_q", [P, 4], F32)
        pow_q = sb("pow_q", [P, 4], F32)
        inv_q = sb("inv_q", [P, 4], F32)
        c_score = sb("c_score", [P, 2], F32)
        c_out = sb("c_out", [P, 1], F32)
        c_score_b = sb("c_score_b", [P, 2], F32)
        c_out_b = sb("c_out_b", [P, 1], F32)
        c_ffn = sb("c_ffn", [P, 1], F32)
        c_gate = sb("c_gate", [P, 1], F32)
        smax = sb("smax", [P, 2, ST], F32)
        shift = sb("shift", [P, 2, ST], F32)
        rsum = sb("rsum", [P, 2, ST], F32)
        rden = sb("rden", [P, 2, ST], F32)
        prob = sb("prob", [P, 2, TRI], F32)
        pt_hi = sb("pt_hi", [P, TRI], F16)
        pt_lo = sb("pt_lo", [P, TRI], F16)

        a_ctx = ExitStack()
        keep, ctx2 = ctx, a_ctx

        def sa(name, shape, dt):
            return a_ctx.enter_context(nc.sbuf_tensor(name, shape, dt))

        cos_a = sa("cos_a", [P, S], F32)
        sin_a = sa("sin_a", [P, S], F32)
        scn = sa("scn", [P, sum(QUANT_COLS.values())], F32)
        qcode = sa("qcode", [P, KT, 512], I32)
        qcode_f = qcode[:].bitcast(F32)
        qscale = sa("qscale", [P, KT, 512], F32)
        kvcode = sa("kvcode", [P, 2, KT, P], I32)
        kvcode_f = kvcode[:].bitcast(F32)
        kvscale = sa("kvscale", [P, 2, KT, P], F32)
        ocode = sa("ocode", [P, GROUP, D], I32)
        ocode_f = ocode[:].bitcast(F32)
        oscale = sa("oscale", [P, GROUP, D], F32)
        wq_hi = sa("wq_hi", [P, KT, 512], F16)
        wq_lo = sa("wq_lo", [P, KT, 512], F16)
        wkv_hi = sa("wkv_hi", [P, 2, KT, P], F16)
        wkv_lo = sa("wkv_lo", [P, 2, KT, P], F16)
        wo_hi = sa("wo_hi", [P, GROUP, D], F16)
        wo_lo = sa("wo_lo", [P, GROUP, D], F16)
        rt1 = sa("rt1", [P, 2, S], F32)
        rt2 = sa("rt2", [P, 2, S], F32)
        arena = sa("arena", [P, 10 * 1024], F32)
        q_hi = arena[:, 0:2048].bitcast(F16).rearrange("p (s n) -> p s n", s=8)
        q_lo = arena[:, 2048:4096].bitcast(F16).rearrange("p (s n) -> p s n", s=8)
        ctx_hi = arena[:, 4096:6144].bitcast(F16).rearrange("p (s n) -> p s n", s=8)
        ctx_lo = arena[:, 6144:8192].bitcast(F16).rearrange("p (s n) -> p s n", s=8)
        k_hi = arena[:, 8192:8704].bitcast(F16).rearrange("p (s n) -> p s n", s=B)
        k_lo = arena[:, 8704:9216].bitcast(F16).rearrange("p (s n) -> p s n", s=B)
        v_hi = arena[:, 9216:9728].bitcast(F16).rearrange("p (s n) -> p s n", s=B)
        v_lo = arena[:, 9728:10240].bitcast(F16).rearrange("p (s n) -> p s n", s=B)
        raw, at = {}, 0
        for n in WEIGHTS:
            raw[n] = arena[:, at:at + W_COLS[n]]
            at += W_COLS[n]
        assert at <= 10 * 1024
        a_ctx.close()

        r1 = sb("r1", [P, D], F32)
        r2 = sb("r2", [P, D], F32)
        rot = sb("rot", [P, D], F32)
        q_stack = sb("q_stack", [P, NT, B_HEADS * B_ST], F16)
        k_stack = sb("k_stack", [P, NT, KV_HEADS * 2 * B_ST], F16)
        bv_hi = sb("bv_hi", [P, NT, KV_HEADS * B_HD], F16)
        bv_lo = sb("bv_lo", [P, NT, KV_HEADS * B_HD], F16)
        qkt = sb("qkt", [P, 6, S], F16)
        ctx_b = sb("ctx_b", [P, NT, D], F32)
        hs = sb("hs", [P, 2, D], F32)
        mt_hi = sb("mt_hi", [P, 2, D], F16)
        mt_lo = sb("mt_lo", [P, 2, D], F16)
        lg = sb("lg", [P, 2, 8], F32)
        top = sb("top", [P, 2, 8], F32)
        topi = sb("topi", [P, 2, 8], U32)
        topf = sb("topf", [P, 2, 8], F32)
        dif = sb("dif", [P, 2, 2], F32)
        ex = sb("ex", [P, 2, 2], F32)
        exs = sb("exs", [P, 2, 1], F32)
        exr = sb("exr", [P, 2, 1], F32)
        wgt = sb("wgt", [P, 2, 2], F32)
        oh0 = sb("oh0", [P, 2, 8], F32)
        oh1 = sb("oh1", [P, 2, 8], F32)
        wfull = sb("wfull", [P, 2, 8], F32)

        scr = {n: nc.dram_tensor(f"scales_{n}", (P * QUANT_COLS[n],), F32).ap() for n in QUANT}

        d_const, d_x, d_scale, d_raw, d_scr, d_out = (sem(n) for n in (
            "d_const", "d_x", "d_scale", "d_raw", "d_scr", "d_out"))
        consts, chain, amaxq_done, amaxw_done, redq, redw, invq_done, invw_done, scn_done, whi_done, wlo_done = (
            sem(n) for n in ("consts", "chain", "amaxq_done", "amaxw_done", "redq", "redw", "invq_done",
                             "invw_done", "scn_done", "whi_done", "wlo_done"))
        ln_stat, ln_rstd, xn_ready, xt_ps, xthi_done, xt_done = (sem(n) for n in (
            "ln_stat", "ln_rstd", "xn_ready", "xt_ps", "xthi_done", "xt_done"))
        d_q, d_kv, d_o = sem("d_q"), sem("d_kv"), sem("d_o")
        wfull_done = sem("wfull_done")
        whi, w32_done, q_code, kv_code, o_code = (sem(n) for n in ("whi", "w32_done", "q_code", "kv_code", "o_code"))
        q_w, kv_w, o_w = sem("q_w"), sem("kv_w"), sem("o_w")
        proj_ps, proj_read, rot_ready, rothi_done, rot_done, vhi_done = (sem(n) for n in (
            "proj_ps", "proj_read", "rot_ready", "rothi_done", "rot_done", "vhi_done"))
        s_ps, smax_done, shift_done, exp_done, rden_done, prob_done = (sem(n) for n in (
            "s_ps", "smax_done", "shift_done", "exp_done", "rden_done", "prob_done"))
        pt_ps, pthi_done, pt_done, ctx_ps, ctxhi_done, ctx_done, o_ps, o_added = (sem(n) for n in (
            "pt_ps", "pthi_done", "pt_done", "ctx_ps", "ctxhi_done", "ctx_done", "o_ps", "o_added"))
        g_ps, lg_done, dif_done, ex_done, gch, h_ps, hs_done, mt_ps, mthi_done, mt_done, y_ps, y_added = (
            sem(n) for n in ("g_ps", "lg_done", "dif_done", "ex_done", "gch", "h_ps", "hs_done", "mt_ps",
                             "mthi_done", "mt_done", "y_ps", "y_added"))
        bq_ps, bkv_ps, bch, bq_rot, bk_rot, bqhi, bkhi, bvhi, bqlo, bkvlo = (sem(n) for n in (
            "bq_ps", "bkv_ps", "bch", "bq_rot", "bk_rot", "bqhi", "bkhi", "bvhi", "bqlo", "bkvlo"))
        bt_ps, bt_done, bs_ps, bsmax, bshift, bexp, brden, bpt_ps, bpthi, bpt, bctx_ps, bctx = (sem(n) for n in (
            "bt_ps", "bt_done", "bs_ps", "bsmax", "bshift", "bexp", "brden", "bpt_ps", "bpthi", "bpt",
            "bctx_ps", "bctx"))

        block = ctx.enter_context(nc.Block())
        N_CONST = 6

        @block.sync
        def _(sp):
            x_in = t_in["x"].rearrange("b s d -> (b s) d").rearrange("(t p) d -> p t d", p=P)
            sp.dma_start(x[:, 0:ST, :], x_in[:, 0:ST, :]).then_inc(d_x, 16)
            off = 0
            for n in QUANT:
                w = QUANT_COLS[n]
                sp.dma_start(scn[:, off:off + w], t_in[f"{n}_scales"].rearrange("(p f) -> p f", p=P)
                             ).then_inc(d_scale, 16)
                off += w
            sp.dma_start(x[:, ST:NT, :], x_in[:, ST:NT, :]).then_inc(d_x, 16)
            for dst, src in ((ident, "ident"), (mask_f, "mask"), (cos_a, "cos_a"), (sin_a, "sin_a"),
                             (cos_b, "cos_b"), (sin_b, "sin_b")):
                sp.dma_start(dst[:], t_in[src]).then_inc(d_const, 16)

            def load_q(j):
                sp.dma_start(qcode[:], t_in["q_codes"][bass.ds(j, 1)].rearrange("o p g n -> (o p) g n")
                             ).then_inc(d_q, 16)
                sp.dma_start(qscale[:].rearrange("p g n -> p (g n)"),
                             scr["q"][bass.ds(j * 2048, 2048)].partition_broadcast(P)).then_inc(d_q, 16)

            def load_kv(j):
                for i, n in enumerate("kv"):
                    sp.dma_start(kvcode[:, i], t_in[f"{n}_codes"][bass.ds(j, 1)].rearrange("o p g n -> (o p) g n")
                                 ).then_inc(d_kv, 16)
                    sp.dma_start(kvscale[:, i].rearrange("p g n -> p (g n)"),
                                 scr[n][bass.ds(j * 512, 512)].partition_broadcast(P)).then_inc(d_kv, 16)

            def load_o(j):
                sp.dma_start(ocode[:], t_in["o_codes"][bass.ds(j, 1)].rearrange("o p g n -> (o p) g n")
                             ).then_inc(d_o, 16)
                sp.dma_start(oscale[:].rearrange("p g n -> p (g n)"),
                             scr["o"][bass.ds(j * 2048, 2048)].partition_broadcast(P)).then_inc(d_o, 16)

            off = 0
            sp.wait_ge(scn_done, 4)
            for n in QUANT:
                w = QUANT_COLS[n]
                sp.dma_start(scr[n].rearrange("(p f) -> p f", p=P), scn[:, off:off + w]).then_inc(d_scr, 16)
                off += w
            sp.wait_ge(d_scr, 64)
            load_kv(0)
            load_q(0)
            load_o(0)
            for n in WEIGHTS:
                sp.dma_start(raw[n], t_in[n]).then_inc(d_raw, 16)
            with sp.Fori(0, KV_HEADS - 1) as j:
                sp.wait_ge(kv_w, 2 * j + 2)
                load_kv(j + 1)
                sp.wait_ge(q_w, 4 * j + 4)
                load_q(j + 1)
                sp.wait_ge(o_w, 4 * j + 4)
                load_o(j + 1)
            o_out = out.rearrange("b s d -> (b s) d").rearrange("(t p) d -> p t d", p=P)
            for t in range(NT):
                sp.wait_ge(y_added, NT + B * ST + t + 1)
                sp.dma_start(o_out[:, t, :], x[:, t, :]).then_inc(d_out, 16)
            sp.wait_ge(d_out, 16 * NT)

        @block.gpsimd
        def _(pool):
            pool.memset(minus_half[:], -0.5).then_inc(consts, 1)
            pool.iota(iota_e[:], pattern=[[1, EXPERTS]], base=0, channel_multiplier=0,
                      allow_small_or_imprecise_dtypes=True).then_inc(consts, 1)
            pool.wait_ge(consts, 2)

            def ln_rsqrt(c, t):
                pool.wait_ge(ln_stat, 3 * (NT * c + t) + 3)
                pool.tensor_tensor(rstd[:, t:t + 1], mv[:, t, 1:2], minus_half[:], ALU.pow).then_inc(ln_rstd, 1)

            pool.wait_ge(amaxq_done, 4)
            pool.partition_all_reduce(pow_q[:], amax_q[:], P, bass.bass_isa.ReduceOp.max).then_inc(redq, 1)
            for t in range(NT):
                ln_rsqrt(0, t)

            def dequant(n, code, scale, hi, lo):
                pool.tensor_tensor(hi, code, scale, ALU.mult).then_inc(whi, 1)
                pool.tensor_tensor(code, code, scale, ALU.mult).then_inc(w32_done, 1)
                pool.wait_ge(whi, n + 1)
                pool.wait_ge(w32_done, n + 1)
                return pool.tensor_tensor(lo, code, hi, ALU.subtract)

            def deq_kv(j, i, n):
                pool.wait_ge(kv_code, j + 1)
                flat = lambda a: a[:, i].rearrange("p g n -> p (g n)")
                dequant(n, flat(kvcode_f), flat(kvscale), flat(wkv_hi), flat(wkv_lo)).then_inc(kv_w, 1)

            def deq_q(j, g, n):
                pool.wait_ge(q_code, j + 1)
                dequant(n, qcode_f[:, g], qscale[:, g], wq_hi[:, g], wq_lo[:, g]).then_inc(q_w, 1)

            def deq_o(j, g, n):
                pool.wait_ge(o_code, j + 1)
                dequant(n, ocode_f[:, g], oscale[:, g], wo_hi[:, g], wo_lo[:, g]).then_inc(o_w, 1)

            def rope_add(j, u, idx):
                pool.wait_ge(proj_read, 12 * j + idx + 1)
                pool.tensor_tensor(rt1[:, u % 2], rt1[:, u % 2], rt2[:, u % 2], ALU.add).then_inc(rot_ready, 1)

            def rope_lo(j, u, dst, src):
                pool.wait_ge(rothi_done, 10 * j + u + 1)
                pool.tensor_tensor(dst, rt1[:, u % 2], src, ALU.subtract).then_inc(rot_done, 1)

            rot_dst = [(k_lo[:, b], k_hi[:, b]) for b in range(B)] + [(q_lo[:, s], q_hi[:, s]) for s in range(8)]
            rot_at = [0, 1, 2, 3, 6, 7, 8, 9, 10, 11]

            def group(j, last):
                n0 = 10 * j + 6
                for u in range(10):
                    rope_add(j, u, rot_at[u])
                    rope_lo(j, u, *rot_dst[u])
                    if 3 <= u < 7:
                        deq_o(j, u - 3, n0 + u - 3)
                    if 7 <= u < 9 and not last:
                        deq_kv(j + 1, u - 7, n0 + u - 3)
                if not last:
                    pool.wait_ge(proj_ps, 12 * j + 12)
                    for g in range(KT):
                        deq_q(j + 1, g, n0 + 6 + g)

            pool.wait_ge(amaxw_done, len(WEIGHTS))
            for i in range(2):
                deq_kv(0, i, i)
            for g in range(KT):
                deq_q(0, g, 2 + g)
            pool.partition_all_reduce(pow_w[:, 0:len(WEIGHTS)], amax_w[:, 0:len(WEIGHTS)], P,
                                      bass.bass_isa.ReduceOp.max).then_inc(redw, 1)
            with pool.Fori(0, KV_HEADS - 1) as j:
                group(j, False)
            group(KV_HEADS - 1, True)
            for c in range(1, 4):
                for t in range(NT):
                    ln_rsqrt(c, t)

        @block.scalar
        def _(act):
            def ln_hi(c, t):
                act.wait_ge(xt_ps, NT * c + t + 1)
                act.activation(xt_hi[:, :, t * P:(t + 1) * P], bank[3 + t % 2][:].rearrange("p (k n) -> p k n", k=KT),
                               ACT.Copy, scale=X_UP).then_inc(xthi_done, 1)

            def codes(j, code, code_f, loaded, count, done):
                act.wait_ge(loaded, count)
                act.activation(code_f[:].rearrange("p a b -> p (a b)") if len(code_f.shape) == 3 else
                               code_f[:].rearrange("p i a b -> p (i a b)"),
                               code[:].rearrange("p a b -> p (a b)") if len(code.shape) == 3 else
                               code[:].rearrange("p i a b -> p (i a b)"), ACT.Copy, bias=-8.0).then_inc(done, 1)

            for t in range(NT):
                ln_hi(0, t)
            codes(0, kvcode, kvcode_f, d_kv, 64, kv_code)
            codes(0, qcode, qcode_f, d_q, 32, q_code)
            act.wait_ge(invw_done, 1)
            act.wait_ge(d_raw, 16 * len(WEIGHTS))
            for i, n in enumerate(WEIGHTS):
                act.activation(w_hi[n][:], raw[n], ACT.Copy, scale=inv_w[:, i:i + 1]).then_inc(whi_done, 1)

            rot_hi = [k_hi[:, b] for b in range(B)] + [q_hi[:, s] for s in range(8)]

            def rope_hi(j, u):
                act.wait_ge(rot_ready, 10 * j + u + 1)
                act.activation(rot_hi[u], rt1[:, u % 2], ACT.Copy).then_inc(rothi_done, 1)

            def v_high(j, b):
                act.wait_ge(proj_ps, 12 * j + 5 + b)
                act.activation(v_hi[:, b], bank[6][:], ACT.Copy, scale=PROJ_DN).then_inc(vhi_done, 1)

            def exps(n, i2, score, ready, done, base):
                act.wait_ge(ready, base + 1)
                for i in S_ORDER:
                    bk, o = S_BANK[i]
                    w = (i + 1) * P
                    act.activation(prob[:, i2, S_OFF[i]:S_OFF[i] + w], bank[bk][:, o:o + w], ACT.Exp,
                                   bias=shift[:, i2, i:i + 1], scale=score[:, 0:1],
                                   accum_out=rsum[:, i2, i:i + 1]).then_inc(done, 1)

            def pt_high(base, piece, ps, done, bk, scale):
                w = S if piece < 2 else 2 * P
                act.wait_ge(ps, base + piece + 1)
                act.activation(pt_hi[:, piece * S:piece * S + w], bank[bk][:, 0:w], ACT.Copy,
                               scale=scale).then_inc(done, 1)

            def ctx_high(j, s):
                act.wait_ge(ctx_ps, 8 * j + s + 1)
                act.activation(ctx_hi[:, s], bank[5][:], ACT.Copy, scale=1.0 / P_UP).then_inc(ctxhi_done, 1)

            def group(j, last):
                for u in range(4):
                    rope_hi(j, u)
                v_high(j, 0)
                v_high(j, 1)
                codes(j, ocode, ocode_f, d_o, 32 * j + 32, o_code)
                for s in range(8):
                    if s:
                        pt_high(24 * j + 3 * (s - 1), 0, pt_ps, pthi_done, 3, 1.0)
                        pt_high(24 * j + 3 * (s - 1), 1, pt_ps, pthi_done, 4, 1.0)
                    exps(s, s % 2, c_score, shift_done, exp_done, 8 * j + s)
                    if s + 2 < 8:
                        rope_hi(j, s + 4)
                    if s:
                        pt_high(24 * j + 3 * (s - 1), 2, pt_ps, pthi_done, 3, 1.0)
                        ctx_high(j, s - 1)
                    if s == 2 and not last:
                        codes(j, kvcode, kvcode_f, d_kv, 64 * (j + 1) + 64, kv_code)
                    if s == 3 and not last:
                        codes(j, qcode, qcode_f, d_q, 32 * (j + 1) + 32, q_code)
                for piece, bk in ((0, 3), (1, 4), (2, 3)):
                    pt_high(24 * j + 21, piece, pt_ps, pthi_done, bk, 1.0)
                ctx_high(j, 7)

            act.wait_ge(wlo_done, len(WEIGHTS))
            with act.Fori(0, KV_HEADS - 1) as j:
                group(j, False)
            group(KV_HEADS - 1, True)

            def m_high(m, src_scale):
                act.wait_ge(mt_ps, m + 1)
                act.activation(mt_hi[:, m % 2], bank[2][:], ACT.Copy, scale=src_scale).then_inc(mthi_done, 1)

            def experts(ph):
                c = 1 + 2 * ph
                m0 = ph * 2 * NT
                for t in range(NT):
                    ln_hi(c, t)
                    f = NT * ph + t
                    act.wait_ge(dif_done, f + 1)
                    act.activation(ex[:, t % 2], dif[:, t % 2], ACT.Exp, accum_out=exs[:, t % 2]).then_inc(ex_done, 1)
                    if t:
                        m_high(m0 + t - 1, PROJ_DN_B)
                m_high(m0 + NT - 1, PROJ_DN_B)

            experts(0)
            for t in range(NT):
                ln_hi(2, t)
                qs = q_stack[:, t].rearrange("p (h a d) -> p h a d", h=B_HEADS, a=4)
                ks = k_stack[:, t].rearrange("p (h u a d) -> p h u a d", h=KV_HEADS, u=2, a=4)
                act.wait_ge(bq_rot, t + 1)
                src = rot[:].rearrange("p (h d) -> p h d", d=B_HD)
                for a in (0, 2):
                    act.activation(qs[:, :, a], src, ACT.Copy).then_inc(bqhi, 1)
                act.wait_ge(bk_rot, t + 1)
                src = rot[:, 0:P].rearrange("p (h d) -> p h d", d=B_HD)
                for u in range(2):
                    for a in (0, 1):
                        act.activation(ks[:, :, u, a], src, ACT.Copy).then_inc(bkhi, 1)
                act.wait_ge(bkv_ps, t + 1)
                act.activation(bv_hi[:, t], bank[5 + t % 2][:, P:2 * P], ACT.Copy, scale=PROJ_DN_B).then_inc(bvhi, 1)
            with act.Fori(0, KV_HEADS) as j:
                for u in range(6):
                    act.wait_ge(bt_ps, 6 * j + u + 1)
                    act.activation(qkt[:, u], bank[3 + u % 2][:], ACT.Copy).then_inc(bt_done, 1)
                for s in range(9):
                    if s:
                        for piece, bk in ((0, 3), (1, 4), (2, 6)):
                            pt_high(24 * j + 3 * (s - 1), piece, bpt_ps, bpthi, bk, P_UP)
                    if s < 8:
                        exps(s, s % 2, c_score_b, bshift, bexp, 8 * j + s)
            for t in range(NT):
                m_high(NT + t, 1.0 / P_UP)
            experts(1)

        @block.tensor
        def _(pe):
            def three(out_ap, a_hi, a_lo, b_hi, b_lo, k, n, stop=True):
                pe.matmul(out_ap, a_hi, b_hi, start=(k == 0), stop=False)
                pe.matmul(out_ap, a_hi, b_lo, start=False, stop=False)
                return pe.matmul(out_ap, a_lo, b_hi, start=False, stop=(stop and k == n - 1))

            def ln_t(c, t):
                i = NT * c + t
                pe.wait_ge(xn_ready, i + 1)
                if i >= 2:
                    pe.wait_ge(xt_done, i - 1)
                for k in range(KT):
                    mm = pe.transpose(bank[3 + t % 2][:, k * P:(k + 1) * P], xn[:, t % 2, k * P:(k + 1) * P], ident[:])
                mm.then_inc(xt_ps, 1)

            pe.wait_ge(d_const, 16 * N_CONST)
            for t in range(NT):
                ln_t(0, t)
            pe.wait_ge(chain, 3)
            pe.wait_ge(xt_done, NT)

            def proj_begin(j, idx):
                if idx:
                    pe.wait_ge(proj_read, 12 * j + idx)

            def proj_k(j, b):
                proj_begin(j, b)
                if b == 0:
                    pe.wait_ge(kv_w, 2 * j + 2)
                for g in range(KT):
                    mm = three(bank[6][:], wkv_hi[:, 0, g], wkv_lo[:, 0, g], xt_hi[:, g, b * S:(b + 1) * S],
                               xt_lo[:, g, b * S:(b + 1) * S], g, KT)
                mm.then_inc(proj_ps, 1)

            def proj_q(j, s, idx):
                hh, b = s // B, s % B
                proj_begin(j, idx)
                if s == 0:
                    pe.wait_ge(q_w, 4 * j + 4)
                for g in range(KT):
                    a_hi = wq_hi[:, g, hh * P:(hh + 1) * P]
                    a_lo = wq_lo[:, g, hh * P:(hh + 1) * P]
                    mm = three(bank[6][:], a_hi, a_lo, xt_hi[:, g, b * S:(b + 1) * S],
                               xt_lo[:, g, b * S:(b + 1) * S], g, KT)
                mm.then_inc(proj_ps, 1)

            def proj_v(j, b):
                proj_begin(j, 4 + b)
                for t in range(ST):
                    c0 = (b * ST + t) * P
                    for g in range(KT):
                        mm = three(bank[6][:, t * P:(t + 1) * P], xt_hi[:, g, c0:c0 + P], xt_lo[:, g, c0:c0 + P],
                                   wkv_hi[:, 1, g], wkv_lo[:, 1, g], g, KT)
                mm.then_inc(proj_ps, 1)

            def scores(j, s):
                hh, b = s // B, s % B
                pe.wait_ge(rot_done, 10 * j + s + 3)
                for i in S_ORDER:
                    bk, o = S_BANK[i]
                    w = (i + 1) * P
                    if i == 0 and s:
                        pe.wait_ge(exp_done, 4 * (8 * j + s))
                    o_ap = bank[bk][:, o:o + w]
                    qs = slice(i * P, (i + 1) * P)
                    pe.matmul(o_ap, q_hi[:, s, qs], k_hi[:, b, 0:w], start=True, stop=False)
                    pe.matmul(o_ap, q_hi[:, s, qs], k_lo[:, b, 0:w], start=False, stop=False)
                    pe.matmul(o_ap, q_lo[:, s, qs], k_hi[:, b, 0:w], start=False, stop=False)
                    mm = pe.matmul(bank[bk][:, o + w - P:o + w], ident_b[:], mask_b[:], start=False, stop=True)
                    if i != 0:
                        mm.then_inc(s_ps, 1)

            def transposes(n, piece, ready, need, ps, bk, i2):
                if piece == 0:
                    pe.wait_ge(ready, need)
                for k, tiles in enumerate([(0,), (1, 3), (2,)][piece]):
                    for i in range(tiles, ST):
                        o = T_OFF[tiles] - piece * S + (i - tiles) * P
                        mm = pe.transpose(bank[bk][:, o:o + P],
                                          prob[:, i2, S_OFF[i] + tiles * P:S_OFF[i] + (tiles + 1) * P], ident[:])
                mm.then_inc(ps, 1)

            def a_transposes(j, s, piece):
                n3 = 24 * j + 3 * s
                bk = 4 if piece == 1 else 3
                if piece == 0 and s:
                    pe.wait_ge(pt_done, n3)
                if piece == 2:
                    pe.wait_ge(pt_done, n3 + 1)
                transposes(s, piece, prob_done, 4 * (8 * j + s) + 4, pt_ps, bk, s % 2)

            def a_pv(j, s):
                b = s % B
                if s < B:
                    pe.wait_ge(proj_read, 12 * j + 6)
                if s:
                    pe.wait_ge(ctx_done, 8 * j + s)
                for kt in (0, 1, 3, 2):
                    piece = {0: 0, 1: 1, 3: 1, 2: 2}[kt]
                    pe.wait_ge(pt_done, 24 * j + 3 * s + piece + 1)
                    w = S - kt * P
                    o_ap = bank[5][:, kt * P:S]
                    tc = slice(T_OFF[kt], T_OFF[kt] + w)
                    vs = slice(kt * P, (kt + 1) * P)
                    pe.matmul(o_ap, v_hi[:, b, vs], pt_hi[:, tc], start=(kt == 0), stop=False)
                    pe.matmul(o_ap, v_hi[:, b, vs], pt_lo[:, tc], start=False, stop=False)
                    mm = pe.matmul(o_ap, v_lo[:, b, vs], pt_hi[:, tc], start=False, stop=(kt == 2))
                mm.then_inc(ctx_ps, 1)

            def a_out(j, t):
                b = t // ST
                if t == 0:
                    pe.wait_ge(o_w, 4 * j + 4)
                    pe.wait_ge(ctx_done, 8 * j + 7)
                    pe.wait_ge(proj_read, 12 * j + 12)
                if t == ST:
                    pe.wait_ge(ctx_done, 8 * j + 8)
                if t >= 2:
                    pe.wait_ge(o_added, NT * j + t - 1)
                ts = slice((t % ST) * P, (t % ST + 1) * P)
                for hh in range(GROUP):
                    mm = three(bank[O_BANK[t]][:], ctx_hi[:, hh * B + b, ts], ctx_lo[:, hh * B + b, ts],
                               wo_hi[:, hh], wo_lo[:, hh], hh, GROUP)
                mm.then_inc(o_ps, 1)

            with pe.Fori(0, KV_HEADS) as j:
                proj_k(j, 0)
                proj_k(j, 1)
                proj_q(j, 0, 2)
                proj_q(j, 1, 3)
                proj_v(j, 0)
                proj_v(j, 1)
                for s in range(8):
                    scores(j, s)
                    if s:
                        a_transposes(j, s - 1, 0)
                        a_transposes(j, s - 1, 1)
                    if s + 2 < 8:
                        proj_q(j, s + 2, s + 6)
                    if s:
                        a_transposes(j, s - 1, 2)
                        a_pv(j, s - 1)
                for t in range(ST):
                    a_out(j, t)
                for piece in range(3):
                    a_transposes(j, 7, piece)
                a_pv(j, 7)
                for t in range(ST, NT):
                    a_out(j, t)

            def back(m, src, name):
                if m >= 1:
                    pe.wait_ge(mt_done, m)
                for k in range(KT):
                    mm = pe.transpose(bank[2][:, k * P:(k + 1) * P], src[:, k * P:(k + 1) * P], ident[:])
                mm.then_inc(mt_ps, 1)
                pe.wait_ge(mt_done, m + 1)
                if m >= 2:
                    pe.wait_ge(y_added, m - 1)
                wh = w_hi[name][:].rearrange("p (k n) -> p k n", k=KT)
                wl = w_lo[name][:].rearrange("p (k n) -> p k n", k=KT)
                for k in range(KT):
                    ks = slice(k * P, (k + 1) * P)
                    mm = three(bank[6 + m % 2][:], mt_hi[:, m % 2, ks], mt_lo[:, m % 2, ks], wh[:, k], wl[:, k], k, KT)
                mm.then_inc(y_ps, 1)

            def wide(out_ap, t, name, n):
                wh = w_hi[name][:].rearrange("p (k n) -> p k n", k=KT)
                wl = w_lo[name][:].rearrange("p (k n) -> p k n", k=KT)
                ts = slice(t * P, (t + 1) * P)
                for k in range(KT):
                    mm = three(out_ap, xt_hi[:, k, ts], xt_lo[:, k, ts], wh[:, k], wl[:, k], k, KT)
                return mm

            def experts(ph):
                c = 1 + 2 * ph
                m0 = ph * 2 * NT
                for t in range(NT):
                    f = NT * ph + t
                    ln_t(c, t)
                    pe.wait_ge(xt_done, NT * c + t + 1)
                    if f:
                        pe.wait_ge(lg_done, f)
                    wide(bank[5][:, 0:EXPERTS], t, "gate", EXPERTS).then_inc(g_ps, 1)
                    if f >= 2:
                        pe.wait_ge(hs_done, f - 1)
                    wide(bank[t % 2][:], t, "lora_a", D).then_inc(h_ps, 1)
                    if t:
                        pe.wait_ge(hs_done, f)
                        back(m0 + t - 1, hs[:, (t - 1) % 2], "lora_b")
                pe.wait_ge(hs_done, NT * ph + NT)
                back(m0 + NT - 1, hs[:, (NT - 1) % 2], "lora_b")

            experts(0)
            for t in range(NT):
                ln_t(2, t)
                pe.wait_ge(xt_done, NT * 2 + t + 1)
                if t >= 2:
                    pe.wait_ge(bq_rot, t - 1)
                wide(bank[t % 2][:], t, "b_q", D).then_inc(bq_ps, 1)
                if t >= 2:
                    pe.wait_ge(bkvlo, 5 * (t - 1))
                wide(bank[5 + t % 2][:, 0:2 * P], t, "b_kv", 2 * P).then_inc(bkv_ps, 1)
            pe.wait_ge(bqlo, 2 * NT)
            pe.wait_ge(bkvlo, 5 * NT)

            def b_scores(j, s):
                hh, b = s // B, s % B
                rows = slice((hh % 2) * B_ST, (hh % 2 + 1) * B_ST)
                qt = qkt[rows, hh // 2 * B + b]
                kk = qkt[rows, 4 + b]
                for i in S_ORDER:
                    bk, o = S_BANK[i]
                    w = (i + 1) * P
                    if i == 0 and s:
                        pe.wait_ge(bexp, 4 * (8 * j + s))
                    pe.matmul(bank[bk][:, o:o + w], qt[:, i * P:(i + 1) * P], kk[:, 0:w], start=True, stop=False)
                    mm = pe.matmul(bank[bk][:, o + w - P:o + w], ident_b[:], mask_b[:], start=False, stop=True)
                    if i != 0:
                        mm.then_inc(bs_ps, 1)

            def b_pv(j, s):
                hh, b = s // B, s % B
                if s:
                    pe.wait_ge(bctx, 8 * j + s)
                pe.wait_ge(bpt, 24 * j + 3 * s + 3)
                vc = bass.ds(j * B_HD, B_HD)
                for i in range(ST):
                    o_ap = bank[5][:, i * B_HD:(i + 1) * B_HD]
                    for kt in range(i + 1):
                        tc = slice(T_OFF[kt] + (i - kt) * P, T_OFF[kt] + (i - kt + 1) * P)
                        vh, vl = bv_hi[:, b * ST + kt, vc], bv_lo[:, b * ST + kt, vc]
                        mm = three(o_ap, pt_hi[:, tc], pt_lo[:, tc], vh, vl, kt, i + 1)
                mm.then_inc(bctx_ps, 1)

            with pe.Fori(0, KV_HEADS) as j:
                for u in range(6):
                    if u >= 2:
                        pe.wait_ge(bt_done, 6 * j + u - 1)
                    for t in range(ST):
                        if u < 4:
                            src = q_stack[:, (u % 2) * ST + t, bass.ds(j * (GROUP * B_ST) + (u // 2) * P, P)]
                        else:
                            src = k_stack[:, (u % 2) * ST + t, bass.ds(j * P, P)]
                        mm = pe.matmul(bank[3 + u % 2][:, t * P:(t + 1) * P], src, ident_h[:], start=True, stop=True)
                    mm.then_inc(bt_ps, 1)
                pe.wait_ge(bt_done, 6 * j + 6)
                for s in range(9):
                    if s < 8:
                        b_scores(j, s)
                    if s:
                        for piece, bk in ((0, 3), (1, 4), (2, 6)):
                            if piece == 0 and s > 1:
                                pe.wait_ge(bpt, 24 * j + 3 * (s - 1))
                            transposes(s - 1, piece, bexp, 4 * (8 * j + s - 1) + 4, bpt_ps, bk, (s - 1) % 2)
                        b_pv(j, s - 1)
            pe.wait_ge(bctx, 8 * KV_HEADS)
            for t in range(NT):
                back(NT + t, ctx_b[:, t], "b_o")
            experts(1)

        @block.vector
        def _(dve):
            off = 0
            dve.wait_ge(d_scale, 64)
            for i, n in enumerate(QUANT):
                w = QUANT_COLS[n]
                dve.tensor_reduce(amax_q[:, i:i + 1], scn[:, off:off + w], AX, ALU.max,
                                  apply_absolute_value=True).then_inc(amaxq_done, 1)
                off += w

            inv_n = [0]

            def power_of_two(value, inv, n, red, done):
                dve.wait_ge(red, 1)
                dve.tensor_scalar(value[:, 0:n], value[:, 0:n], 1e-30, None, ALU.max).then_inc(red, 1)
                dve.wait_ge(red, 2)
                dve.tensor_single_scalar(value[:, 0:n].bitcast(U32), value[:, 0:n].bitcast(U32), 0x7F800000,
                                         ALU.bitwise_and).then_inc(red, 1)
                dve.wait_ge(red, 3)
                dve.reciprocal(inv[:, 0:n], value[:, 0:n]).then_inc(red, 1)
                dve.wait_ge(red, 4)
                dve.tensor_scalar(inv[:, 0:n], inv[:, 0:n], W_UP, None, ALU.mult).then_inc(done, 1)
                dve.wait_ge(done, 1)

            def ln_stats(c, t):
                i = 3 * (NT * c + t)
                dve.bn_stats(bn[:, t], x[:, t]).then_inc(ln_stat, 1)
                dve.wait_ge(ln_stat, i + 1)
                dve.bn_aggr(mv[:, t], bn[:, t]).then_inc(ln_stat, 1)
                dve.wait_ge(ln_stat, i + 2)
                dve.tensor_scalar(mv[:, t, 1:2], mv[:, t, 1:2], EPS, None, ALU.add).then_inc(ln_stat, 1)

            def ln_norm(c, t):
                i = NT * c + t
                if i >= 2:
                    dve.wait_ge(xt_ps, i - 1)
                dve.wait_ge(ln_rstd, i + 1)
                dve.tensor_scalar(xn[:, t % 2], x[:, t], mv[:, t, 0:1], rstd[:, t:t + 1], ALU.subtract,
                                  ALU.mult).then_inc(xn_ready, 1)

            def ln_lo(c, t):
                dve.wait_ge(xthi_done, NT * c + t + 1)
                dve.scalar_tensor_tensor(out=xt_lo[:, :, t * P:(t + 1) * P],
                                         in0=bank[3 + t % 2][:].rearrange("p (k n) -> p k n", k=KT), scalar=X_UP,
                                         in1=xt_hi[:, :, t * P:(t + 1) * P], op0=ALU.mult,
                                         op1=ALU.subtract).then_inc(xt_done, 1)

            dve.wait_ge(d_x, 32)
            for t in range(NT):
                ln_stats(0, t)
            power_of_two(pow_q, inv_q, 4, redq, invq_done)
            off = 0
            for i, n in enumerate(QUANT):
                w = QUANT_COLS[n]
                dve.tensor_scalar(scn[:, off:off + w], scn[:, off:off + w], inv_q[:, i:i + 1], None,
                                  ALU.mult).then_inc(scn_done, 1)
                off += w
            dve.wait_ge(d_const, 16 * N_CONST)
            dve.tensor_copy(ident_h[:], ident[:]).then_inc(chain, 1)
            dve.tensor_copy(ident_b[:], ident[:]).then_inc(chain, 1)
            dve.tensor_copy(mask_b[:], mask_f[:]).then_inc(chain, 1)
            for t in range(NT):
                ln_norm(0, t)
                if t:
                    ln_lo(0, t - 1)
            ln_lo(0, NT - 1)
            dve.tensor_tensor(c_score[:, 0:1], pow_q[:, 0:1], pow_q[:, 1:2], ALU.mult).then_inc(chain, 1)
            dve.tensor_tensor(c_out[:], pow_q[:, 2:3], pow_q[:, 3:4], ALU.mult).then_inc(chain, 1)
            dve.wait_ge(chain, 5)
            k_a = float(A_HD ** -0.5) / 16.0
            dve.tensor_scalar(c_score[:, 1:2], c_score[:, 0:1], -k_a, None, ALU.mult).then_inc(chain, 1)
            dve.tensor_scalar(c_out[:], c_out[:], 1.0 / (4.0 * W_UP), None, ALU.mult).then_inc(chain, 1)
            dve.wait_ge(chain, 7)
            dve.tensor_scalar(c_score[:, 0:1], c_score[:, 0:1], k_a, None, ALU.mult).then_inc(chain, 1)

            dve.wait_ge(d_raw, 16 * len(WEIGHTS))
            for i, n in enumerate(WEIGHTS):
                dve.tensor_reduce(amax_w[:, i:i + 1], raw[n], AX, ALU.max,
                                  apply_absolute_value=True).then_inc(amaxw_done, 1)
            power_of_two(pow_w, inv_w, len(WEIGHTS), redw, invw_done)
            for i, n in enumerate(WEIGHTS):
                dve.wait_ge(whi_done, i + 1)
                dve.scalar_tensor_tensor(out=w_lo[n][:], in0=raw[n], scalar=inv_w[:, i:i + 1], in1=w_hi[n][:],
                                         op0=ALU.mult, op1=ALU.subtract).then_inc(wlo_done, 1)
            p_a, p_b, p_q, p_kv, p_o, p_g = (pow_w[:, i:i + 1] for i in range(6))
            k_b = float(B_HD ** -0.5) / 1024.0
            dve.tensor_tensor(c_ffn[:], p_a, p_b, ALU.mult).then_inc(chain, 1)
            dve.tensor_tensor(c_score_b[:, 0:1], p_q, p_kv, ALU.mult).then_inc(chain, 1)
            dve.tensor_tensor(c_out_b[:], p_kv, p_o, ALU.mult).then_inc(chain, 1)
            dve.tensor_scalar(c_gate[:], p_g, 1.0 / (X_UP * W_UP), None, ALU.mult).then_inc(chain, 1)
            dve.wait_ge(chain, 12)
            dve.tensor_scalar(c_ffn[:], c_ffn[:], 1.0 / (32.0 * W_UP), None, ALU.mult).then_inc(chain, 1)
            dve.tensor_scalar(c_out_b[:], c_out_b[:], 1.0 / (32.0 * W_UP), None, ALU.mult).then_inc(chain, 1)
            dve.tensor_scalar(c_score_b[:, 1:2], c_score_b[:, 0:1], -k_b, None, ALU.mult).then_inc(chain, 1)
            dve.wait_ge(chain, 15)
            dve.tensor_scalar(c_score_b[:, 0:1], c_score_b[:, 0:1], k_b, None, ALU.mult).then_inc(chain, 1)
            dve.wait_ge(chain, 16)

            def rope(j, u, idx):
                dve.wait_ge(proj_ps, 12 * j + idx + 1)
                if u >= 2:
                    dve.wait_ge(rot_done, 10 * j + u - 1)
                h = P // 2
                dve.tensor_tensor(rt2[0:h, u % 2], bank[6][h:P], sin_a[h:P], ALU.mult)
                dve.tensor_tensor(rt2[h:P, u % 2], bank[6][0:h], sin_a[0:h], ALU.mult)
                dve.tensor_tensor(rt1[:, u % 2], bank[6][:], cos_a[:], ALU.mult).then_inc(proj_read, 1)

            def v_low(j, b):
                dve.wait_ge(vhi_done, 2 * j + b + 1)
                dve.scalar_tensor_tensor(out=v_lo[:, b], in0=bank[6][:], scalar=PROJ_DN, in1=v_hi[:, b], op0=ALU.mult,
                                         op1=ALU.subtract).then_inc(proj_read, 1)

            def row_max(n, i2, ps, own, done, score):
                for c, i in enumerate(S_ORDER):
                    bk, o = S_BANK[i]
                    if c != 1:
                        dve.wait_ge(ps, 3 * n + {0: 1, 2: 2, 3: 3}[c])
                    dve.tensor_reduce(smax[:, i2, i:i + 1], bank[bk][:, o:o + (i + 1) * P], AX,
                                      ALU.max).then_inc(own, 1)
                dve.wait_ge(own, 4 * n + 4)
                dve.tensor_scalar(shift[:, i2], smax[:, i2], score[:, 1:2], None, ALU.mult).then_inc(done, 1)

            def pt_low(base, piece, hi_done, done, bk, scale):
                w = S if piece < 2 else 2 * P
                c = slice(piece * S, piece * S + w)
                dve.wait_ge(hi_done, base + piece + 1)
                dve.scalar_tensor_tensor(out=pt_lo[:, c], in0=bank[bk][:, 0:w], scalar=scale, in1=pt_hi[:, c],
                                         op0=ALU.mult, op1=ALU.subtract).then_inc(done, 1)

            def normalise(j, s):
                n = 8 * j + s
                dve.wait_ge(exp_done, 4 * n + 4)
                dve.reciprocal(rden[:, s % 2], rsum[:, s % 2]).then_inc(rden_done, 1)
                dve.wait_ge(rden_done, n + 1)
                for i in range(ST):
                    w = (i + 1) * P
                    pr = prob[:, s % 2, S_OFF[i]:S_OFF[i] + w]
                    dve.tensor_scalar(pr, pr, rden[:, s % 2, i:i + 1], P_UP, ALU.mult, ALU.mult).then_inc(prob_done, 1)

            def ctx_low(j, s):
                dve.wait_ge(ctxhi_done, 8 * j + s + 1)
                dve.scalar_tensor_tensor(out=ctx_lo[:, s], in0=bank[5][:], scalar=1.0 / P_UP, in1=ctx_hi[:, s],
                                         op0=ALU.mult, op1=ALU.subtract).then_inc(ctx_done, 1)

            def o_add(j, t):
                dve.wait_ge(o_ps, NT * j + t + 1)
                dve.scalar_tensor_tensor(out=x[:, t], in0=bank[O_BANK[t]][:], scalar=c_out[:, 0:1], in1=x[:, t],
                                         op0=ALU.mult, op1=ALU.add).then_inc(o_added, 1)

            rot_at = [0, 1, 2, 3, 6, 7, 8, 9, 10, 11]
            with dve.Fori(0, KV_HEADS) as j:
                for u in range(4):
                    rope(j, u, rot_at[u])
                v_low(j, 0)
                v_low(j, 1)
                for s in range(8):
                    row_max(8 * j + s, s % 2, s_ps, smax_done, shift_done, c_score)
                    if s:
                        pt_low(24 * j + 3 * (s - 1), 0, pthi_done, pt_done, 3, 1.0)
                        pt_low(24 * j + 3 * (s - 1), 1, pthi_done, pt_done, 4, 1.0)
                    if s + 2 < 8:
                        rope(j, s + 4, rot_at[s + 4])
                    if s:
                        pt_low(24 * j + 3 * (s - 1), 2, pthi_done, pt_done, 3, 1.0)
                    normalise(j, s)
                    if s:
                        ctx_low(j, s - 1)
                for t in range(ST):
                    o_add(j, t)
                for piece, bk in ((0, 3), (1, 4), (2, 3)):
                    pt_low(24 * j + 21, piece, pthi_done, pt_done, bk, 1.0)
                ctx_low(j, 7)
                for t in range(ST, NT):
                    o_add(j, t)

            def gate(ph, t):
                f = NT * ph + t
                i2 = t % 2
                g0 = 7 * f
                dve.wait_ge(g_ps, f + 1)
                dve.tensor_copy(lg[:, i2], bank[5][:, 0:EXPERTS]).then_inc(lg_done, 1)
                dve.wait_ge(lg_done, f + 1)
                dve.max(top[:, i2], lg[:, i2]).then_inc(gch, 1)
                dve.wait_ge(gch, g0 + 1)
                dve.tensor_scalar(dif[:, i2], top[:, i2, 0:2], top[:, i2, 0:1], c_gate[:, 0:1], ALU.subtract,
                                  ALU.mult).then_inc(dif_done, 1)
                dve.max_index(topi[:, i2], top[:, i2], lg[:, i2]).then_inc(gch, 1)
                dve.wait_ge(gch, g0 + 2)
                dve.tensor_copy(topf[:, i2], topi[:, i2]).then_inc(gch, 1)
                dve.wait_ge(ex_done, f + 1)
                dve.reciprocal(exr[:, i2], exs[:, i2]).then_inc(gch, 1)
                dve.wait_ge(gch, g0 + 4)
                dve.tensor_scalar(wgt[:, i2], ex[:, i2], exr[:, i2], None, ALU.mult).then_inc(gch, 1)
                dve.wait_ge(gch, g0 + 5)
                dve.tensor_scalar(oh0[:, i2], iota_e[:], topf[:, i2, 0:1], wgt[:, i2, 0:1], ALU.is_equal,
                                  ALU.mult).then_inc(gch, 1)
                dve.tensor_scalar(oh1[:, i2], iota_e[:], topf[:, i2, 1:2], wgt[:, i2, 1:2], ALU.is_equal,
                                  ALU.mult).then_inc(gch, 1)
                dve.wait_ge(gch, g0 + 7)
                dve.tensor_tensor(wfull[:, i2], oh0[:, i2], oh1[:, i2], ALU.add).then_inc(wfull_done, 1)
                dve.wait_ge(wfull_done, f + 1)
                dve.wait_ge(h_ps, f + 1)
                dve.tensor_tensor(hs[:, i2].rearrange("p (e r) -> p e r", e=EXPERTS),
                                  bank[t % 2][:].rearrange("p (e r) -> p e r", e=EXPERTS),
                                  wfull[:, i2].unsqueeze(2).broadcast_to([P, EXPERTS, RANK]), ALU.mult).then_inc(hs_done, 1)

            def m_low(m, scale):
                dve.wait_ge(mthi_done, m + 1)
                dve.scalar_tensor_tensor(out=mt_lo[:, m % 2], in0=bank[2][:], scalar=scale, in1=mt_hi[:, m % 2],
                                         op0=ALU.mult, op1=ALU.subtract).then_inc(mt_done, 1)

            def y_add(m, t, factor):
                dve.wait_ge(y_ps, m + 1)
                dve.scalar_tensor_tensor(out=x[:, t], in0=bank[6 + m % 2][:], scalar=factor[:, 0:1], in1=x[:, t],
                                         op0=ALU.mult, op1=ALU.add).then_inc(y_added, 1)
                dve.wait_ge(y_added, m + 1)

            def experts(ph, after):
                c = 1 + 2 * ph
                m0 = ph * 2 * NT
                ln_norm(c, 0)
                for t in range(NT):
                    ln_lo(c, t)
                    if t + 1 < NT:
                        ln_norm(c, t + 1)
                    gate(ph, t)
                    if t:
                        m_low(m0 + t - 1, PROJ_DN_B)
                        y_add(m0 + t - 1, t - 1, c_ffn)
                        if after is not None:
                            ln_stats(after, t - 1)
                m_low(m0 + NT - 1, PROJ_DN_B)
                y_add(m0 + NT - 1, NT - 1, c_ffn)
                if after is not None:
                    ln_stats(after, NT - 1)

            dve.wait_ge(o_added, NT * KV_HEADS)
            for t in range(NT):
                ln_stats(1, t)
            experts(0, 2)

            H2 = B_HD // 2
            ch = [0]

            def b_rope(src, n, t):
                heads = n // B_HD
                cs = cos_b[:, t % ST].unsqueeze(1)
                sn = sin_b[:, t % ST].unsqueeze(1)
                s4 = src.rearrange("p (h a d) -> p h a d", a=2, d=H2)
                o1 = r1[:, 0:n].rearrange("p (h d) -> p h d", d=H2)
                o2 = r2[:, 0:n].rearrange("p (h a d) -> p h a d", a=2, d=H2)
                dve.tensor_tensor(o1, src.rearrange("p (h d) -> p h d", d=H2),
                                  cs.broadcast_to([P, 2 * heads, H2]), ALU.mult).then_inc(bch, 1)
                dve.tensor_tensor(o2[:, :, 0], s4[:, :, 1], sn.broadcast_to([P, heads, H2]), ALU.mult).then_inc(bch, 1)
                dve.tensor_tensor(o2[:, :, 1], s4[:, :, 0], sn.broadcast_to([P, heads, H2]), ALU.mult).then_inc(bch, 1)
                ch[0] += 3
                dve.wait_ge(bch, ch[0])
                a1 = r1[:, 0:n].rearrange("p (h a d) -> p h a d", a=2, d=H2)
                rr = rot[:, 0:n].rearrange("p (h a d) -> p h a d", a=2, d=H2)
                dve.tensor_tensor(rr[:, :, 0], a1[:, :, 0], o2[:, :, 0], ALU.subtract).then_inc(bch, 1)
                last = dve.tensor_tensor(rr[:, :, 1], a1[:, :, 1], o2[:, :, 1], ALU.add)
                ch[0] += 1
                return last

            ln_norm(2, 0)
            for t in range(NT):
                ln_lo(2, t)
                if t + 1 < NT:
                    ln_norm(2, t + 1)
                qs = q_stack[:, t].rearrange("p (h a d) -> p h a d", h=B_HEADS, a=4)
                ks = k_stack[:, t].rearrange("p (h u a d) -> p h u a d", h=KV_HEADS, u=2, a=4)
                dve.wait_ge(bq_ps, t + 1)
                if t:
                    dve.wait_ge(bkvlo, 5 * t)
                b_rope(bank[t % 2][:], D, t).then_inc(bq_rot, 1)
                dve.wait_ge(bq_rot, t + 1)
                src = rot[:].rearrange("p (h d) -> p h d", d=B_HD)
                dve.wait_ge(bqhi, 2 * t + 2)
                for a in (1, 3):
                    last = dve.tensor_tensor(qs[:, :, a], src, qs[:, :, a - 1], ALU.subtract)
                    last.then_inc(bqlo, 1)
                dve.wait_ge(bqlo, 2 * t + 2)
                dve.wait_ge(bkv_ps, t + 1)
                dve.wait_ge(bvhi, t) if t else None
                b_rope(bank[5 + t % 2][:, 0:P], P, t).then_inc(bk_rot, 1)
                dve.wait_ge(bk_rot, t + 1)
                src = rot[:, 0:P].rearrange("p (h d) -> p h d", d=B_HD)
                dve.wait_ge(bkhi, 4 * t + 4)
                for u in range(2):
                    for a in (2, 3):
                        dve.tensor_tensor(ks[:, :, u, a], src, ks[:, :, u, a - 2], ALU.subtract).then_inc(bkvlo, 1)
                dve.wait_ge(bvhi, t + 1)
                dve.scalar_tensor_tensor(out=bv_lo[:, t], in0=bank[5 + t % 2][:, P:2 * P], scalar=PROJ_DN_B,
                                         in1=bv_hi[:, t], op0=ALU.mult, op1=ALU.subtract).then_inc(bkvlo, 1)

            def b_ctx(j, s):
                hh, b = s // B, s % B
                n = 8 * j + s
                dve.wait_ge(bctx_ps, n + 1)
                dve.wait_ge(brden, n + 1)
                dve.tensor_tensor(ctx_b[:, b * ST:(b + 1) * ST, bass.ds(j * (GROUP * B_HD) + hh * B_HD, B_HD)],
                                  bank[5][:, 0:ST * B_HD].rearrange("p (i d) -> p i d", d=B_HD),
                                  rden[:, s % 2].unsqueeze(2).broadcast_to([P, ST, B_HD]), ALU.mult).then_inc(bctx, 1)

            with dve.Fori(0, KV_HEADS) as j:
                for s in range(9):
                    if s < 8:
                        row_max(8 * j + s, s % 2, bs_ps, bsmax, bshift, c_score_b)
                    if s:
                        for piece, bk in ((0, 3), (1, 4), (2, 6)):
                            pt_low(24 * j + 3 * (s - 1), piece, bpthi, bpt, bk, P_UP)
                    if s < 8:
                        dve.wait_ge(bexp, 4 * (8 * j + s) + 4)
                        dve.reciprocal(rden[:, s % 2], rsum[:, s % 2]).then_inc(brden, 1)
                    if s:
                        b_ctx(j, s - 1)
            for t in range(NT):
                m_low(NT + t, 1.0 / P_UP)
                y_add(NT + t, t, c_out_b)
                ln_stats(3, t)
            experts(1, None)


def constants():
    pos = np.arange(S, dtype=np.float32)
    inv = (np.float32(1.0) / np.float32(10000.0) ** (np.arange(0, A_HD, 2, dtype=np.float32) / np.float32(A_HD)))
    f = pos[:, None] * inv.astype(np.float32)[None, :]
    cos, sin = np.cos(f).T.astype(np.float32), np.sin(f).T.astype(np.float32)
    cos_a = np.concatenate([cos, cos]) * np.float32(PROJ_DN)
    sin_a = np.concatenate([sin, -sin]) * np.float32(PROJ_DN)

    theta, factor, hi, lo, ctx_len = 500000.0, 32.0, 4.0, 1.0, 1024
    idx = np.arange(0, B_HD, 2, dtype=np.float32) / np.float32(B_HD)
    freq = np.float32(1.0 / (2.0 * np.pi)) * (np.float32(theta) ** (-idx)).astype(np.float32)
    scaled = np.where(freq < lo / ctx_len, freq / np.float32(factor), freq)
    smooth = np.clip((ctx_len * freq - np.float32(lo)) / np.float32(hi - lo), 0.0, 1.0).astype(np.float32)
    mid = (1 - smooth) * (freq / np.float32(factor)) + smooth * freq
    freq = np.where((freq >= lo / ctx_len) & (freq <= hi / ctx_len), mid, scaled).astype(np.float32)
    phase = (np.float32(2.0 * np.pi) * pos)[:, None] * freq[None, :]
    table = lambda a: np.ascontiguousarray(
        (a.astype(np.float32) * np.float32(PROJ_DN_B)).reshape(ST, P, B_HD // 2).transpose(1, 0, 2))
    i = np.arange(P)
    mask = np.where(i[None, :] <= i[:, None], 0.0, MASKED).astype(np.float32)
    return {"ident": np.eye(P, dtype=np.float32), "mask": mask, "cos_a": cos_a.astype(np.float32),
            "sin_a": sin_a.astype(np.float32), "cos_b": table(np.cos(phase)), "sin_b": table(np.sin(phase))}


def kernel(**inputs):
    import concourse.bacc as bacc
    from concourse.bass_utils import run_bass_kernel_spmd

    a = {n: np.asarray(v) for n, v in inputs.items()}
    pre = "L0_attn_a_"
    tiles = lambda w: w.reshape(KT, P, -1).transpose(1, 0, 2).reshape(P, -1)

    def even_odd(w, heads):
        return w.reshape(-1, heads, A_HD // 2, 2).swapaxes(2, 3).reshape(w.shape)

    def by_group(w):
        return w.reshape(KT, P, KV_HEADS, -1).transpose(2, 1, 0, 3)

    def scales_by_group(w):
        return w.reshape(KT, KV_HEADS, -1).transpose(1, 0, 2).reshape(-1)

    q, k = even_odd(a[pre + "q_codes"], A_HEADS), even_odd(a[pre + "k_codes"], KV_HEADS)
    qs, ks = even_odd(a[pre + "q_scales"], A_HEADS), even_odd(a[pre + "k_scales"], KV_HEADS)
    lora_a, lora_b = a["L0_ffn_lora_A"], a["L0_ffn_lora_B"]
    arrays = {
        "x": a[pre + "hidden_states"],
        "q_codes": by_group(q), "k_codes": by_group(k), "v_codes": by_group(a[pre + "v_codes"]),
        "o_codes": a[pre + "o_codes"].reshape(KV_HEADS, GROUP, P, D).transpose(0, 2, 1, 3),
        "q_scales": scales_by_group(qs), "k_scales": scales_by_group(ks),
        "v_scales": scales_by_group(a[pre + "v_scales"]), "o_scales": a[pre + "o_scales"].reshape(-1),
        "lora_a": tiles(lora_a.reshape(EXPERTS * RANK, D).T),
        "lora_b": tiles(lora_b.transpose(0, 2, 1).reshape(EXPERTS * RANK, D)),
        "b_q": tiles(a["L0_attn_b_Wq"]), "b_o": tiles(a["L0_attn_b_Wo"]),
        "b_kv": tiles(np.concatenate([a["L0_attn_b_Wk"], a["L0_attn_b_Wv"]], axis=1)),
        "gate": tiles(a["L0_ffn_gate_w"].T),
        **constants(),
    }
    nc = bacc.Bacc("TRN2", target_bir_lowering=False, num_devices=1)
    arrays = {f"in_{n}": np.ascontiguousarray(v) for n, v in arrays.items()}
    t_in = {n[3:]: nc.dram_tensor(n, v.shape, mybir.dt.from_np(v.dtype), kind="ExternalInput").ap()
            for n, v in arrays.items()}
    out = nc.dram_tensor("out", (B, S, D), F32, kind="ExternalOutput").ap()
    build(nc, t_in, out)
    r = run_bass_kernel_spmd(nc, [arrays], core_ids=[0])
    return r.results[0]["out"]
```

```python
from contextlib import ExitStack

import numpy as np

import concourse.bass as bass
from concourse import mybir

F32 = mybir.dt.float32
F16 = mybir.dt.float16
BF16 = mybir.dt.bfloat16
I32 = mybir.dt.int32
U32 = mybir.dt.uint32
ALU = mybir.AluOpType
ACT = mybir.ActivationFunctionType
AX = mybir.AxisListType.X

P = 128
B, S, D = 2, 512, 512
TOK = B * S
NT = TOK // P
ST = S // P
KT = D // P
EPS = 1e-5

A_HEADS, KV_HEADS, A_HD = 32, 8, 128
GROUP = A_HEADS // KV_HEADS
B_HEADS, B_HD = 32, 16
B_ST = 4 * B_HD
EXPERTS, RANK = 8, 64

X_UP = 2.0 ** 10
W_UP = 2.0 ** 10
PROJ_DN = 2.0 ** -18
PROJ_DN_B = 2.0 ** -15
P_UP = 2.0 ** 15
MASKED = -1e30

S_OFF = [0, P, 3 * P, 6 * P]
TRI = 10 * P
S_BANK = [(0, 0), (1, 0), (0, P), (2, 0)]
S_ORDER = (0, 2, 1, 3)
S_PLACE = {0: 0, 2: 1, 1: 2, 3: 3}
PT_BANK = [3, 4, 7]
O_BANK = [6, 6, 6, 0, 1, 2, 6, 0]
PROJ = [("k", 0), ("q", 0), ("q", 1), ("v", 0), ("q", 2), ("q", 3), ("k", 1), ("q", 4), ("v", 1), ("q", 5), ("q", 6),
        ("q", 7)]
PROJ_BANK = [3, 4, 6, 7, 6, 6, 6, 6, 6, 6, 6, 6]
V_AT = [PROJ.index(("v", b)) for b in range(B)]
ROT_AT = [i for i, (n, _) in enumerate(PROJ) if n != "v"]
HEAD = 4
MID = {0: 4, 1: 5, 2: 7, 3: 9, 4: 10, 5: 11}
LATE = {1: 6, 2: 8}
O_MID = {6: 1, 7: 2}
O_LATE = {5: 0}
T_OFF = {0: 0, 1: S, 3: S + 3 * P, 2: 2 * S}

WEIGHTS = ("lora_a", "lora_b", "b_q", "b_kv", "b_o", "gate")
W_COLS = {"lora_a": KT * EXPERTS * RANK, "lora_b": KT * D, "b_q": KT * D, "b_kv": KT * 2 * KV_HEADS * B_HD,
          "b_o": KT * D, "gate": KT * EXPERTS}
QUANT = ("q", "k", "v", "o")
QUANT_COLS = {"q": P, "k": P // 4, "v": P // 4, "o": P}


def build(nc, t_in, out):
    ctx = ExitStack()
    with ctx:
        def sb(name, shape, dt):
            return ctx.enter_context(nc.sbuf_tensor(name, shape, dt))

        def sem(name):
            return ctx.enter_context(nc.semaphore(name))

        bank = [ctx.enter_context(nc.psum_tensor(f"bank{i}", [P, 512], F32)) for i in range(8)]

        x = sb("x", [P, NT, D], F32)
        xt_hi = sb("xt_hi", [P, KT, TOK], F16)
        xt_lo = sb("xt_lo", [P, KT, TOK], F16)
        xn = sb("xn", [P, 2, D], F32)
        ident = sb("ident", [P, P], F32)
        ident_h = sb("ident_h", [P, P], F16)
        ident_b = sb("ident_b", [P, P], BF16)
        mask_f = sb("mask_f", [P, P], F32)
        mask_b = sb("mask_b", [P, P], BF16)
        cos_b = sb("cos_b", [P, ST, B_HD // 2], F32)
        sin_b = sb("sin_b", [P, ST, B_HD // 2], F32)
        iota_e = sb("iota_e", [P, EXPERTS], F32)
        minus_half = sb("minus_half", [P, 1], F32)
        bn = sb("bn", [P, NT, 6], F32)
        mv = sb("mv", [P, NT, 2], F32)
        rstd = sb("rstd", [P, NT], F32)
        w_hi = {n: sb(f"{n}_hi", [P, W_COLS[n]], F16) for n in WEIGHTS}
        w_lo = {n: sb(f"{n}_lo", [P, W_COLS[n]], F16) for n in WEIGHTS}
        amax_w = sb("amax_w", [P, 8], F32)
        pow_w = sb("pow_w", [P, 8], F32)
        inv_w = sb("inv_w", [P, 8], F32)
        amax_q = sb("amax_q", [P, 4], F32)
        pow_q = sb("pow_q", [P, 4], F32)
        inv_q = sb("inv_q", [P, 4], F32)
        c_score = sb("c_score", [P, 2], F32)
        c_out = sb("c_out", [P, 1], F32)
        c_score_b = sb("c_score_b", [P, 2], F32)
        c_out_b = sb("c_out_b", [P, 1], F32)
        c_ffn = sb("c_ffn", [P, 1], F32)
        c_gate = sb("c_gate", [P, 1], F32)
        smax = sb("smax", [P, 2, ST], F32)
        shift = sb("shift", [P, 2, ST], F32)
        rsum = sb("rsum", [P, 2, ST], F32)
        rden = sb("rden", [P, 2, ST], F32)
        prob = sb("prob", [P, 2, TRI], F32)
        pt_hi = sb("pt_hi", [P, TRI], F16)
        pt_lo = sb("pt_lo", [P, TRI], F16)

        a_ctx = ExitStack()

        def sa(name, shape, dt):
            return a_ctx.enter_context(nc.sbuf_tensor(name, shape, dt))

        cos_a = sa("cos_a", [P, S], F32)
        sin_a = sa("sin_a", [P, S], F32)
        scn = sa("scn", [P, sum(QUANT_COLS.values())], F32)
        qcode = sa("qcode", [P, KT, 512], I32)
        qcode_f = qcode[:].bitcast(F32)
        qscale = sa("qscale", [P, KT, 512], F32)
        kvcode = sa("kvcode", [P, 2, KT, P], I32)
        kvcode_f = kvcode[:].bitcast(F32)
        kvscale = sa("kvscale", [P, 2, KT, P], F32)
        ocode = sa("ocode", [P, GROUP, D], I32)
        ocode_f = ocode[:].bitcast(F32)
        oscale = sa("oscale", [P, GROUP, D], F32)
        wq_hi = sa("wq_hi", [P, KT, 512], F16)
        wq_lo = sa("wq_lo", [P, KT, 512], F16)
        wkv_hi = sa("wkv_hi", [P, 2, KT, P], F16)
        wkv_lo = sa("wkv_lo", [P, 2, KT, P], F16)
        wo_hi = sa("wo_hi", [P, GROUP, D], F16)
        wo_lo = sa("wo_lo", [P, GROUP, D], F16)
        rt1 = sa("rt1", [P, 2, S], F32)
        rt2 = sa("rt2", [P, 2, S], F32)
        arena = sa("arena", [P, 10 * 1024], F32)
        q_hi = arena[:, 0:2048].bitcast(F16).rearrange("p (s n) -> p s n", s=8)
        q_lo = arena[:, 2048:4096].bitcast(F16).rearrange("p (s n) -> p s n", s=8)
        ctx_hi = arena[:, 4096:6144].bitcast(F16).rearrange("p (s n) -> p s n", s=8)
        ctx_lo = arena[:, 6144:8192].bitcast(F16).rearrange("p (s n) -> p s n", s=8)
        k_hi = arena[:, 8192:8704].bitcast(F16).rearrange("p (s n) -> p s n", s=B)
        k_lo = arena[:, 8704:9216].bitcast(F16).rearrange("p (s n) -> p s n", s=B)
        v_hi = arena[:, 9216:9728].bitcast(F16).rearrange("p (s n) -> p s n", s=B)
        v_lo = arena[:, 9728:10240].bitcast(F16).rearrange("p (s n) -> p s n", s=B)
        raw, at = {}, 0
        for n in WEIGHTS:
            raw[n] = arena[:, at:at + W_COLS[n]]
            at += W_COLS[n]
        assert at <= 10 * 1024
        a_ctx.close()

        r1 = sb("r1", [P, D], F32)
        r2 = sb("r2", [P, D], F32)
        rot = sb("rot", [P, D], F32)
        q_stack = sb("q_stack", [P, NT, B_HEADS * B_ST], F16)
        k_stack = sb("k_stack", [P, NT, KV_HEADS * 2 * B_ST], F16)
        bv_hi = sb("bv_hi", [P, NT, KV_HEADS * B_HD], F16)
        bv_lo = sb("bv_lo", [P, NT, KV_HEADS * B_HD], F16)
        qkt = sb("qkt", [P, 6, S], F16)
        ctx_b = sb("ctx_b", [P, NT, D], F32)
        hs = sb("hs", [P, 2, D], F32)
        mt_hi = sb("mt_hi", [P, 2, D], F16)
        mt_lo = sb("mt_lo", [P, 2, D], F16)
        lg = sb("lg", [P, 2, 8], F32)
        top = sb("top", [P, 2, 8], F32)
        topi = sb("topi", [P, 2, 8], U32)
        topf = sb("topf", [P, 2, 8], F32)
        dif = sb("dif", [P, 2, 2], F32)
        ex = sb("ex", [P, 2, 2], F32)
        exs = sb("exs", [P, 2, 1], F32)
        exr = sb("exr", [P, 2, 1], F32)
        wgt = sb("wgt", [P, 2, 2], F32)
        oh0 = sb("oh0", [P, 2, 8], F32)
        oh1 = sb("oh1", [P, 2, 8], F32)
        wfull = sb("wfull", [P, 2, 8], F32)

        scr = {n: nc.dram_tensor(f"scales_{n}", (P * QUANT_COLS[n],), F32).ap() for n in QUANT}

        d_const, d_x, d_scale, d_raw, d_scr, d_out = (sem(n) for n in (
            "d_const", "d_x", "d_scale", "d_raw", "d_scr", "d_out"))
        consts, chain, amaxq_done, amaxw_done, redq, redw, invq_done, invw_done, scn_done, whi_done, wlo_done = (
            sem(n) for n in ("consts", "chain", "amaxq_done", "amaxw_done", "redq", "redw", "invq_done",
                             "invw_done", "scn_done", "whi_done", "wlo_done"))
        ln_stat, ln_rstd, xn_ready, xt_ps, xthi_done, xt_done = (sem(n) for n in (
            "ln_stat", "ln_rstd", "xn_ready", "xt_ps", "xthi_done", "xt_done"))
        d_q, d_kv, d_o = sem("d_q"), sem("d_kv"), sem("d_o")
        wfull_done = sem("wfull_done")
        whi, w32_done, q_code, kv_code, o_code = (sem(n) for n in ("whi", "w32_done", "q_code", "kv_code", "o_code"))
        q_w, kv_w, o_w = sem("q_w"), sem("kv_w"), sem("o_w")
        proj_ps, proj_read, rot_ready, rothi_done, rot_done, vhi_done = (sem(n) for n in (
            "proj_ps", "proj_read", "rot_ready", "rothi_done", "rot_done", "vhi_done"))
        s_ps, smax_done, shift_done, exp_done, rden_done, prob_done = (sem(n) for n in (
            "s_ps", "smax_done", "shift_done", "exp_done", "rden_done", "prob_done"))
        pt_ps, pthi_done, pt_done, ctx_ps, ctxhi_done, ctx_done, o_ps, o_added = (sem(n) for n in (
            "pt_ps", "pthi_done", "pt_done", "ctx_ps", "ctxhi_done", "ctx_done", "o_ps", "o_added"))
        g_ps, lg_done, dif_done, ex_done, gch, h_ps, hs_done, mt_ps, mthi_done, mt_done, y_ps, y_added = (
            sem(n) for n in ("g_ps", "lg_done", "dif_done", "ex_done", "gch", "h_ps", "hs_done", "mt_ps",
                             "mthi_done", "mt_done", "y_ps", "y_added"))
        bq_ps, bkv_ps, bch, bq_rot, bk_rot, bqhi, bkhi, bvhi, bqlo, bkvlo = (sem(n) for n in (
            "bq_ps", "bkv_ps", "bch", "bq_rot", "bk_rot", "bqhi", "bkhi", "bvhi", "bqlo", "bkvlo"))
        bt_ps, bt_done, bs_ps, bsmax, bshift, bexp, brden, bpt_ps, bpthi, bpt, bctx_ps, bctx = (sem(n) for n in (
            "bt_ps", "bt_done", "bs_ps", "bsmax", "bshift", "bexp", "brden", "bpt_ps", "bpthi", "bpt",
            "bctx_ps", "bctx"))

        block = ctx.enter_context(nc.Block())
        N_CONST = 6

        @block.sync
        def _(sp):
            x_in = t_in["x"].rearrange("b s d -> (b s) d").rearrange("(t p) d -> p t d", p=P)
            sp.dma_start(x[:, 0:ST, :], x_in[:, 0:ST, :]).then_inc(d_x, 16)
            off = 0
            for n in QUANT:
                w = QUANT_COLS[n]
                sp.dma_start(scn[:, off:off + w], t_in[f"{n}_scales"].rearrange("(p f) -> p f", p=P)
                             ).then_inc(d_scale, 16)
                off += w
            sp.dma_start(x[:, ST:NT, :], x_in[:, ST:NT, :]).then_inc(d_x, 16)
            for dst, src in ((ident, "ident"), (mask_f, "mask"), (cos_a, "cos_a"), (sin_a, "sin_a"),
                             (cos_b, "cos_b"), (sin_b, "sin_b")):
                sp.dma_start(dst[:], t_in[src]).then_inc(d_const, 16)

            def load_q(j):
                sp.dma_start(qcode[:], t_in["q_codes"][bass.ds(j, 1)].rearrange("o p g n -> (o p) g n")
                             ).then_inc(d_q, 16)
                sp.dma_start(qscale[:].rearrange("p g n -> p (g n)"),
                             scr["q"][bass.ds(j * 2048, 2048)].partition_broadcast(P)).then_inc(d_q, 16)

            def load_kv(j):
                for i, n in enumerate("kv"):
                    sp.dma_start(kvcode[:, i], t_in[f"{n}_codes"][bass.ds(j, 1)].rearrange("o p g n -> (o p) g n")
                                 ).then_inc(d_kv, 16)
                    sp.dma_start(kvscale[:, i].rearrange("p g n -> p (g n)"),
                                 scr[n][bass.ds(j * 512, 512)].partition_broadcast(P)).then_inc(d_kv, 16)

            def load_o(j):
                sp.dma_start(ocode[:], t_in["o_codes"][bass.ds(j, 1)].rearrange("o p g n -> (o p) g n")
                             ).then_inc(d_o, 16)
                sp.dma_start(oscale[:].rearrange("p g n -> p (g n)"),
                             scr["o"][bass.ds(j * 2048, 2048)].partition_broadcast(P)).then_inc(d_o, 16)

            off = 0
            sp.wait_ge(scn_done, 4)
            for n in QUANT:
                w = QUANT_COLS[n]
                sp.dma_start(scr[n].rearrange("(p f) -> p f", p=P), scn[:, off:off + w]).then_inc(d_scr, 16)
                off += w
            sp.wait_ge(d_scr, 64)
            load_kv(0)
            load_q(0)
            load_o(0)
            for n in WEIGHTS:
                sp.dma_start(raw[n], t_in[n]).then_inc(d_raw, 16)
            with sp.Fori(0, KV_HEADS - 1) as j:
                sp.wait_ge(kv_w, 2 * j + 2)
                load_kv(j + 1)
                sp.wait_ge(q_w, 4 * j + 4)
                load_q(j + 1)
                sp.wait_ge(o_w, 4 * j + 4)
                load_o(j + 1)
            o_out = out.rearrange("b s d -> (b s) d").rearrange("(t p) d -> p t d", p=P)
            for t in range(NT):
                sp.wait_ge(y_added, NT + B * ST + t + 1)
                sp.dma_start(o_out[:, t, :], x[:, t, :]).then_inc(d_out, 16)
            sp.wait_ge(d_out, 16 * NT)

        @block.gpsimd
        def _(pool):
            pool.memset(minus_half[:], -0.5).then_inc(consts, 1)
            pool.iota(iota_e[:], pattern=[[1, EXPERTS]], base=0, channel_multiplier=0,
                      allow_small_or_imprecise_dtypes=True).then_inc(consts, 1)
            pool.wait_ge(consts, 2)

            def ln_rsqrt(c, t):
                pool.wait_ge(ln_stat, 3 * (NT * c + t) + 3)
                pool.tensor_tensor(rstd[:, t:t + 1], mv[:, t, 1:2], minus_half[:], ALU.pow).then_inc(ln_rstd, 1)

            pool.wait_ge(amaxq_done, 4)
            pool.partition_all_reduce(pow_q[:], amax_q[:], P, bass.bass_isa.ReduceOp.max).then_inc(redq, 1)
            for t in range(NT):
                ln_rsqrt(0, t)

            def dequant(n, code, scale, hi, lo):
                pool.tensor_tensor(hi, code, scale, ALU.mult).then_inc(whi, 1)
                pool.tensor_tensor(code, code, scale, ALU.mult).then_inc(w32_done, 1)
                pool.wait_ge(whi, n + 1)
                pool.wait_ge(w32_done, n + 1)
                return pool.tensor_tensor(lo, code, hi, ALU.subtract)

            def deq_kv(j, i, n):
                pool.wait_ge(kv_code, j + 1)
                flat = lambda a: a[:, i].rearrange("p g n -> p (g n)")
                dequant(n, flat(kvcode_f), flat(kvscale), flat(wkv_hi), flat(wkv_lo)).then_inc(kv_w, 1)

            def deq_q(j, g, n):
                pool.wait_ge(q_code, j + 1)
                dequant(n, qcode_f[:, g], qscale[:, g], wq_hi[:, g], wq_lo[:, g]).then_inc(q_w, 1)

            def deq_o(j, g, n):
                pool.wait_ge(o_code, j + 1)
                dequant(n, ocode_f[:, g], oscale[:, g], wo_hi[:, g], wo_lo[:, g]).then_inc(o_w, 1)

            def rope_add(j, u, idx):
                pool.wait_ge(proj_read, 12 * j + idx + 1)
                pool.tensor_tensor(rt1[:, u % 2], rt1[:, u % 2], rt2[:, u % 2], ALU.add).then_inc(rot_ready, 1)

            def rope_lo(j, u, dst, src):
                pool.wait_ge(rothi_done, 10 * j + u + 1)
                pool.tensor_tensor(dst, rt1[:, u % 2], src, ALU.subtract).then_inc(rot_done, 1)

            rot_dst = [(k_lo[:, i], k_hi[:, i]) if n == "k" else (q_lo[:, i], q_hi[:, i])
                       for n, i in PROJ if n != "v"]

            def group(j, last):
                n0 = 10 * j + 6
                o_piece = {3: 0, 4: 1, 6: 2, 7: 3}
                for u in range(10):
                    rope_add(j, u, ROT_AT[u])
                    if u in o_piece:
                        deq_o(j, o_piece[u], n0 + o_piece[u])
                    if u == 4:
                        continue
                    if u == 5:
                        rope_lo(j, 4, *rot_dst[4])
                    rope_lo(j, u, *rot_dst[u])
                    if u >= 8 and not last:
                        deq_kv(j + 1, u - 8, n0 + u - 4)
                if not last:
                    for g in range(KT):
                        deq_q(j + 1, g, n0 + 6 + g)

            for i in range(2):
                deq_kv(0, i, i)
            for g in range(KT):
                deq_q(0, g, 2 + g)
            pool.wait_ge(amaxw_done, len(WEIGHTS))
            pool.partition_all_reduce(pow_w[:, 0:len(WEIGHTS)], amax_w[:, 0:len(WEIGHTS)], P,
                                      bass.bass_isa.ReduceOp.max).then_inc(redw, 1)
            with pool.Fori(0, KV_HEADS - 1) as j:
                group(j, False)
            group(KV_HEADS - 1, True)
            for c in range(1, 4):
                for t in range(NT):
                    ln_rsqrt(c, t)

        @block.scalar
        def _(act):
            def ln_hi(c, t):
                act.wait_ge(xt_ps, NT * c + t + 1)
                act.activation(xt_hi[:, :, t * P:(t + 1) * P], bank[3 + t % 2][:].rearrange("p (k n) -> p k n", k=KT),
                               ACT.Copy, scale=X_UP).then_inc(xthi_done, 1)

            def codes(j, code, code_f, loaded, count, done):
                act.wait_ge(loaded, count)
                act.activation(code_f[:].rearrange("p a b -> p (a b)") if len(code_f.shape) == 3 else
                               code_f[:].rearrange("p i a b -> p (i a b)"),
                               code[:].rearrange("p a b -> p (a b)") if len(code.shape) == 3 else
                               code[:].rearrange("p i a b -> p (i a b)"), ACT.Copy, bias=-8.0).then_inc(done, 1)

            for t in range(NT):
                ln_hi(0, t)
            codes(0, kvcode, kvcode_f, d_kv, 64, kv_code)
            codes(0, qcode, qcode_f, d_q, 32, q_code)
            act.wait_ge(invw_done, 1)
            act.wait_ge(d_raw, 16 * len(WEIGHTS))
            for i, n in enumerate(WEIGHTS):
                act.activation(w_hi[n][:], raw[n], ACT.Copy, scale=inv_w[:, i:i + 1]).then_inc(whi_done, 1)

            rot_hi = [k_hi[:, i] if n == "k" else q_hi[:, i] for n, i in PROJ if n != "v"]

            def rope_hi(j, u):
                act.wait_ge(rot_ready, 10 * j + u + 1)
                act.activation(rot_hi[u], rt1[:, u % 2], ACT.Copy).then_inc(rothi_done, 1)

            def v_high(j, b):
                act.wait_ge(proj_ps, 12 * j + V_AT[b] + 1)
                act.activation(v_hi[:, b], bank[PROJ_BANK[V_AT[b]]][:], ACT.Copy, scale=PROJ_DN).then_inc(vhi_done, 1)

            def exps(n, i2, score, ready, done):
                for i in S_ORDER:
                    bk, o = S_BANK[i]
                    w = (i + 1) * P
                    c = S_PLACE[i]
                    if i != 2:
                        act.wait_ge(ready, 3 * n + bk + 1)
                    act.activation(prob[:, i2, S_OFF[i]:S_OFF[i] + w], bank[bk][:, o:o + w], ACT.Exp,
                                   bias=shift[:, i2, c:c + 1], scale=score[:, 0:1],
                                   accum_out=rsum[:, i2, c:c + 1]).then_inc(done, 1)

            def pt_high(base, piece, ps, done, scale):
                w = S if piece < 2 else 2 * P
                act.wait_ge(ps, base + piece + 1)
                act.activation(pt_hi[:, piece * S:piece * S + w], bank[PT_BANK[piece]][:, 0:w], ACT.Copy,
                               scale=scale).then_inc(done, 1)

            def ctx_high(j, s):
                act.wait_ge(ctx_ps, 8 * j + s + 1)
                act.activation(ctx_hi[:, s], bank[5][:], ACT.Copy, scale=1.0 / P_UP).then_inc(ctxhi_done, 1)

            def evict(j, idx):
                if PROJ[idx][0] == "v":
                    v_high(j, PROJ[idx][1])
                else:
                    rope_hi(j, ROT_AT.index(idx))

            def group(j, last):
                for idx in range(HEAD):
                    evict(j, idx)
                codes(j, ocode, ocode_f, d_o, 32 * j + 32, o_code)
                for s in range(8):
                    if s - 1 in LATE and PROJ[LATE[s - 1]][0] == "v":
                        evict(j, LATE[s - 1])
                    if s:
                        for piece in range(3):
                            pt_high(24 * j + 3 * (s - 1), piece, pt_ps, pthi_done, 1.0)
                    if s - 1 in MID:
                        evict(j, MID[s - 1])
                    if s - 1 in LATE and PROJ[LATE[s - 1]][0] != "v":
                        evict(j, LATE[s - 1])
                    exps(8 * j + s, s % 2, c_score, shift_done, exp_done)
                    if s:
                        ctx_high(j, s - 1)
                    if s == 3 and not last:
                        codes(j, kvcode, kvcode_f, d_kv, 64 * (j + 1) + 64, kv_code)
                    if s == 4 and not last:
                        codes(j, qcode, qcode_f, d_q, 32 * (j + 1) + 32, q_code)
                for piece in range(3):
                    pt_high(24 * j + 21, piece, pt_ps, pthi_done, 1.0)
                ctx_high(j, 7)

            act.wait_ge(wlo_done, len(WEIGHTS))
            with act.Fori(0, KV_HEADS - 1) as j:
                group(j, False)
            group(KV_HEADS - 1, True)

            def m_high(m, src_scale):
                act.wait_ge(mt_ps, m + 1)
                act.activation(mt_hi[:, m % 2], bank[2][:], ACT.Copy, scale=src_scale).then_inc(mthi_done, 1)

            def experts(ph):
                c = 1 + 2 * ph
                m0 = ph * 2 * NT
                for t in range(NT):
                    ln_hi(c, t)
                    f = NT * ph + t
                    act.wait_ge(dif_done, f + 1)
                    act.activation(ex[:, t % 2], dif[:, t % 2], ACT.Exp, accum_out=exs[:, t % 2]).then_inc(ex_done, 1)
                    if t:
                        m_high(m0 + t - 1, PROJ_DN_B)
                m_high(m0 + NT - 1, PROJ_DN_B)

            experts(0)
            for t in range(NT):
                ln_hi(2, t)
                qs = q_stack[:, t].rearrange("p (h a d) -> p h a d", h=B_HEADS, a=4)
                ks = k_stack[:, t].rearrange("p (h u a d) -> p h u a d", h=KV_HEADS, u=2, a=4)
                act.wait_ge(bq_rot, t + 1)
                src = rot[:].rearrange("p (h d) -> p h d", d=B_HD)
                for a in (0, 2):
                    act.activation(qs[:, :, a], src, ACT.Copy).then_inc(bqhi, 1)
                act.wait_ge(bk_rot, t + 1)
                src = rot[:, 0:P].rearrange("p (h d) -> p h d", d=B_HD)
                for u in range(2):
                    for a in (0, 1):
                        act.activation(ks[:, :, u, a], src, ACT.Copy).then_inc(bkhi, 1)
                act.wait_ge(bkv_ps, t + 1)
                act.activation(bv_hi[:, t], bank[5 + t % 2][:, P:2 * P], ACT.Copy, scale=PROJ_DN_B).then_inc(bvhi, 1)
            with act.Fori(0, KV_HEADS) as j:
                for u in range(6):
                    act.wait_ge(bt_ps, 6 * j + u + 1)
                    act.activation(qkt[:, u], bank[3 + u % 2][:], ACT.Copy).then_inc(bt_done, 1)
                for s in range(9):
                    if s:
                        for piece in range(3):
                            pt_high(24 * j + 3 * (s - 1), piece, bpt_ps, bpthi, P_UP)
                    if s < 8:
                        exps(8 * j + s, s % 2, c_score_b, bshift, bexp)
            for t in range(NT):
                m_high(NT + t, 1.0 / P_UP)
            experts(1)

        @block.tensor
        def _(pe):
            def three(out_ap, a_hi, a_lo, b_hi, b_lo, k, n, stop=True):
                pe.matmul(out_ap, a_hi, b_hi, start=(k == 0), stop=False)
                pe.matmul(out_ap, a_hi, b_lo, start=False, stop=False)
                return pe.matmul(out_ap, a_lo, b_hi, start=False, stop=(stop and k == n - 1))

            def ln_t(c, t):
                i = NT * c + t
                pe.wait_ge(xn_ready, i + 1)
                if i >= 2:
                    pe.wait_ge(xt_done, i - 1)
                for k in range(KT):
                    mm = pe.transpose(bank[3 + t % 2][:, k * P:(k + 1) * P], xn[:, t % 2, k * P:(k + 1) * P], ident[:])
                mm.then_inc(xt_ps, 1)

            pe.wait_ge(d_const, 16 * N_CONST)
            for t in range(NT):
                ln_t(0, t)
            pe.wait_ge(chain, 3)
            pe.wait_ge(xt_done, NT)

            def project(j, idx):
                kind, s = PROJ[idx]
                o_ap = bank[PROJ_BANK[idx]]
                if idx == 2:
                    pe.wait_ge(proj_read, 12 * j + 1)
                if idx >= HEAD:
                    before = max(i for i in range(idx) if PROJ_BANK[i] == PROJ_BANK[idx])
                    pe.wait_ge(proj_read, 12 * j + before + 1)
                b = s if kind != "q" else s // GROUP
                cols = slice(b * S, (b + 1) * S)
                if idx == 0:
                    pe.wait_ge(kv_w, 2 * j + 2)
                if idx == 1:
                    pe.wait_ge(q_w, 4 * j + 4)
                if kind == "v":
                    for t in range(ST):
                        c0 = (b * ST + t) * P
                        for g in range(KT):
                            mm = three(o_ap[:, t * P:(t + 1) * P], xt_hi[:, g, c0:c0 + P], xt_lo[:, g, c0:c0 + P],
                                       wkv_hi[:, 1, g], wkv_lo[:, 1, g], g, KT)
                else:
                    for g in range(KT):
                        hd = slice(s % GROUP * P, (s % GROUP + 1) * P)
                        a_hi, a_lo = ((wkv_hi[:, 0, g], wkv_lo[:, 0, g]) if kind == "k" else
                                      (wq_hi[:, g, hd], wq_lo[:, g, hd]))
                        mm = three(o_ap[:], a_hi, a_lo, xt_hi[:, g, cols], xt_lo[:, g, cols], g, KT)
                mm.then_inc(proj_ps, 1)

            def scores(j, s):
                b = s // GROUP
                pe.wait_ge(rot_done, 10 * j + ROT_AT.index(PROJ.index(("q", s))) + 1)
                for i in S_ORDER:
                    bk, o = S_BANK[i]
                    w = (i + 1) * P
                    if i != 2 and s:
                        pe.wait_ge(exp_done, 4 * (8 * j + s - 1) + bk + 2)
                    o_ap = bank[bk][:, o:o + w]
                    qs = slice(i * P, (i + 1) * P)
                    pe.matmul(o_ap, q_hi[:, s, qs], k_hi[:, b, 0:w], start=True, stop=False)
                    pe.matmul(o_ap, q_hi[:, s, qs], k_lo[:, b, 0:w], start=False, stop=False)
                    pe.matmul(o_ap, q_lo[:, s, qs], k_hi[:, b, 0:w], start=False, stop=False)
                    mm = pe.matmul(bank[bk][:, o + w - P:o + w], ident_b[:], mask_b[:], start=False, stop=True)
                    if i != 0:
                        mm.then_inc(s_ps, 1)

            def transposes(n, piece, ready, need, ps, bk, i2):
                if piece == 0:
                    pe.wait_ge(ready, need)
                for k, tiles in enumerate([(0,), (1, 3), (2,)][piece]):
                    for i in range(tiles, ST):
                        o = T_OFF[tiles] - piece * S + (i - tiles) * P
                        mm = pe.transpose(bank[bk][:, o:o + P],
                                          prob[:, i2, S_OFF[i] + tiles * P:S_OFF[i] + (tiles + 1) * P], ident[:])
                mm.then_inc(ps, 1)

            def a_transposes(j, s):
                for piece in range(3):
                    if s:
                        pe.wait_ge(pt_done, 24 * j + 3 * (s - 1) + piece + 1)
                    elif piece == 2:
                        pe.wait_ge(proj_read, 12 * j + V_AT[0] + 1)
                    transposes(s, piece, prob_done, 4 * (8 * j + s) + 4, pt_ps, PT_BANK[piece], s % 2)

            def a_pv(j, s):
                b = s // GROUP
                if s % GROUP == 0:
                    pe.wait_ge(proj_read, 12 * j + V_AT[b] + 1)
                if s:
                    pe.wait_ge(ctx_done, 8 * j + s)
                for kt in (0, 1, 3, 2):
                    piece = {0: 0, 1: 1, 3: 1, 2: 2}[kt]
                    pe.wait_ge(pt_done, 24 * j + 3 * s + piece + 1)
                    w = S - kt * P
                    o_ap = bank[5][:, kt * P:S]
                    tc = slice(T_OFF[kt], T_OFF[kt] + w)
                    vs = slice(kt * P, (kt + 1) * P)
                    pe.matmul(o_ap, v_hi[:, b, vs], pt_hi[:, tc], start=(kt == 0), stop=False)
                    pe.matmul(o_ap, v_hi[:, b, vs], pt_lo[:, tc], start=False, stop=False)
                    mm = pe.matmul(o_ap, v_lo[:, b, vs], pt_hi[:, tc], start=False, stop=(kt == 2))
                mm.then_inc(ctx_ps, 1)

            def a_out(j, t):
                b = t // ST
                if t == 0:
                    pe.wait_ge(o_w, 4 * j + 4)
                    pe.wait_ge(ctx_done, 8 * j + GROUP)
                    pe.wait_ge(proj_read, 12 * j + 12)
                if t == 3:
                    pe.wait_ge(exp_done, 32 * j + 32)
                if O_BANK[t] in O_BANK[:t]:
                    before = max(i for i in range(t) if O_BANK[i] == O_BANK[t])
                    pe.wait_ge(o_added, NT * j + before + 1)
                ts = slice((t % ST) * P, (t % ST + 1) * P)
                for hh in range(GROUP):
                    if t == ST and hh == GROUP - 1:
                        pe.wait_ge(ctx_done, 8 * j + 8)
                    mm = three(bank[O_BANK[t]][:], ctx_hi[:, b * GROUP + hh, ts], ctx_lo[:, b * GROUP + hh, ts],
                               wo_hi[:, hh], wo_lo[:, hh], hh, GROUP)
                mm.then_inc(o_ps, 1)

            with pe.Fori(0, KV_HEADS) as j:
                for idx in range(HEAD):
                    project(j, idx)
                for s in range(8):
                    scores(j, s)
                    if s:
                        a_transposes(j, s - 1)
                    if s in MID:
                        project(j, MID[s])
                    if s in O_MID:
                        a_out(j, O_MID[s])
                    if s:
                        a_pv(j, s - 1)
                    if s in LATE:
                        project(j, LATE[s])
                    if s in O_LATE:
                        a_out(j, O_LATE[s])
                a_transposes(j, 7)
                a_out(j, 3)
                a_pv(j, 7)
                for t in range(ST, NT):
                    a_out(j, t)

            def back(m, src, name):
                if m >= 1:
                    pe.wait_ge(mt_done, m)
                for k in range(KT):
                    mm = pe.transpose(bank[2][:, k * P:(k + 1) * P], src[:, k * P:(k + 1) * P], ident[:])
                mm.then_inc(mt_ps, 1)
                pe.wait_ge(mt_done, m + 1)
                if m >= 2:
                    pe.wait_ge(y_added, m - 1)
                wh = w_hi[name][:].rearrange("p (k n) -> p k n", k=KT)
                wl = w_lo[name][:].rearrange("p (k n) -> p k n", k=KT)
                for k in range(KT):
                    ks = slice(k * P, (k + 1) * P)
                    mm = three(bank[6 + m % 2][:], mt_hi[:, m % 2, ks], mt_lo[:, m % 2, ks], wh[:, k], wl[:, k], k, KT)
                mm.then_inc(y_ps, 1)

            def wide(out_ap, t, name, n):
                wh = w_hi[name][:].rearrange("p (k n) -> p k n", k=KT)
                wl = w_lo[name][:].rearrange("p (k n) -> p k n", k=KT)
                ts = slice(t * P, (t + 1) * P)
                for k in range(KT):
                    mm = three(out_ap, xt_hi[:, k, ts], xt_lo[:, k, ts], wh[:, k], wl[:, k], k, KT)
                return mm

            def experts(ph):
                c = 1 + 2 * ph
                m0 = ph * 2 * NT
                for t in range(NT):
                    f = NT * ph + t
                    ln_t(c, t)
                    pe.wait_ge(xt_done, NT * c + t + 1)
                    if f:
                        pe.wait_ge(lg_done, f)
                    wide(bank[5][:, 0:EXPERTS], t, "gate", EXPERTS).then_inc(g_ps, 1)
                    if f >= 2:
                        pe.wait_ge(hs_done, f - 1)
                    wide(bank[t % 2][:], t, "lora_a", D).then_inc(h_ps, 1)
                    if t:
                        pe.wait_ge(hs_done, f)
                        back(m0 + t - 1, hs[:, (t - 1) % 2], "lora_b")
                pe.wait_ge(hs_done, NT * ph + NT)
                back(m0 + NT - 1, hs[:, (NT - 1) % 2], "lora_b")

            experts(0)
            for t in range(NT):
                ln_t(2, t)
                pe.wait_ge(xt_done, NT * 2 + t + 1)
                if t >= 2:
                    pe.wait_ge(bq_rot, t - 1)
                wide(bank[t % 2][:], t, "b_q", D).then_inc(bq_ps, 1)
                if t >= 2:
                    pe.wait_ge(bkvlo, 5 * (t - 1))
                wide(bank[5 + t % 2][:, 0:2 * P], t, "b_kv", 2 * P).then_inc(bkv_ps, 1)
            pe.wait_ge(bqlo, 2 * NT)
            pe.wait_ge(bkvlo, 5 * NT)

            def b_scores(j, s):
                hh, b = s // B, s % B
                rows = slice((hh % 2) * B_ST, (hh % 2 + 1) * B_ST)
                qt = qkt[rows, hh // 2 * B + b]
                kk = qkt[rows, 4 + b]
                for i in S_ORDER:
                    bk, o = S_BANK[i]
                    w = (i + 1) * P
                    if i != 2 and s:
                        pe.wait_ge(bexp, 4 * (8 * j + s - 1) + bk + 2)
                    pe.matmul(bank[bk][:, o:o + w], qt[:, i * P:(i + 1) * P], kk[:, 0:w], start=True, stop=False)
                    mm = pe.matmul(bank[bk][:, o + w - P:o + w], ident_b[:], mask_b[:], start=False, stop=True)
                    if i != 0:
                        mm.then_inc(bs_ps, 1)

            def b_pv(j, s):
                hh, b = s // B, s % B
                if s:
                    pe.wait_ge(bctx, 8 * j + s)
                pe.wait_ge(bpt, 24 * j + 3 * s + 3)
                vc = bass.ds(j * B_HD, B_HD)
                for i in range(ST):
                    o_ap = bank[5][:, i * B_HD:(i + 1) * B_HD]
                    for kt in range(i + 1):
                        tc = slice(T_OFF[kt] + (i - kt) * P, T_OFF[kt] + (i - kt + 1) * P)
                        vh, vl = bv_hi[:, b * ST + kt, vc], bv_lo[:, b * ST + kt, vc]
                        mm = three(o_ap, pt_hi[:, tc], pt_lo[:, tc], vh, vl, kt, i + 1)
                mm.then_inc(bctx_ps, 1)

            with pe.Fori(0, KV_HEADS) as j:
                for u in range(6):
                    if u >= 2:
                        pe.wait_ge(bt_done, 6 * j + u - 1)
                    for t in range(ST):
                        if u < 4:
                            src = q_stack[:, (u % 2) * ST + t, bass.ds(j * (GROUP * B_ST) + (u // 2) * P, P)]
                        else:
                            src = k_stack[:, (u % 2) * ST + t, bass.ds(j * P, P)]
                        mm = pe.matmul(bank[3 + u % 2][:, t * P:(t + 1) * P], src, ident_h[:], start=True, stop=True)
                    mm.then_inc(bt_ps, 1)
                pe.wait_ge(bt_done, 6 * j + 6)
                for s in range(9):
                    if s < 8:
                        b_scores(j, s)
                    if s:
                        for piece in range(3):
                            if s > 1:
                                pe.wait_ge(bpt, 24 * j + 3 * (s - 2) + piece + 1)
                            transposes(s - 1, piece, bexp, 4 * (8 * j + s - 1) + 4, bpt_ps, PT_BANK[piece], (s - 1) % 2)
                        b_pv(j, s - 1)
            pe.wait_ge(bctx, 8 * KV_HEADS)
            for t in range(NT):
                back(NT + t, ctx_b[:, t], "b_o")
            experts(1)

        @block.vector
        def _(dve):
            off = 0
            dve.wait_ge(d_scale, 64)
            for i, n in enumerate(QUANT):
                w = QUANT_COLS[n]
                dve.tensor_reduce(amax_q[:, i:i + 1], scn[:, off:off + w], AX, ALU.max,
                                  apply_absolute_value=True).then_inc(amaxq_done, 1)
                off += w

            def power_of_two(value, inv, n, red, done):
                dve.wait_ge(red, 1)
                dve.tensor_scalar(value[:, 0:n], value[:, 0:n], 1e-30, None, ALU.max).then_inc(red, 1)
                dve.wait_ge(red, 2)
                dve.tensor_single_scalar(value[:, 0:n].bitcast(U32), value[:, 0:n].bitcast(U32), 0x7F800000,
                                         ALU.bitwise_and).then_inc(red, 1)
                dve.wait_ge(red, 3)
                dve.reciprocal(inv[:, 0:n], value[:, 0:n]).then_inc(red, 1)
                dve.wait_ge(red, 4)
                dve.tensor_scalar(inv[:, 0:n], inv[:, 0:n], W_UP, None, ALU.mult).then_inc(done, 1)
                dve.wait_ge(done, 1)

            def ln_stats(c, t):
                i = 3 * (NT * c + t)
                dve.bn_stats(bn[:, t], x[:, t]).then_inc(ln_stat, 1)
                dve.wait_ge(ln_stat, i + 1)
                dve.bn_aggr(mv[:, t], bn[:, t]).then_inc(ln_stat, 1)
                dve.wait_ge(ln_stat, i + 2)
                dve.tensor_scalar(mv[:, t, 1:2], mv[:, t, 1:2], EPS, None, ALU.add).then_inc(ln_stat, 1)

            def ln_norm(c, t):
                i = NT * c + t
                if i >= 2:
                    dve.wait_ge(xt_ps, i - 1)
                dve.wait_ge(ln_rstd, i + 1)
                dve.tensor_scalar(xn[:, t % 2], x[:, t], mv[:, t, 0:1], rstd[:, t:t + 1], ALU.subtract,
                                  ALU.mult).then_inc(xn_ready, 1)

            def ln_lo(c, t):
                dve.wait_ge(xthi_done, NT * c + t + 1)
                dve.scalar_tensor_tensor(out=xt_lo[:, :, t * P:(t + 1) * P],
                                         in0=bank[3 + t % 2][:].rearrange("p (k n) -> p k n", k=KT), scalar=X_UP,
                                         in1=xt_hi[:, :, t * P:(t + 1) * P], op0=ALU.mult,
                                         op1=ALU.subtract).then_inc(xt_done, 1)

            power_of_two(pow_q, inv_q, 4, redq, invq_done)
            off = 0
            for i, n in enumerate(QUANT):
                w = QUANT_COLS[n]
                dve.tensor_scalar(scn[:, off:off + w], scn[:, off:off + w], inv_q[:, i:i + 1], None,
                                  ALU.mult).then_inc(scn_done, 1)
                off += w
            dve.wait_ge(d_x, 32)
            for t in range(NT):
                ln_stats(0, t)
            dve.wait_ge(d_const, 16 * N_CONST)
            dve.tensor_copy(ident_h[:], ident[:]).then_inc(chain, 1)
            dve.tensor_copy(ident_b[:], ident[:]).then_inc(chain, 1)
            dve.tensor_copy(mask_b[:], mask_f[:]).then_inc(chain, 1)
            for t in range(NT):
                ln_norm(0, t)
                if t:
                    ln_lo(0, t - 1)
            ln_lo(0, NT - 1)
            dve.tensor_tensor(c_score[:, 0:1], pow_q[:, 0:1], pow_q[:, 1:2], ALU.mult).then_inc(chain, 1)
            dve.tensor_tensor(c_out[:], pow_q[:, 2:3], pow_q[:, 3:4], ALU.mult).then_inc(chain, 1)
            dve.wait_ge(chain, 5)
            k_a = float(A_HD ** -0.5) / 16.0
            dve.tensor_scalar(c_score[:, 1:2], c_score[:, 0:1], -k_a, None, ALU.mult).then_inc(chain, 1)
            dve.tensor_scalar(c_out[:], c_out[:], 1.0 / (4.0 * W_UP), None, ALU.mult).then_inc(chain, 1)
            dve.wait_ge(chain, 7)
            dve.tensor_scalar(c_score[:, 0:1], c_score[:, 0:1], k_a, None, ALU.mult).then_inc(chain, 1)

            dve.wait_ge(d_raw, 16 * len(WEIGHTS))
            for i, n in enumerate(WEIGHTS):
                dve.tensor_reduce(amax_w[:, i:i + 1], raw[n], AX, ALU.max,
                                  apply_absolute_value=True).then_inc(amaxw_done, 1)
            power_of_two(pow_w, inv_w, len(WEIGHTS), redw, invw_done)
            for i, n in enumerate(WEIGHTS):
                dve.wait_ge(whi_done, i + 1)
                dve.scalar_tensor_tensor(out=w_lo[n][:], in0=raw[n], scalar=inv_w[:, i:i + 1], in1=w_hi[n][:],
                                         op0=ALU.mult, op1=ALU.subtract).then_inc(wlo_done, 1)
            p_a, p_b, p_q, p_kv, p_o, p_g = (pow_w[:, i:i + 1] for i in range(6))
            k_b = float(B_HD ** -0.5) / 1024.0
            dve.tensor_tensor(c_ffn[:], p_a, p_b, ALU.mult).then_inc(chain, 1)
            dve.tensor_tensor(c_score_b[:, 0:1], p_q, p_kv, ALU.mult).then_inc(chain, 1)
            dve.tensor_tensor(c_out_b[:], p_kv, p_o, ALU.mult).then_inc(chain, 1)
            dve.tensor_scalar(c_gate[:], p_g, 1.0 / (X_UP * W_UP), None, ALU.mult).then_inc(chain, 1)
            dve.wait_ge(chain, 12)
            dve.tensor_scalar(c_ffn[:], c_ffn[:], 1.0 / (32.0 * W_UP), None, ALU.mult).then_inc(chain, 1)
            dve.tensor_scalar(c_out_b[:], c_out_b[:], 1.0 / (32.0 * W_UP), None, ALU.mult).then_inc(chain, 1)
            dve.tensor_scalar(c_score_b[:, 1:2], c_score_b[:, 0:1], -k_b, None, ALU.mult).then_inc(chain, 1)
            dve.wait_ge(chain, 15)
            dve.tensor_scalar(c_score_b[:, 0:1], c_score_b[:, 0:1], k_b, None, ALU.mult).then_inc(chain, 1)
            dve.wait_ge(chain, 16)

            def rope(j, u, idx):
                dve.wait_ge(proj_ps, 12 * j + idx + 1)
                if u >= 2:
                    dve.wait_ge(rot_done, 10 * j + u - 1)
                h = P // 2
                ps = bank[PROJ_BANK[idx]]
                dve.tensor_tensor(rt2[0:h, u % 2], ps[h:P], sin_a[h:P], ALU.mult)
                dve.tensor_tensor(rt2[h:P, u % 2], ps[0:h], sin_a[0:h], ALU.mult)
                dve.tensor_tensor(rt1[:, u % 2], ps[:], cos_a[:], ALU.mult).then_inc(proj_read, 1)

            def v_low(j, b):
                dve.wait_ge(vhi_done, 2 * j + b + 1)
                dve.scalar_tensor_tensor(out=v_lo[:, b], in0=bank[PROJ_BANK[V_AT[b]]][:], scalar=PROJ_DN,
                                         in1=v_hi[:, b], op0=ALU.mult, op1=ALU.subtract).then_inc(proj_read, 1)

            def row_max(n, i2, ps, own, done, score):
                for bk, places in enumerate(((0, 1), (2,), (3,))):
                    dve.wait_ge(ps, 3 * n + bk + 1)
                    for c in places:
                        i = S_ORDER[c]
                        o = S_BANK[i][1]
                        dve.tensor_reduce(smax[:, i2, c:c + 1], bank[bk][:, o:o + (i + 1) * P], AX,
                                          ALU.max).then_inc(own, 1)
                    c0, c1 = places[0], places[-1] + 1
                    dve.wait_ge(own, 4 * n + c1)
                    dve.tensor_scalar(shift[:, i2, c0:c1], smax[:, i2, c0:c1], score[:, 1:2], None,
                                      ALU.mult).then_inc(done, 1)

            def pt_low(base, piece, hi_done, done, scale):
                w = S if piece < 2 else 2 * P
                c = slice(piece * S, piece * S + w)
                dve.wait_ge(hi_done, base + piece + 1)
                dve.scalar_tensor_tensor(out=pt_lo[:, c], in0=bank[PT_BANK[piece]][:, 0:w], scalar=scale,
                                         in1=pt_hi[:, c], op0=ALU.mult, op1=ALU.subtract).then_inc(done, 1)

            def normalise(j, s):
                n = 8 * j + s
                dve.wait_ge(exp_done, 4 * n + 4)
                dve.reciprocal(rden[:, s % 2], rsum[:, s % 2]).then_inc(rden_done, 1)
                dve.wait_ge(rden_done, n + 1)
                for i in range(ST):
                    w = (i + 1) * P
                    pr = prob[:, s % 2, S_OFF[i]:S_OFF[i] + w]
                    c = S_PLACE[i]
                    dve.tensor_scalar(pr, pr, rden[:, s % 2, c:c + 1], P_UP, ALU.mult, ALU.mult).then_inc(prob_done, 1)

            def ctx_low(j, s):
                dve.wait_ge(ctxhi_done, 8 * j + s + 1)
                dve.scalar_tensor_tensor(out=ctx_lo[:, s], in0=bank[5][:], scalar=1.0 / P_UP, in1=ctx_hi[:, s],
                                         op0=ALU.mult, op1=ALU.subtract).then_inc(ctx_done, 1)

            def o_add(j, t):
                dve.wait_ge(o_ps, NT * j + t + 1)
                dve.scalar_tensor_tensor(out=x[:, t], in0=bank[O_BANK[t]][:], scalar=c_out[:, 0:1], in1=x[:, t],
                                         op0=ALU.mult, op1=ALU.add).then_inc(o_added, 1)

            def read(j, idx):
                if PROJ[idx][0] == "v":
                    v_low(j, PROJ[idx][1])
                else:
                    rope(j, ROT_AT.index(idx), idx)

            with dve.Fori(0, KV_HEADS) as j:
                for idx in range(HEAD):
                    read(j, idx)
                for s in range(8):
                    row_max(8 * j + s, s % 2, s_ps, smax_done, shift_done, c_score)
                    if s:
                        for piece in range(3):
                            pt_low(24 * j + 3 * (s - 1), piece, pthi_done, pt_done, 1.0)
                    if s in MID:
                        read(j, MID[s])
                    if s in O_MID:
                        o_add(j, O_MID[s])
                    normalise(j, s)
                    if s:
                        ctx_low(j, s - 1)
                    if s in LATE:
                        read(j, LATE[s])
                    if s in O_LATE:
                        o_add(j, O_LATE[s])
                for piece in range(3):
                    pt_low(24 * j + 21, piece, pthi_done, pt_done, 1.0)
                o_add(j, 3)
                ctx_low(j, 7)
                for t in range(ST, NT):
                    o_add(j, t)

            def gate(ph, t):
                f = NT * ph + t
                i2 = t % 2
                g0 = 7 * f
                dve.wait_ge(g_ps, f + 1)
                dve.tensor_copy(lg[:, i2], bank[5][:, 0:EXPERTS]).then_inc(lg_done, 1)
                dve.wait_ge(lg_done, f + 1)
                dve.max(top[:, i2], lg[:, i2]).then_inc(gch, 1)
                dve.wait_ge(gch, g0 + 1)
                dve.tensor_scalar(dif[:, i2], top[:, i2, 0:2], top[:, i2, 0:1], c_gate[:, 0:1], ALU.subtract,
                                  ALU.mult).then_inc(dif_done, 1)
                dve.max_index(topi[:, i2], top[:, i2], lg[:, i2]).then_inc(gch, 1)
                dve.wait_ge(gch, g0 + 2)
                dve.tensor_copy(topf[:, i2], topi[:, i2]).then_inc(gch, 1)
                dve.wait_ge(ex_done, f + 1)
                dve.reciprocal(exr[:, i2], exs[:, i2]).then_inc(gch, 1)
                dve.wait_ge(gch, g0 + 4)
                dve.tensor_scalar(wgt[:, i2], ex[:, i2], exr[:, i2], None, ALU.mult).then_inc(gch, 1)
                dve.wait_ge(gch, g0 + 5)
                dve.tensor_scalar(oh0[:, i2], iota_e[:], topf[:, i2, 0:1], wgt[:, i2, 0:1], ALU.is_equal,
                                  ALU.mult).then_inc(gch, 1)
                dve.tensor_scalar(oh1[:, i2], iota_e[:], topf[:, i2, 1:2], wgt[:, i2, 1:2], ALU.is_equal,
                                  ALU.mult).then_inc(gch, 1)
                dve.wait_ge(gch, g0 + 7)
                dve.tensor_tensor(wfull[:, i2], oh0[:, i2], oh1[:, i2], ALU.add).then_inc(wfull_done, 1)
                dve.wait_ge(wfull_done, f + 1)
                dve.wait_ge(h_ps, f + 1)
                dve.tensor_tensor(hs[:, i2].rearrange("p (e r) -> p e r", e=EXPERTS),
                                  bank[t % 2][:].rearrange("p (e r) -> p e r", e=EXPERTS),
                                  wfull[:, i2].unsqueeze(2).broadcast_to([P, EXPERTS, RANK]), ALU.mult).then_inc(hs_done, 1)

            def m_low(m, scale):
                dve.wait_ge(mthi_done, m + 1)
                dve.scalar_tensor_tensor(out=mt_lo[:, m % 2], in0=bank[2][:], scalar=scale, in1=mt_hi[:, m % 2],
                                         op0=ALU.mult, op1=ALU.subtract).then_inc(mt_done, 1)

            def y_add(m, t, factor):
                dve.wait_ge(y_ps, m + 1)
                dve.scalar_tensor_tensor(out=x[:, t], in0=bank[6 + m % 2][:], scalar=factor[:, 0:1], in1=x[:, t],
                                         op0=ALU.mult, op1=ALU.add).then_inc(y_added, 1)
                dve.wait_ge(y_added, m + 1)

            def experts(ph, after):
                c = 1 + 2 * ph
                m0 = ph * 2 * NT
                ln_norm(c, 0)
                for t in range(NT):
                    ln_lo(c, t)
                    if t + 1 < NT:
                        ln_norm(c, t + 1)
                    gate(ph, t)
                    if t:
                        m_low(m0 + t - 1, PROJ_DN_B)
                        y_add(m0 + t - 1, t - 1, c_ffn)
                        if after is not None:
                            ln_stats(after, t - 1)
                m_low(m0 + NT - 1, PROJ_DN_B)
                y_add(m0 + NT - 1, NT - 1, c_ffn)
                if after is not None:
                    ln_stats(after, NT - 1)

            dve.wait_ge(o_added, NT * KV_HEADS)
            for t in range(NT):
                ln_stats(1, t)
            experts(0, 2)

            H2 = B_HD // 2
            ch = [0]

            def b_rope(src, n, t):
                heads = n // B_HD
                cs = cos_b[:, t % ST].unsqueeze(1)
                sn = sin_b[:, t % ST].unsqueeze(1)
                s4 = src.rearrange("p (h a d) -> p h a d", a=2, d=H2)
                o1 = r1[:, 0:n].rearrange("p (h d) -> p h d", d=H2)
                o2 = r2[:, 0:n].rearrange("p (h a d) -> p h a d", a=2, d=H2)
                dve.tensor_tensor(o1, src.rearrange("p (h d) -> p h d", d=H2),
                                  cs.broadcast_to([P, 2 * heads, H2]), ALU.mult).then_inc(bch, 1)
                dve.tensor_tensor(o2[:, :, 0], s4[:, :, 1], sn.broadcast_to([P, heads, H2]), ALU.mult).then_inc(bch, 1)
                dve.tensor_tensor(o2[:, :, 1], s4[:, :, 0], sn.broadcast_to([P, heads, H2]), ALU.mult).then_inc(bch, 1)
                ch[0] += 3
                dve.wait_ge(bch, ch[0])
                a1 = r1[:, 0:n].rearrange("p (h a d) -> p h a d", a=2, d=H2)
                rr = rot[:, 0:n].rearrange("p (h a d) -> p h a d", a=2, d=H2)
                dve.tensor_tensor(rr[:, :, 0], a1[:, :, 0], o2[:, :, 0], ALU.subtract).then_inc(bch, 1)
                last = dve.tensor_tensor(rr[:, :, 1], a1[:, :, 1], o2[:, :, 1], ALU.add)
                ch[0] += 1
                return last

            ln_norm(2, 0)
            for t in range(NT):
                ln_lo(2, t)
                if t + 1 < NT:
                    ln_norm(2, t + 1)
                qs = q_stack[:, t].rearrange("p (h a d) -> p h a d", h=B_HEADS, a=4)
                ks = k_stack[:, t].rearrange("p (h u a d) -> p h u a d", h=KV_HEADS, u=2, a=4)
                dve.wait_ge(bq_ps, t + 1)
                if t:
                    dve.wait_ge(bkvlo, 5 * t)
                b_rope(bank[t % 2][:], D, t).then_inc(bq_rot, 1)
                dve.wait_ge(bq_rot, t + 1)
                src = rot[:].rearrange("p (h d) -> p h d", d=B_HD)
                dve.wait_ge(bqhi, 2 * t + 2)
                for a in (1, 3):
                    last = dve.tensor_tensor(qs[:, :, a], src, qs[:, :, a - 1], ALU.subtract)
                    last.then_inc(bqlo, 1)
                dve.wait_ge(bqlo, 2 * t + 2)
                dve.wait_ge(bkv_ps, t + 1)
                b_rope(bank[5 + t % 2][:, 0:P], P, t).then_inc(bk_rot, 1)
                dve.wait_ge(bk_rot, t + 1)
                src = rot[:, 0:P].rearrange("p (h d) -> p h d", d=B_HD)
                dve.wait_ge(bkhi, 4 * t + 4)
                for u in range(2):
                    for a in (2, 3):
                        dve.tensor_tensor(ks[:, :, u, a], src, ks[:, :, u, a - 2], ALU.subtract).then_inc(bkvlo, 1)
                dve.wait_ge(bvhi, t + 1)
                dve.scalar_tensor_tensor(out=bv_lo[:, t], in0=bank[5 + t % 2][:, P:2 * P], scalar=PROJ_DN_B,
                                         in1=bv_hi[:, t], op0=ALU.mult, op1=ALU.subtract).then_inc(bkvlo, 1)

            def b_ctx(j, s):
                hh, b = s // B, s % B
                n = 8 * j + s
                dve.wait_ge(bctx_ps, n + 1)
                dve.wait_ge(brden, n + 1)
                dve.tensor_tensor(ctx_b[:, b * ST:(b + 1) * ST, bass.ds(j * (GROUP * B_HD) + hh * B_HD, B_HD)
                                        ].rearrange("p (u v) d -> p u v d", u=2),
                                  bank[5][:, 0:ST * B_HD].rearrange("p (u v d) -> p u v d", u=2, v=2),
                                  rden[:, s % 2].rearrange("p (v u) -> p u v", u=2).unsqueeze(3)
                                  .broadcast_to([P, 2, 2, B_HD]), ALU.mult).then_inc(bctx, 1)

            with dve.Fori(0, KV_HEADS) as j:
                for s in range(9):
                    if s < 8:
                        row_max(8 * j + s, s % 2, bs_ps, bsmax, bshift, c_score_b)
                    if s:
                        for piece in range(3):
                            pt_low(24 * j + 3 * (s - 1), piece, bpthi, bpt, P_UP)
                    if s < 8:
                        dve.wait_ge(bexp, 4 * (8 * j + s) + 4)
                        dve.reciprocal(rden[:, s % 2], rsum[:, s % 2]).then_inc(brden, 1)
                    if s:
                        b_ctx(j, s - 1)
            for t in range(NT):
                m_low(NT + t, 1.0 / P_UP)
                y_add(NT + t, t, c_out_b)
                ln_stats(3, t)
            experts(1, None)


def constants():
    pos = np.arange(S, dtype=np.float32)
    inv = (np.float32(1.0) / np.float32(10000.0) ** (np.arange(0, A_HD, 2, dtype=np.float32) / np.float32(A_HD)))
    f = pos[:, None] * inv.astype(np.float32)[None, :]
    cos, sin = np.cos(f).T.astype(np.float32), np.sin(f).T.astype(np.float32)
    cos_a = np.concatenate([cos, cos]) * np.float32(PROJ_DN)
    sin_a = np.concatenate([sin, -sin]) * np.float32(PROJ_DN)

    theta, factor, hi, lo, ctx_len = 500000.0, 32.0, 4.0, 1.0, 1024
    idx = np.arange(0, B_HD, 2, dtype=np.float32) / np.float32(B_HD)
    freq = np.float32(1.0 / (2.0 * np.pi)) * (np.float32(theta) ** (-idx)).astype(np.float32)
    scaled = np.where(freq < lo / ctx_len, freq / np.float32(factor), freq)
    smooth = np.clip((ctx_len * freq - np.float32(lo)) / np.float32(hi - lo), 0.0, 1.0).astype(np.float32)
    mid = (1 - smooth) * (freq / np.float32(factor)) + smooth * freq
    freq = np.where((freq >= lo / ctx_len) & (freq <= hi / ctx_len), mid, scaled).astype(np.float32)
    phase = (np.float32(2.0 * np.pi) * pos)[:, None] * freq[None, :]
    table = lambda a: np.ascontiguousarray(
        (a.astype(np.float32) * np.float32(PROJ_DN_B)).reshape(ST, P, B_HD // 2).transpose(1, 0, 2))
    i = np.arange(P)
    mask = np.where(i[None, :] <= i[:, None], 0.0, MASKED).astype(np.float32)
    return {"ident": np.eye(P, dtype=np.float32), "mask": mask, "cos_a": cos_a.astype(np.float32),
            "sin_a": sin_a.astype(np.float32), "cos_b": table(np.cos(phase)), "sin_b": table(np.sin(phase))}


def kernel(**inputs):
    import concourse.bacc as bacc
    from concourse.bass_utils import run_bass_kernel_spmd

    a = {n: np.asarray(v) for n, v in inputs.items()}
    pre = "L0_attn_a_"
    tiles = lambda w: w.reshape(KT, P, -1).transpose(1, 0, 2).reshape(P, -1)

    def even_odd(w, heads):
        return w.reshape(-1, heads, A_HD // 2, 2).swapaxes(2, 3).reshape(w.shape)

    def by_group(w):
        return w.reshape(KT, P, KV_HEADS, -1).transpose(2, 1, 0, 3)

    def scales_by_group(w):
        return w.reshape(KT, KV_HEADS, -1).transpose(1, 0, 2).reshape(-1)

    q, k = even_odd(a[pre + "q_codes"], A_HEADS), even_odd(a[pre + "k_codes"], KV_HEADS)
    qs, ks = even_odd(a[pre + "q_scales"], A_HEADS), even_odd(a[pre + "k_scales"], KV_HEADS)
    lora_a, lora_b = a["L0_ffn_lora_A"], a["L0_ffn_lora_B"]
    arrays = {
        "x": a[pre + "hidden_states"],
        "q_codes": by_group(q), "k_codes": by_group(k), "v_codes": by_group(a[pre + "v_codes"]),
        "o_codes": a[pre + "o_codes"].reshape(KV_HEADS, GROUP, P, D).transpose(0, 2, 1, 3),
        "q_scales": scales_by_group(qs), "k_scales": scales_by_group(ks),
        "v_scales": scales_by_group(a[pre + "v_scales"]), "o_scales": a[pre + "o_scales"].reshape(-1),
        "lora_a": tiles(lora_a.reshape(EXPERTS * RANK, D).T),
        "lora_b": tiles(lora_b.transpose(0, 2, 1).reshape(EXPERTS * RANK, D)),
        "b_q": tiles(a["L0_attn_b_Wq"]), "b_o": tiles(a["L0_attn_b_Wo"]),
        "b_kv": tiles(np.concatenate([a["L0_attn_b_Wk"], a["L0_attn_b_Wv"]], axis=1)),
        "gate": tiles(a["L0_ffn_gate_w"].T),
        **constants(),
    }
    nc = bacc.Bacc("TRN2", target_bir_lowering=False, num_devices=1)
    arrays = {f"in_{n}": np.ascontiguousarray(v) for n, v in arrays.items()}
    t_in = {n[3:]: nc.dram_tensor(n, v.shape, mybir.dt.from_np(v.dtype), kind="ExternalInput").ap()
            for n, v in arrays.items()}
    out = nc.dram_tensor("out", (B, S, D), F32, kind="ExternalOutput").ap()
    build(nc, t_in, out)
    r = run_bass_kernel_spmd(nc, [arrays], core_ids=[0])
    return r.results[0]["out"]
```

```python
from contextlib import ExitStack

import numpy as np

import concourse.bass as bass
from concourse import mybir

F32 = mybir.dt.float32
F16 = mybir.dt.float16
BF16 = mybir.dt.bfloat16
I32 = mybir.dt.int32
U32 = mybir.dt.uint32
ALU = mybir.AluOpType
ACT = mybir.ActivationFunctionType
AX = mybir.AxisListType.X

P = 128
B, S, D = 2, 512, 512
TOK = B * S
NT = TOK // P
ST = S // P
KT = D // P
EPS = 1e-5

A_HEADS, KV_HEADS, A_HD = 32, 8, 128
GROUP = A_HEADS // KV_HEADS
B_HEADS, B_HD = 32, 16
B_ST = 4 * B_HD
B_VD = B_HD + 1
EXPERTS, RANK, TOP_K = 8, 64, 2

X_UP = 2.0 ** 10
W_UP = 2.0 ** 10
PROJ_DN = 2.0 ** -18
PROJ_DN_B = 2.0 ** -15
P_UP = 2.0 ** 15
MASKED = -1e30

S_OFF = [0, P, 3 * P, 6 * P]
TRI = 10 * P
S_BANK = [(0, 0), (1, 0), (0, P), (2, 0)]
S_ORDER = (0, 2, 1, 3)
S_PLACE = {0: 0, 2: 1, 1: 2, 3: 3}
BANK_PLACES = ((0, 2), (2, 3), (3, 4))
PT_BANK = [3, 4, 7]
O_BANK = [7, 6, 6, 0, 1, 2, 6, 0]
PROJ = [("k", 0), ("q", 0), ("q", 1), ("v", 0), ("q", 2), ("q", 3), ("k", 1), ("q", 4), ("v", 1), ("q", 5), ("q", 6),
        ("q", 7)]
PROJ_BANK = [3, 4, 6, 7, 5, 6, 6, 6, 7, 6, 6, 6]
V_AT = [PROJ.index(("v", b)) for b in range(B)]
ROT_AT = [i for i, (n, _) in enumerate(PROJ) if n != "v"]
HEAD = 5
MID = {0: 5, 1: 6, 2: 7, 3: 9, 4: 10, 5: 11}
LATE = {2: 8}
O_MID = {6: 1, 7: 2}
O_LATE = {5: 0}
T_OFF = {0: 0, 1: S, 3: S + 3 * P, 2: 2 * S}

LN_BANK = [(0, 1), (3, 4), (3, 4), (3, 4)]
HALF = NT // 2
GATE_BANK = [5, 7]
MT_BANK = [2, 0]
CTX_BANK = 5
B_PT_BANK = [[3, 4, 7], [3, 6, 7]]

LOTS = (("lora_a", "gate", "lora_b"), ("b_q", "b_kv", "b_o"))
WEIGHTS = LOTS[0] + LOTS[1]
W_COLS = {"lora_a": KT * EXPERTS * RANK, "lora_b": KT * D, "b_q": KT * D, "b_kv": KT * 2 * KV_HEADS * B_HD,
          "b_o": KT * D, "gate": KT * EXPERTS}
QUANT = ("q", "k", "v", "o")
QUANT_COLS = {"q": P, "k": P // 4, "v": P // 4, "o": P}


def t_bank(unit):
    return (2, 7)[unit % 2]


def build(nc, t_in, out):
    ctx = ExitStack()
    with ctx:
        def sb(name, shape, dt):
            return ctx.enter_context(nc.sbuf_tensor(name, shape, dt))

        def sem(name):
            return ctx.enter_context(nc.semaphore(name))

        bank = [ctx.enter_context(nc.psum_tensor(f"bank{i}", [P, 512], F32)) for i in range(8)]

        x = sb("x", [P, NT, D], F32)
        xt_hi = sb("xt_hi", [P, KT, TOK], F16)
        xt_lo = sb("xt_lo", [P, KT, TOK], F16)
        xn = sb("xn", [P, 2, D], F32)
        ident = sb("ident", [P, P], F32)
        ident_h = sb("ident_h", [P, P], F16)
        ident_b = sb("ident_b", [P, P], BF16)
        mask_f = sb("mask_f", [P, P], F32)
        mask_b = sb("mask_b", [P, P], BF16)
        cos_b = sb("cos_b", [P, ST, B_HD // 2], F32)
        sin_b = sb("sin_b", [P, ST, 2, B_HD // 2], F32)
        iota_e = sb("iota_e", [P, EXPERTS], F32)
        minus_half = sb("minus_half", [P, 1], F32)
        one = sb("one", [P, 1], F32)
        bn = sb("bn", [P, NT, 6], F32)
        mv = sb("mv", [P, NT, 2], F32)
        rstd = sb("rstd", [P, NT], F32)
        w_hi = {n: sb(f"{n}_hi", [P, W_COLS[n]], F16) for n in WEIGHTS}
        w_lo = {n: sb(f"{n}_lo", [P, W_COLS[n]], F16) for n in WEIGHTS}
        amax_w = sb("amax_w", [P, 8], F32)
        pow_w = sb("pow_w", [P, 8], F32)
        inv_w = sb("inv_w", [P, 8], F32)
        amax_q = sb("amax_q", [P, 4], F32)
        pow_q = sb("pow_q", [P, 4], F32)
        inv_q = sb("inv_q", [P, 4], F32)
        c_score = sb("c_score", [P, 2], F32)
        c_out = sb("c_out", [P, 1], F32)
        c_score_b = sb("c_score_b", [P, 2], F32)
        c_out_b = sb("c_out_b", [P, 1], F32)
        c_ffn = sb("c_ffn", [P, 1], F32)
        c_gate = sb("c_gate", [P, 1], F32)
        smax = sb("smax", [P, 2, ST], F32)
        shift = sb("shift", [P, 2, ST], F32)
        rsum = sb("rsum", [P, 2, ST], F32)
        rden = sb("rden", [P, 2, ST], F32)
        prob = sb("prob", [P, 2, TRI], F32)

        a_ctx = ExitStack()

        def sa(name, shape, dt):
            return a_ctx.enter_context(nc.sbuf_tensor(name, shape, dt))

        ocode = sa("ocode", [P, GROUP, D], I32)
        ocode_f = ocode[:].bitcast(F32)
        oscale = sa("oscale", [P, GROUP, D], F32)
        kvcode = sa("kvcode", [P, 2, KT, P], I32)
        kvcode_f = kvcode[:].bitcast(F32)
        kvscale = sa("kvscale", [P, 2, KT, P], F32)
        qcode = sa("qcode", [P, KT, 512], I32)
        qcode_f = qcode[:].bitcast(F32)
        qscale = sa("qscale", [P, KT, 512], F32)
        pt_hi = sa("pt_hi", [P, TRI], F16)
        pt_lo = sa("pt_lo", [P, TRI], F16)
        cos_a = sa("cos_a", [P, S], F32)
        sin_a = sa("sin_a", [P, S], F32)
        scn = sa("scn", [P, sum(QUANT_COLS.values())], F32)
        wq_hi = sa("wq_hi", [P, KT, 512], F16)
        wq_lo = sa("wq_lo", [P, KT, 512], F16)
        wkv_hi = sa("wkv_hi", [P, 2, KT, P], F16)
        wkv_lo = sa("wkv_lo", [P, 2, KT, P], F16)
        wo_hi = sa("wo_hi", [P, GROUP, D], F16)
        wo_lo = sa("wo_lo", [P, GROUP, D], F16)
        rt1 = sa("rt1", [P, 2, S], F32)
        rt2 = sa("rt2", [P, 2, S], F32)
        arena = sa("arena", [P, 10 * 1024], F32)
        q_hi = arena[:, 0:2048].bitcast(F16).rearrange("p (s n) -> p s n", s=8)
        q_lo = arena[:, 2048:4096].bitcast(F16).rearrange("p (s n) -> p s n", s=8)
        ctx_hi = arena[:, 4096:6144].bitcast(F16).rearrange("p (s n) -> p s n", s=8)
        ctx_lo = arena[:, 6144:8192].bitcast(F16).rearrange("p (s n) -> p s n", s=8)
        k_hi = arena[:, 8192:8704].bitcast(F16).rearrange("p (s n) -> p s n", s=B)
        k_lo = arena[:, 8704:9216].bitcast(F16).rearrange("p (s n) -> p s n", s=B)
        v_hi = arena[:, 9216:9728].bitcast(F16).rearrange("p (s n) -> p s n", s=B)
        v_lo = arena[:, 9728:10240].bitcast(F16).rearrange("p (s n) -> p s n", s=B)
        raw = {"lora_a": qcode_f.rearrange("p g n -> p (g n)"), "lora_b": qscale[:].rearrange("p g n -> p (g n)"),
               "gate": kvscale[:].rearrange("p i g n -> p (i g n)")[:, 0:W_COLS["gate"]],
               "b_kv": kvcode_f.rearrange("p i g n -> p (i g n)"), "b_q": ocode_f.rearrange("p g n -> p (g n)"),
               "b_o": oscale[:].rearrange("p g n -> p (g n)")}
        for n in WEIGHTS:
            assert raw[n].shape[1] == W_COLS[n]
        a_ctx.close()

        qt_b = sb("qt_b", [P, B_HEADS // 2, TOK], F16)
        kt_b = sb("kt_b", [P, KV_HEADS, 2, TOK], F16)
        bv_hi = sb("bv_hi", [P, NT, KV_HEADS * B_VD], F16)
        bv_lo = sb("bv_lo", [P, NT, KV_HEADS * B_VD], F16)
        ctx_b = sb("ctx_b", [P, NT, D], F32)
        hs = sb("hs", [P, 2, D], F32)
        mt_hi = sb("mt_hi", [P, 2, D], F16)
        mt_lo = sb("mt_lo", [P, 2, D], F16)
        lg = sb("lg", [P, NT, EXPERTS], F32)
        top = sb("top", [P, NT, 8], F32)
        topi = sb("topi", [P, NT, 8], U32)
        topf = sb("topf", [P, NT, TOP_K], F32)
        dif = sb("dif", [P, NT, TOP_K], F32)
        ex = sb("ex", [P, NT, TOP_K], F32)
        exs = sb("exs", [P, NT, 1], F32)
        exr = sb("exr", [P, NT, 1], F32)
        wgt = sb("wgt", [P, NT, TOP_K], F32)
        chosen = sb("chosen", [P, NT, TOP_K, EXPERTS], F32)
        wfull = sb("wfull", [P, NT, EXPERTS], F32)
        hidden_ = ExitStack()
        hidden = hidden_.enter_context(nc.sbuf_tensor("hidden", [P, NT, EXPERTS * RANK], F32))
        hidden_.close()

        stage = ExitStack()

        def staged(name, shape, dt):
            return stage.enter_context(nc.sbuf_tensor(name, shape, dt))

        rq1 = staged("rq1", [P, 2, D], F32)
        rq2 = staged("rq2", [P, 2, D], F32)
        rk1 = staged("rk1", [P, 2, P], F32)
        rk2 = staged("rk2", [P, 2, P], F32)
        q_stack = staged("q_stack", [P, 2, B_HEADS * B_ST], F16)
        k_stack = staged("k_stack", [P, 2, KV_HEADS * B_ST], F16)
        stage.close()
        ptb_hi = sb("ptb_hi", [P, 2, TRI], F16)
        ptb_lo = sb("ptb_lo", [P, 2, TRI], F16)
        ptb_32 = sb("ptb_32", [P, 2, TRI - 2 * S], F32)

        def heads_v(v, t):
            return v[:, t].rearrange("p (h d) -> p h d", d=B_VD)[:, :, 0:B_HD]

        scr = {n: nc.dram_tensor(f"scales_{n}", (P * QUANT_COLS[n],), F32).ap() for n in QUANT}

        d_const, d_scale, d_scr, d_out = (sem(n) for n in ("d_const", "d_scale", "d_scr", "d_out"))
        d_x = [sem(f"d_x{b}") for b in range(B)]
        d_raw, amaxw_done, redw, invw_done = ([sem(f"{n}{i}") for i in range(2)] for n in (
            "d_raw", "amaxw_done", "redw", "invw_done"))
        w_scaled, whi_done, wlo_done = (sem(n) for n in ("w_scaled", "whi_done", "wlo_done"))
        consts, chain, amaxq_done, redq, invq_done, scn_done = (
            sem(n) for n in ("consts", "chain", "amaxq_done", "redq", "invq_done", "scn_done"))
        ln_stat, ln_rstd, xn_ready, xt_ps, xthi_done, xt_done = (sem(n) for n in (
            "ln_stat", "ln_rstd", "xn_ready", "xt_ps", "xthi_done", "xt_done"))
        d_code = {n: sem(f"d_code_{n}") for n in ("q", "kv", "o")}
        d_wscale = {n: sem(f"d_wscale_{n}") for n in ("q", "kv", "o")}
        wfull_done, w_first = sem("wfull_done"), sem("w_first")
        whi, w32_done, q_code, kv_code, o_code = (sem(n) for n in ("whi", "w32_done", "q_code", "kv_code", "o_code"))
        q_w, kv_w, o_w = sem("q_w"), sem("kv_w"), sem("o_w")
        proj_ps, proj_read, rot_ready, rothi_done, rot_done, vhi_done = (sem(n) for n in (
            "proj_ps", "proj_read", "rot_ready", "rothi_done", "rot_done", "vhi_done"))
        s_ps, smax_done, shift_done, exp_done, rden_done, prob_done, prob_last = (sem(n) for n in (
            "s_ps", "smax_done", "shift_done", "exp_done", "rden_done", "prob_done", "prob_last"))
        pt_ps, pthi_done, pt_done, ctx_ps, ctxhi_done, ctx_done, o_ps, o_added = (sem(n) for n in (
            "pt_ps", "pthi_done", "pt_done", "ctx_ps", "ctxhi_done", "ctx_done", "o_ps", "o_added"))
        g_ps, dif_done, ex_done, gate_step, h_ps, h_done, hs_done, mt_ps, mthi_done, mt_done, y_ps, y_added = (
            sem(n) for n in ("g_ps", "dif_done", "ex_done", "gate_step", "h_ps", "h_done", "hs_done",
                             "mt_ps", "mthi_done", "mt_done", "y_ps", "y_added"))
        bq_ps, bkv_ps, bq_mul, bk_mul, bq_rot, bk_rot, bq_hi, bk_hi, bv_hi_done, bq_lo, bk_lo, bv_lo_done = (
            sem(n) for n in ("bq_ps", "bkv_ps", "bq_mul", "bk_mul", "bq_rot", "bk_rot", "bq_hi", "bk_hi",
                             "bv_hi_done", "bq_lo", "bk_lo", "bv_lo_done"))
        zeros_done, bt_ps, bt_act, bt_dve = (sem(n) for n in ("zeros_done", "bt_ps", "bt_act", "bt_dve"))
        bs_ps, bsmax, bshift, bexp, brden, bpt_ps, bpthi, bpt, bpthi_last, bpt_last, bctx_ps, bctx = (sem(n) for n in (
            "bs_ps", "bsmax", "bshift", "bexp", "brden", "bpt_ps", "bpthi", "bpt",
            "bpthi_last", "bpt_last", "bctx_ps", "bctx"))

        def load_codes(eng, n, j):
            if n == "kv":
                for i, m in enumerate(n):
                    eng.dma_start(kvcode[:, i], t_in[f"{m}_codes"][bass.ds(j, 1)].rearrange("o p g n -> (o p) g n")
                                  ).then_inc(d_code[n], 16)
            else:
                eng.dma_start({"q": qcode, "o": ocode}[n][:],
                              t_in[f"{n}_codes"][bass.ds(j, 1)].rearrange("o p g n -> (o p) g n")
                              ).then_inc(d_code[n], 16)

        def load_scales(eng, n, j):
            if n == "kv":
                for i, m in enumerate(n):
                    eng.dma_start(kvscale[:, i].rearrange("p g n -> p (g n)"),
                                  scr[m][bass.ds(j * 512, 512)].partition_broadcast(P)).then_inc(d_wscale[n], 16)
            else:
                eng.dma_start({"q": qscale, "o": oscale}[n][:].rearrange("p g n -> p (g n)"),
                              scr[n][bass.ds(j * 2048, 2048)].partition_broadcast(P)).then_inc(d_wscale[n], 16)

        block = ctx.enter_context(nc.Block())
        N_CONST = 6

        @block.sync
        def _(sp):
            x_in = t_in["x"].rearrange("b s d -> (b s) d").rearrange("(t p) d -> p t d", p=P)
            off = 0
            for n in QUANT:
                w = QUANT_COLS[n]
                sp.dma_start(scn[:, off:off + w], t_in[f"{n}_scales"].rearrange("(p f) -> p f", p=P)
                             ).then_inc(d_scale, 16)
                off += w
            sp.dma_start(x[:, 0:ST, :], x_in[:, 0:ST, :]).then_inc(d_x[0], 16)
            for dst, src in ((ident, "ident"), (mask_f, "mask"), (cos_a, "cos_a"), (sin_a, "sin_a"),
                             (cos_b, "cos_b"), (sin_b, "sin_b")):
                sp.dma_start(dst[:], t_in[src]).then_inc(d_const, 16)

            off = 0
            sp.wait_ge(scn_done, 4)
            for n in QUANT:
                w = QUANT_COLS[n]
                sp.dma_start(scr[n].rearrange("(p f) -> p f", p=P), scn[:, off:off + w]).then_inc(d_scr, 16)
                off += w
            sp.wait_ge(d_scr, 64)
            load_scales(sp, "kv", 0)
            sp.dma_start(x[:, ST:NT, :], x_in[:, ST:NT, :]).then_inc(d_x[1], 16)
            for n in "qo":
                load_scales(sp, n, 0)
            load_codes(sp, "o", 0)
            with sp.Fori(0, KV_HEADS - 1) as j:
                for n, pieces in (("kv", 2), ("q", 4), ("o", 4)):
                    sp.wait_ge({"kv": kv_w, "q": q_w, "o": o_w}[n], pieces * j + pieces)
                    load_codes(sp, n, j + 1)
                    load_scales(sp, n, j + 1)
            sp.wait_ge(kv_w, 2 * KV_HEADS)
            sp.wait_ge(q_w, 4 * KV_HEADS)
            for n in LOTS[0]:
                sp.dma_start(raw[n], t_in[n]).then_inc(d_raw[0], 16)
            sp.wait_ge(o_w, 4 * KV_HEADS)
            for n in LOTS[1]:
                sp.dma_start(raw[n], t_in[n]).then_inc(d_raw[1], 16)
            o_out = out.rearrange("b s d -> (b s) d").rearrange("(t p) d -> p t d", p=P)
            for t in range(NT):
                sp.wait_ge(y_added, NT + B * ST + t + 1)
                sp.dma_start(o_out[:, t, :], x[:, t, :]).then_inc(d_out, 16)
            sp.wait_ge(d_out, 16 * NT)

        @block.gpsimd
        def _(pool):
            pool.memset(minus_half[:], -0.5).then_inc(consts, 1)
            pool.memset(one[:], 1.0).then_inc(consts, 1)
            pool.iota(iota_e[:], pattern=[[1, EXPERTS]], base=0, channel_multiplier=0,
                      allow_small_or_imprecise_dtypes=True).then_inc(consts, 1)
            pool.wait_ge(consts, 3)

            def ln_rsqrt(c, t):
                pool.wait_ge(ln_stat, 3 * (NT * c + t) + 3)
                pool.tensor_tensor(rstd[:, t:t + 1], mv[:, t, 1:2], minus_half[:], ALU.pow).then_inc(ln_rstd, 1)

            pool.wait_ge(amaxq_done, 4)
            pool.partition_all_reduce(pow_q[:], amax_q[:], P, bass.bass_isa.ReduceOp.max).then_inc(redq, 1)
            for t in range(ST):
                ln_rsqrt(0, t)

            def dequant(n, code, scale, hi, lo):
                pool.tensor_tensor(hi, code, scale, ALU.mult).then_inc(whi, 1)
                pool.tensor_tensor(code, code, scale, ALU.mult).then_inc(w32_done, 1)
                pool.wait_ge(whi, n + 1)
                pool.wait_ge(w32_done, n + 1)
                return pool.tensor_tensor(lo, code, hi, ALU.subtract)

            def deq_kv(j, i, n):
                pool.wait_ge(kv_code, j + 1)
                pool.wait_ge(d_wscale["kv"], 32 * j + 32)
                flat = lambda a: a[:, i].rearrange("p g n -> p (g n)")
                dequant(n, flat(kvcode_f), flat(kvscale), flat(wkv_hi), flat(wkv_lo)).then_inc(kv_w, 1)

            def deq_q(j, g, n):
                pool.wait_ge(q_code, j + 1)
                pool.wait_ge(d_wscale["q"], 16 * j + 16)
                dequant(n, qcode_f[:, g], qscale[:, g], wq_hi[:, g], wq_lo[:, g]).then_inc(q_w, 1)

            def deq_o(j, g, n):
                pool.wait_ge(o_code, j + 1)
                pool.wait_ge(d_wscale["o"], 16 * j + 16)
                dequant(n, ocode_f[:, g], oscale[:, g], wo_hi[:, g], wo_lo[:, g]).then_inc(o_w, 1)

            def rope_add(j, u, idx):
                pool.wait_ge(proj_read, 12 * j + idx + 1)
                pool.tensor_tensor(rt1[:, u % 2], rt1[:, u % 2], rt2[:, u % 2], ALU.add).then_inc(rot_ready, 1)

            def rope_lo(j, u, dst, src):
                pool.wait_ge(rothi_done, 10 * j + u + 1)
                pool.tensor_tensor(dst, rt1[:, u % 2], src, ALU.subtract).then_inc(rot_done, 1)

            rot_dst = [(k_lo[:, i], k_hi[:, i]) if n == "k" else (q_lo[:, i], q_hi[:, i])
                       for n, i in PROJ if n != "v"]

            def group(j, last):
                n0 = 10 * j + FIRST
                o_piece = {3: 0, 4: 1, 6: 2, 7: 3}
                for u in range(10):
                    rope_add(j, u, ROT_AT[u])
                    if u in o_piece:
                        deq_o(j, o_piece[u], n0 + o_piece[u])
                    rope_lo(j, u, *rot_dst[u])
                    if u >= 8 and not last:
                        deq_kv(j + 1, u - 8, n0 + u - 4)
                if not last:
                    for g in range(KT):
                        deq_q(j + 1, g, n0 + 6 + g)

            FIRST = 4
            deq_kv(0, 0, 0)
            ln_rsqrt(0, ST)
            ln_rsqrt(0, ST + 1)
            deq_q(0, 0, 1)
            ln_rsqrt(0, ST + 2)
            ln_rsqrt(0, ST + 3)
            deq_q(0, 1, 2)
            deq_kv(0, 1, 3)
            with pool.Fori(0, KV_HEADS - 1) as j:
                group(j, False)
            group(KV_HEADS - 1, True)

            def largest(lot):
                c = slice(lot * 3, lot * 3 + 3)
                pool.wait_ge(amaxw_done[lot], 3)
                pool.partition_all_reduce(pow_w[:, c], amax_w[:, c], P, bass.bass_isa.ReduceOp.max
                                          ).then_inc(redw[lot], 1)

            def w_low(n, part, parts):
                pool.wait_ge(whi_done, WEIGHTS.index(n) + 1)
                w = W_COLS[n] // parts
                c = slice(part * w, (part + 1) * w)
                pool.tensor_tensor(w_lo[n][:, c], raw[n][:, c], w_hi[n][:, c], ALU.subtract).then_inc(wlo_done, 1)

            largest(0)
            for t in range(ST):
                ln_rsqrt(1, t)
            w_low("lora_a", 0, 1)
            w_low("gate", 0, 1)

            between = {2 + i: ("b_q", i, 4) for i in range(4)}
            between.update({6 + i: ("b_kv", i, 2) for i in range(2)})

            def weighted(ph):
                for t in range(NT):
                    if t % HALF == 0:
                        pool.wait_ge(wfull_done, 2 * ph + t // HALF + 1)
                    pool.wait_ge(h_done, NT * ph + t + 1)
                    if t >= 2:
                        pool.wait_ge(mt_ps, 2 * NT * ph + t - 1)
                    pool.tensor_tensor(hs[:, t % 2].rearrange("p (e r) -> p e r", e=EXPERTS),
                                       hidden[:, t].rearrange("p (e r) -> p e r", e=EXPERTS),
                                       wfull[:, t].unsqueeze(2).broadcast_to([P, EXPERTS, RANK]),
                                       ALU.mult).then_inc(hs_done, 1)
                    if ph == 0 and t in between:
                        w_low(*between[t])

            for t in range(ST, NT):
                ln_rsqrt(1, t)
            w_low("lora_b", 0, 1)
            largest(1)
            pool.wait_ge(wlo_done, 3)
            pool.memset(kt_b[:].rearrange("p h f n -> p (h f n)").bitcast(F32), 0.0).then_inc(zeros_done, 1)
            for v, value in ((bv_hi, 1.0), (bv_lo, 0.0)):
                pool.memset(v[:].rearrange("p t (h d) -> p t h d", d=B_VD)[:, :, :, B_HD:B_VD], value
                            ).then_inc(zeros_done, 1)
            weighted(0)
            w_low("b_o", 0, 1)
            for t in range(NT):
                ln_rsqrt(2, t)

            for t in range(NT):
                i2 = t % 2
                pool.wait_ge(bq_mul, t + 1)
                pool.tensor_tensor(rq1[:, i2], rq1[:, i2], rq2[:, i2], ALU.add).then_inc(bq_rot, 1)
                pool.wait_ge(bk_mul, t + 1)
                pool.tensor_tensor(rk1[:, i2], rk1[:, i2], rk2[:, i2], ALU.add).then_inc(bk_rot, 1)
                if t < NT - 1:
                    pool.wait_ge(bq_hi, t + 1)
                    st = q_stack[:, i2].rearrange("p (h e a d) -> p h e a d", h=B_HEADS, e=2, a=2)
                    rq = rq1[:, i2].rearrange("p (h d) -> p h d", d=B_HD).unsqueeze(2)
                    pool.tensor_tensor(st[:, :, :, 1], rq.broadcast_to([P, B_HEADS, 2, B_HD]), st[:, :, :, 0],
                                       ALU.subtract).then_inc(bq_lo, 1)

            def b_last_piece(n, i2):
                piece = slice(2 * S, TRI)
                pool.wait_ge(bpt, 3 * n + 1)
                pool.tensor_tensor(ptb_hi[:, i2, piece], ptb_32[:, i2],
                                   one[:].broadcast_to([P, TRI - 2 * S]), ALU.mult).then_inc(bpthi_last, 1)
                pool.wait_ge(bpthi_last, n + 1)
                pool.tensor_tensor(ptb_lo[:, i2, piece], ptb_32[:, i2], ptb_hi[:, i2, piece], ALU.subtract
                                   ).then_inc(bpt_last, 1)

            def b_group(j, first):
                for s in range(8):
                    n = 8 * j + s
                    for c0, c1 in BANK_PLACES:
                        pool.wait_ge(bsmax, 4 * n + c1)
                        pool.tensor_tensor(shift[:, s % 2, c0:c1], smax[:, s % 2, c0:c1],
                                           c_score_b[:, 1:2].broadcast_to([P, c1 - c0]), ALU.mult).then_inc(bshift, 1)
                    if not (first and s == 0):
                        b_last_piece(n - 1, (s - 1) % 2)

            b_group(0, True)
            with pool.Fori(1, KV_HEADS) as j:
                b_group(j, False)
            b_last_piece(8 * KV_HEADS - 1, 1)
            for t in range(NT):
                ln_rsqrt(3, t)
            weighted(1)

        @block.scalar
        def _(act):
            def ln_hi(c, t):
                act.wait_ge(xt_ps, NT * c + t + 1)
                act.activation(xt_hi[:, :, t * P:(t + 1) * P],
                               bank[LN_BANK[c][t % 2]][:].rearrange("p (k n) -> p k n", k=KT),
                               ACT.Copy, scale=X_UP).then_inc(xthi_done, 1)

            def codes(j, code, code_f, loaded, count, done):
                act.wait_ge(loaded, count)
                act.activation(code_f[:].rearrange("p a b -> p (a b)") if len(code_f.shape) == 3 else
                               code_f[:].rearrange("p i a b -> p (i a b)"),
                               code[:].rearrange("p a b -> p (a b)") if len(code.shape) == 3 else
                               code[:].rearrange("p i a b -> p (i a b)"), ACT.Copy, bias=-8.0).then_inc(done, 1)

            load_codes(act, "kv", 0)
            act.wait_ge(scn_done, 4)
            load_codes(act, "q", 0)
            codes(0, kvcode, kvcode_f, d_code["kv"], 32, kv_code)
            ln_hi(0, 0)
            codes(0, qcode, qcode_f, d_code["q"], 16, q_code)
            for t in range(1, NT):
                ln_hi(0, t)
            codes(0, ocode, ocode_f, d_code["o"], 16, o_code)

            rot_hi = [k_hi[:, i] if n == "k" else q_hi[:, i] for n, i in PROJ if n != "v"]

            def rope_hi(j, u):
                act.wait_ge(rot_ready, 10 * j + u + 1)
                act.activation(rot_hi[u], rt1[:, u % 2], ACT.Copy).then_inc(rothi_done, 1)

            def v_high(j, b):
                act.wait_ge(proj_ps, 12 * j + V_AT[b] + 1)
                act.activation(v_hi[:, b], bank[PROJ_BANK[V_AT[b]]][:], ACT.Copy, scale=PROJ_DN).then_inc(vhi_done, 1)

            def exps(n, i2, score, ready, done, sums=None):
                for i in S_ORDER:
                    bk, o = S_BANK[i]
                    w = (i + 1) * P
                    c = S_PLACE[i]
                    if i != 2:
                        act.wait_ge(ready, 3 * n + bk + 1)
                    act.activation(prob[:, i2, S_OFF[i]:S_OFF[i] + w], bank[bk][:, o:o + w], ACT.Exp,
                                   bias=shift[:, i2, c:c + 1], scale=score[:, 0:1],
                                   accum_out=None if sums is None else sums[:, i2, c:c + 1]).then_inc(done, 1)

            def pt_high(base, piece, ps, done, scale, pt, banks=PT_BANK):
                w = S if piece < 2 else 2 * P
                act.wait_ge(ps, base + piece + 1)
                act.activation(pt[:, piece * S:piece * S + w], bank[banks[piece]][:, 0:w], ACT.Copy,
                               scale=scale).then_inc(done, 1)

            def normalise_last(j, s):
                act.wait_ge(rden_done, 8 * j + s + 1)
                pr = prob[:, s % 2, S_OFF[ST - 1]:TRI]
                c = S_PLACE[ST - 1]
                act.activation(pr, pr, ACT.Copy, scale=rden[:, s % 2, c:c + 1]).then_inc(prob_last, 1)

            def ctx_high(j, s):
                act.wait_ge(ctx_ps, 8 * j + s + 1)
                act.activation(ctx_hi[:, s], bank[5][:], ACT.Copy, scale=1.0 / P_UP).then_inc(ctxhi_done, 1)

            def evict(j, idx):
                if PROJ[idx][0] == "v":
                    v_high(j, PROJ[idx][1])
                else:
                    rope_hi(j, ROT_AT.index(idx))

            def group(j, last):
                for idx in (0, 1, 3, 2):
                    evict(j, idx)
                for s in range(8):
                    if s - 1 in LATE:
                        evict(j, LATE[s - 1])
                    if s:
                        for piece in range(3):
                            pt_high(24 * j + 3 * (s - 1), piece, pt_ps, pthi_done, P_UP, pt_hi)
                    if s - 1 in MID:
                        evict(j, MID[s - 1])
                    exps(8 * j + s, s % 2, c_score, shift_done, exp_done, rsum)
                    if s == 7:
                        normalise_last(j, s)
                    if s:
                        ctx_high(j, s - 1)
                    if s < 7:
                        normalise_last(j, s)
                    if s == 0:
                        evict(j, HEAD - 1)
                    if s == 3 and not last:
                        codes(j, kvcode, kvcode_f, d_code["kv"], 32 * (j + 1) + 32, kv_code)
                    if s == 4 and not last:
                        codes(j, qcode, qcode_f, d_code["q"], 16 * (j + 1) + 16, q_code)
                for piece in range(3):
                    pt_high(24 * j + 21, piece, pt_ps, pthi_done, P_UP, pt_hi)
                ctx_high(j, 7)
                if not last:
                    codes(j, ocode, ocode_f, d_code["o"], 16 * (j + 1) + 16, o_code)

            with act.Fori(0, KV_HEADS - 1) as j:
                group(j, False)
            group(KV_HEADS - 1, True)

            def w_scale(n):
                i = WEIGHTS.index(n)
                act.wait_ge(invw_done[i // 3], 1)
                act.activation(raw[n], raw[n], ACT.Copy, scale=inv_w[:, i:i + 1]).then_inc(w_scaled, 1)

            def w_high(n):
                act.wait_ge(w_scaled, WEIGHTS.index(n) + 1)
                act.activation(w_hi[n][:], raw[n], ACT.Copy).then_inc(whi_done, 1)

            for n in LOTS[0]:
                w_scale(n)
                w_high(n)
            beside = [(w, n) for n in LOTS[1] for w in (w_scale, w_high)]

            def m_high(m, src_scale):
                act.wait_ge(mt_ps, m + 1)
                act.activation(mt_hi[:, m % 2], bank[MT_BANK[m % 2]][:],
                               ACT.Copy, scale=src_scale).then_inc(mthi_done, 1)

            def gate_exp(ph, h):
                ts = slice(h * HALF, (h + 1) * HALF)
                act.wait_ge(dif_done, 2 * ph + h + 1)
                act.activation(ex[:, ts], dif[:, ts], ACT.Exp, scale=c_gate[:, 0:1]).then_inc(ex_done, 1)

            def experts(ph):
                c = 1 + 2 * ph
                m0 = ph * 2 * NT
                ln_hi(c, 0)
                for t in range(NT):
                    if t + 1 < NT:
                        ln_hi(c, t + 1)
                    if t == NT - 1:
                        m_high(m0, PROJ_DN_B)
                        gate_exp(ph, 1)
                    act.wait_ge(h_ps, NT * ph + t + 1)
                    act.activation(hidden[:, t], bank[t % 2][:], ACT.Copy).then_inc(h_done, 1)
                    if t == HALF:
                        gate_exp(ph, 0)
                    if ph == 0 and HALF < t < NT - 1:
                        w, n = beside[t - HALF - 1]
                        w(n)
                for t in range(1, NT):
                    m_high(m0 + t, PROJ_DN_B)
                    if ph == 0 and t < 5:
                        w, n = beside[t + 1]
                        w(n)

            experts(0)
            def stack_high(t):
                i2 = t % 2
                act.wait_ge(bq_rot, t + 1)
                st = q_stack[:, i2].rearrange("p (h e a d) -> p h e a d", h=B_HEADS, e=2, a=2)
                rq = rq1[:, i2].rearrange("p (h d) -> p h d", d=B_HD).unsqueeze(2)
                act.activation(st[:, :, :, 0], rq.broadcast_to([P, B_HEADS, 2, B_HD]), ACT.Copy).then_inc(bq_hi, 1)
                act.wait_ge(bk_rot, t + 1)
                st = k_stack[:, i2].rearrange("p (h e a d) -> p h e a d", h=KV_HEADS, e=2, a=2)
                rk = rk1[:, i2].rearrange("p (h d) -> p h d", d=B_HD).unsqueeze(2)
                act.activation(st[:, :, 0], rk.broadcast_to([P, KV_HEADS, 2, B_HD]), ACT.Copy).then_inc(bk_hi, 1)
                act.wait_ge(bkv_ps, t + 1)
                act.activation(heads_v(bv_hi, t), bank[5 + t % 2][:, P:2 * P].rearrange("p (h d) -> p h d", d=B_HD),
                               ACT.Copy, scale=PROJ_DN_B).then_inc(bv_hi_done, 1)

            def q_out(t):
                ts = slice(t * P, (t + 1) * P)
                for w in range(2):
                    act.wait_ge(bt_ps, 5 * t + w + 1)
                    act.activation(qt_b[:, 4 * w:4 * w + 4, ts],
                                   bank[t_bank(5 * t + w)][:].rearrange("p (c n) -> p c n", c=4),
                                   ACT.Copy).then_inc(bt_act, 1)

            def k_out(t):
                ts = slice(t * P, (t + 1) * P)
                act.wait_ge(bt_ps, 5 * t + 5)
                if t == 0:
                    act.wait_ge(zeros_done, 3)
                h = P // 2
                kt = kt_b[:].rearrange("p (c e) f n -> p c e f n", e=2)
                for e in range(2):
                    for f in range(2):
                        last = act.activation(
                            kt[f * h:(f + 1) * h, :, e, f, ts],
                            bank[t_bank(5 * t + 4)][e * h:(e + 1) * h].rearrange("p (c n) -> p c n", c=4), ACT.Copy)
                last.then_inc(bt_act, 1)

            ln_hi(2, 0)
            ln_hi(2, 1)
            for t in range(NT):
                if t:
                    q_out(t - 1)
                stack_high(t)
                if t + 2 < NT:
                    ln_hi(2, t + 2)
                if t:
                    k_out(t - 1)
            q_out(NT - 1)
            k_out(NT - 1)

            def b_group(j, first):
                for s in range(8):
                    n = 8 * j + s
                    if not (first and s == 0):
                        for piece in range(2):
                            pt_high(3 * (n - 1), piece, bpt_ps, bpthi, P_UP, ptb_hi[:, (s - 1) % 2],
                                    B_PT_BANK[(s - 1) % 2])
                    exps(n, s % 2, c_score_b, bshift, bexp)

            b_group(0, True)
            with act.Fori(1, KV_HEADS) as j:
                b_group(j, False)
            for piece in range(2):
                pt_high(3 * (8 * KV_HEADS - 1), piece, bpt_ps, bpthi, P_UP, ptb_hi[:, 1], B_PT_BANK[1])
            for t in range(NT):
                m_high(NT + t, 1.0)
            experts(1)

        @block.tensor
        def _(pe):
            def three(out_ap, a_hi, a_lo, b_hi, b_lo, k, n, stop=True):
                pe.matmul(out_ap, a_hi, b_hi, start=(k == 0), stop=False)
                pe.matmul(out_ap, a_hi, b_lo, start=False, stop=False)
                return pe.matmul(out_ap, a_lo, b_hi, start=False, stop=(stop and k == n - 1))

            def ln_t(c, t):
                i = NT * c + t
                pe.wait_ge(xn_ready, i + 1)
                if i >= 2:
                    pe.wait_ge(xt_done, i - 1)
                for k in range(KT):
                    mm = pe.transpose(bank[LN_BANK[c][t % 2]][:, k * P:(k + 1) * P],
                                      xn[:, t % 2, k * P:(k + 1) * P], ident[:])
                mm.then_inc(xt_ps, 1)

            pe.wait_ge(d_const, 16 * N_CONST)
            for t in range(NT):
                ln_t(0, t)
            pe.wait_ge(chain, 3)
            pe.wait_ge(xt_done, ST)

            def project(j, idx):
                kind, s = PROJ[idx]
                o_ap = bank[PROJ_BANK[idx]]
                if idx == 2:
                    pe.wait_ge(proj_read, 12 * j + 1)
                if idx >= HEAD:
                    before = max(i for i in range(idx) if PROJ_BANK[i] == PROJ_BANK[idx])
                    pe.wait_ge(proj_read, 12 * j + before + 1)
                b = s if kind != "q" else s // GROUP
                cols = slice(b * S, (b + 1) * S)
                if idx == 0:
                    pe.wait_ge(kv_w, 2 * j + 1)
                if idx == V_AT[0]:
                    pe.wait_ge(kv_w, 2 * j + 2)
                if idx == 1:
                    pe.wait_ge(q_w, 4 * j + 4)
                    pe.wait_ge(xt_done, NT)
                if kind == "v":
                    for t in range(ST):
                        c0 = (b * ST + t) * P
                        for g in range(KT):
                            mm = three(o_ap[:, t * P:(t + 1) * P], xt_hi[:, g, c0:c0 + P], xt_lo[:, g, c0:c0 + P],
                                       wkv_hi[:, 1, g], wkv_lo[:, 1, g], g, KT)
                else:
                    for g in range(KT):
                        hd = slice(s % GROUP * P, (s % GROUP + 1) * P)
                        a_hi, a_lo = ((wkv_hi[:, 0, g], wkv_lo[:, 0, g]) if kind == "k" else
                                      (wq_hi[:, g, hd], wq_lo[:, g, hd]))
                        mm = three(o_ap[:], a_hi, a_lo, xt_hi[:, g, cols], xt_lo[:, g, cols], g, KT)
                mm.then_inc(proj_ps, 1)

            def scores(j, s):
                b = s // GROUP
                pe.wait_ge(rot_done, 10 * j + ROT_AT.index(PROJ.index(("q", s))) + 1)
                for i in S_ORDER:
                    bk, o = S_BANK[i]
                    w = (i + 1) * P
                    if i != 2 and s:
                        pe.wait_ge(exp_done, 4 * (8 * j + s - 1) + bk + 2)
                    o_ap = bank[bk][:, o:o + w]
                    qs = slice(i * P, (i + 1) * P)
                    pe.matmul(o_ap, q_hi[:, s, qs], k_hi[:, b, 0:w], start=True, stop=False)
                    pe.matmul(o_ap, q_hi[:, s, qs], k_lo[:, b, 0:w], start=False, stop=False)
                    pe.matmul(o_ap, q_lo[:, s, qs], k_hi[:, b, 0:w], start=False, stop=False)
                    mm = pe.matmul(bank[bk][:, o + w - P:o + w], ident_b[:], mask_b[:], start=False, stop=True)
                    if i != 0:
                        mm.then_inc(s_ps, 1)

            def a_transposes(j, s):
                for piece, key_tiles in enumerate(((0,), (1, 3), (2,))):
                    if s:
                        pe.wait_ge(pt_done, 24 * j + 3 * (s - 1) + piece + 1)
                    if piece == 2 and (s == 0 or s in LATE):
                        pe.wait_ge(proj_read, 12 * j + V_AT[s // 2] + 1)
                    if piece == 2 and s in O_LATE:
                        pe.wait_ge(o_added, NT * j + O_LATE[s] + 1)
                    if piece == 0:
                        pe.wait_ge(prob_done, 3 * (8 * j + s) + 3)
                        pe.wait_ge(prob_last, 8 * j + s + 1)
                    for kt in key_tiles:
                        for i in range(kt, ST):
                            o = T_OFF[kt] - piece * S + (i - kt) * P
                            mm = pe.transpose(bank[PT_BANK[piece]][:, o:o + P],
                                              prob[:, s % 2, S_OFF[i] + kt * P:S_OFF[i] + (kt + 1) * P], ident[:])
                    mm.then_inc(pt_ps, 1)

            def a_pv(j, s):
                b = s // GROUP
                if s == 0:
                    pe.wait_ge(proj_read, 12 * j + HEAD)
                if s == GROUP:
                    pe.wait_ge(proj_read, 12 * j + V_AT[b] + 1)
                if s:
                    pe.wait_ge(ctx_done, 8 * j + s)
                for kt in (0, 1, 3, 2):
                    piece = {0: 0, 1: 1, 3: 1, 2: 2}[kt]
                    pe.wait_ge(pt_done, 24 * j + 3 * s + piece + 1)
                    w = S - kt * P
                    o_ap = bank[5][:, kt * P:S]
                    tc = slice(T_OFF[kt], T_OFF[kt] + w)
                    vs = slice(kt * P, (kt + 1) * P)
                    pe.matmul(o_ap, v_hi[:, b, vs], pt_hi[:, tc], start=(kt == 0), stop=False)
                    pe.matmul(o_ap, v_hi[:, b, vs], pt_lo[:, tc], start=False, stop=False)
                    mm = pe.matmul(o_ap, v_lo[:, b, vs], pt_hi[:, tc], start=False, stop=(kt == 2))
                mm.then_inc(ctx_ps, 1)

            def a_out(j, t):
                b = t // ST
                if t == 0:
                    pe.wait_ge(o_w, 4 * j + 4)
                    pe.wait_ge(ctx_done, 8 * j + GROUP)
                if t == 1:
                    pe.wait_ge(proj_read, 12 * j + 12)
                if t == 3:
                    pe.wait_ge(exp_done, 32 * j + 32)
                if O_BANK[t] in O_BANK[:t]:
                    before = max(i for i in range(t) if O_BANK[i] == O_BANK[t])
                    pe.wait_ge(o_added, NT * j + before + 1)
                ts = slice((t % ST) * P, (t % ST + 1) * P)
                for hh in range(GROUP):
                    if t == ST and hh == GROUP - 1:
                        pe.wait_ge(ctx_done, 8 * j + 8)
                    mm = three(bank[O_BANK[t]][:], ctx_hi[:, b * GROUP + hh, ts], ctx_lo[:, b * GROUP + hh, ts],
                               wo_hi[:, hh], wo_lo[:, hh], hh, GROUP)
                mm.then_inc(o_ps, 1)

            with pe.Fori(0, KV_HEADS) as j:
                for idx in range(HEAD):
                    project(j, idx)
                for s in range(8):
                    scores(j, s)
                    if s:
                        a_transposes(j, s - 1)
                    if s in MID:
                        project(j, MID[s])
                    if s in O_MID:
                        a_out(j, O_MID[s])
                    if s:
                        a_pv(j, s - 1)
                    if s in LATE:
                        project(j, LATE[s])
                    if s in O_LATE:
                        a_out(j, O_LATE[s])
                a_transposes(j, 7)
                a_out(j, 3)
                a_pv(j, 7)
                for t in range(ST, NT):
                    a_out(j, t)

            def turn(m, src, ready, count):
                pe.wait_ge(ready, count)
                if m >= 2:
                    pe.wait_ge(mt_done, m - 1)
                bk = bank[MT_BANK[m % 2]]
                for k in range(KT):
                    mm = pe.transpose(bk[:, k * P:(k + 1) * P], src[:, k * P:(k + 1) * P], ident[:])
                mm.then_inc(mt_ps, 1)

            def second(m, name):
                wh = w_hi[name][:].rearrange("p (k n) -> p k n", k=KT)
                wl = w_lo[name][:].rearrange("p (k n) -> p k n", k=KT)
                pe.wait_ge(mt_done, m + 1)
                if m >= 2:
                    pe.wait_ge(y_added, m - 1)
                for k in range(KT):
                    ks = slice(k * P, (k + 1) * P)
                    mm = three(bank[6 + m % 2][:], mt_hi[:, m % 2, ks], mt_lo[:, m % 2, ks], wh[:, k], wl[:, k], k, KT)
                mm.then_inc(y_ps, 1)

            def wide(out_ap, t, name, n):
                wh = w_hi[name][:].rearrange("p (k n) -> p k n", k=KT)
                wl = w_lo[name][:].rearrange("p (k n) -> p k n", k=KT)
                ts = slice(t * P, (t + 1) * P)
                for k in range(KT):
                    mm = three(out_ap, xt_hi[:, k, ts], xt_lo[:, k, ts], wh[:, k], wl[:, k], k, KT)
                return mm

            def experts(ph):
                c = 1 + 2 * ph
                m0, f0 = ph * 2 * NT, ph * NT
                if ph == 0:
                    ln_t(c, 0)
                if ph == 0:
                    pe.wait_ge(wlo_done, 2)
                for t in range(NT):
                    if t + 1 < NT and (ph == 0 or t):
                        ln_t(c, t + 1)
                    pe.wait_ge(xt_done, NT * c + t + 1)
                    e0 = t % HALF * EXPERTS
                    wide(bank[GATE_BANK[t // HALF]][:, e0:e0 + EXPERTS], t, "gate", EXPERTS).then_inc(g_ps, 1)
                    if t == NT - 1:
                        turn(m0, hs[:, 0], hs_done, f0 + 1)
                    if t >= 2:
                        pe.wait_ge(h_done, f0 + t - 1)
                    wide(bank[t % 2][:], t, "lora_a", D).then_inc(h_ps, 1)
                if ph == 0:
                    pe.wait_ge(wlo_done, 3)
                pe.wait_ge(h_done, f0 + NT - 1)
                for t in range(NT):
                    if t + 1 < NT:
                        turn(m0 + t + 1, hs[:, (t + 1) % 2], hs_done, f0 + t + 2)
                    elif ph == 0:
                        ln_t(2, 0)
                        ln_t(2, 1)
                    second(m0 + t, "lora_b")

            experts(0)
            def stack_t(t, units):
                for w in units:
                    bk = bank[t_bank(5 * t + w)]
                    if w == 0:
                        pe.wait_ge(bq_lo, t + 1)
                    if w == 4:
                        pe.wait_ge(bk_lo, t + 1)
                    if w == 0 and t:
                        pe.wait_ge(bt_dve, 2 * t)
                    if w == 1 and t:
                        pe.wait_ge(bt_act, 3 * t)
                    if w == 2 or w == 3:
                        pe.wait_ge(bt_act, 3 * t + w - 1)
                    if w == 4:
                        pe.wait_ge(bt_dve, 2 * t + 1)
                    for c in range(4):
                        src = (q_stack[:, t % 2, (4 * w + c) * P:(4 * w + c + 1) * P] if w < 4 else
                               k_stack[:, t % 2, c * P:(c + 1) * P])
                        mm = pe.matmul(bk[:, c * P:(c + 1) * P], src, ident_h[:], start=True, stop=True)
                    mm.then_inc(bt_ps, 1)

            pe.wait_ge(wlo_done, 3 + 4 + 2 + 1)
            for t in range(NT):
                pe.wait_ge(xt_done, NT * 2 + t + 1)
                if t >= 2:
                    pe.wait_ge(bq_mul, t - 1)
                wide(bank[t % 2][:], t, "b_q", D).then_inc(bq_ps, 1)
                if t:
                    stack_t(t - 1, (0, 1))
                if t >= 2:
                    pe.wait_ge(bv_lo_done, t - 1)
                wide(bank[5 + t % 2][:, 0:2 * P], t, "b_kv", 2 * P).then_inc(bkv_ps, 1)
                if t:
                    stack_t(t - 1, (2, 3))
                if t + 2 < NT:
                    ln_t(2, t + 2)
                if t:
                    stack_t(t - 1, (4,))
            def b_scores(j, s, bk, first):
                hh, b = s // B, s % B
                n = 8 * j + s
                if not (first and s == 0) and bk < 2:
                    pe.wait_ge(bexp, 4 * n - 4 + bk + 2)
                for i in [i for i in S_ORDER if S_BANK[i][0] == bk]:
                    o = S_BANK[i][1]
                    w = (i + 1) * P
                    pe.matmul(bank[bk][:, o:o + w],
                              qt_b[:, bass.ds(2 * j + hh // 2, 1), b * S + i * P:b * S + (i + 1) * P].rearrange(
                                  "p o n -> p (o n)"),
                              kt_b[:, bass.ds(j, 1), hh % 2, b * S:b * S + w].rearrange("p o n -> p (o n)"),
                              start=True, stop=False)
                    mm = pe.matmul(bank[bk][:, o + w - P:o + w], ident_b[:], mask_b[:], start=False, stop=True)
                mm.then_inc(bs_ps, 1)

            pe.wait_ge(bt_act, 3 * ST)
            pe.wait_ge(bt_dve, 2 * ST)
            pe.wait_ge(bq_mul, NT)
            b_scores(0, 0, 0, True)
            b_scores(0, 0, 1, True)
            stack_t(NT - 1, range(5))
            pe.wait_ge(bt_act, 3 * (NT - 1) + 2)
            pe.wait_ge(bt_dve, 2 * NT)
            b_scores(0, 0, 2, True)
            pe.wait_ge(bt_act, 3 * NT)
            pe.wait_ge(bv_lo_done, NT)

            def b_transposes(n, i, i2, first, awaited):
                if i == 0 and not first:
                    pe.wait_ge(bpt, 3 * n - 1)
                if awaited:
                    pe.wait_ge(bexp, 4 * n + S_PLACE[i] + 1)
                for kt in (0, 1, 3, 2):
                    if kt > i:
                        continue
                    piece = {0: 0, 1: 1, 3: 1, 2: 2}[kt]
                    o = T_OFF[kt] - piece * S + (i - kt) * P
                    mm = pe.transpose(bank[B_PT_BANK[i2][piece]][:, o:o + P],
                                      prob[:, i2, S_OFF[i] + kt * P:S_OFF[i] + (kt + 1) * P], ident[:])
                    if i == 3 and kt != 1:
                        mm.then_inc(bpt_ps, 1)

            def b_pv(j, s, first):
                b = s % B
                n = 8 * j + s
                if not first:
                    pe.wait_ge(bctx, n)
                pe.wait_ge(bpt, 3 * n + 3)
                pe.wait_ge(bpt_last, n + 1)
                vc = bass.ds(j * B_VD, B_VD)
                hi, lo = ptb_hi[:, s % 2], ptb_lo[:, s % 2]
                for i in range(ST):
                    o_ap = bank[CTX_BANK][:, i * B_VD:(i + 1) * B_VD]
                    for kt in range(i + 1):
                        tc = slice(T_OFF[kt] + (i - kt) * P, T_OFF[kt] + (i - kt + 1) * P)
                        vh, vl = bv_hi[:, b * ST + kt, vc], bv_lo[:, b * ST + kt, vc]
                        mm = three(o_ap, hi[:, tc], lo[:, tc], vh, vl, kt, i + 1)
                mm.then_inc(bctx_ps, 1)

            def b_group(j, first):
                for s in range(1 if first else 0, 8):
                    for bk, tiles in enumerate(((0, 2), (1, 3), ())):
                        b_scores(j, s, bk, first)
                        for i in tiles:
                            b_transposes(8 * j + s - 1, i, (s - 1) % 2, first and s == 1, i == 3)
                    if s >= 2:
                        b_pv(j, s - 2, first and s < 3)
                    elif not first:
                        b_pv(j - 1, s + 6, False)

            b_group(0, True)
            with pe.Fori(1, KV_HEADS) as j:
                b_group(j, False)
            for i in range(ST):
                b_transposes(8 * KV_HEADS - 1, i, 1, False, True)
            b_pv(KV_HEADS - 1, 6, False)
            b_pv(KV_HEADS - 1, 7, False)
            turn(NT, ctx_b[:, 0], bctx, 8 * KV_HEADS - 1)
            for t in range(NT):
                if t + 1 < NT:
                    turn(NT + t + 1, ctx_b[:, t + 1], bctx, 8 * KV_HEADS - (t + 1 < ST))
                else:
                    ln_t(3, 0)
                    ln_t(3, 1)
                second(NT + t, "b_o")
            experts(1)

        @block.vector
        def _(dve):
            off = 0
            dve.wait_ge(d_scale, 64)
            for i, n in enumerate(QUANT):
                w = QUANT_COLS[n]
                dve.tensor_reduce(amax_q[:, i:i + 1], scn[:, off:off + w], AX, ALU.max,
                                  apply_absolute_value=True).then_inc(amaxq_done, 1)
                off += w

            def power_of_two(value, inv, c, red, done):
                dve.wait_ge(red, 1)
                dve.tensor_scalar(value[:, c], value[:, c], 1e-30, None, ALU.max).then_inc(red, 1)
                dve.wait_ge(red, 2)
                dve.tensor_single_scalar(value[:, c].bitcast(U32), value[:, c].bitcast(U32), 0x7F800000,
                                         ALU.bitwise_and).then_inc(red, 1)
                dve.wait_ge(red, 3)
                dve.reciprocal(inv[:, c], value[:, c]).then_inc(red, 1)
                dve.wait_ge(red, 4)
                dve.tensor_scalar(inv[:, c], inv[:, c], W_UP, None, ALU.mult).then_inc(done, 1)
                dve.wait_ge(done, 1)

            def ln_stats(c, t):
                i = 3 * (NT * c + t)
                dve.bn_stats(bn[:, t], x[:, t]).then_inc(ln_stat, 1)
                dve.wait_ge(ln_stat, i + 1)
                dve.bn_aggr(mv[:, t], bn[:, t]).then_inc(ln_stat, 1)
                dve.wait_ge(ln_stat, i + 2)
                dve.tensor_scalar(mv[:, t, 1:2], mv[:, t, 1:2], EPS, None, ALU.add).then_inc(ln_stat, 1)

            def ln_norm(c, t):
                i = NT * c + t
                if i >= 2:
                    dve.wait_ge(xt_ps, i - 1)
                dve.wait_ge(ln_rstd, i + 1)
                dve.tensor_scalar(xn[:, t % 2], x[:, t], mv[:, t, 0:1], rstd[:, t:t + 1], ALU.subtract,
                                  ALU.mult).then_inc(xn_ready, 1)

            def ln_lo(c, t):
                dve.wait_ge(xthi_done, NT * c + t + 1)
                dve.scalar_tensor_tensor(out=xt_lo[:, :, t * P:(t + 1) * P],
                                         in0=bank[LN_BANK[c][t % 2]][:].rearrange("p (k n) -> p k n", k=KT),
                                         scalar=X_UP, in1=xt_hi[:, :, t * P:(t + 1) * P], op0=ALU.mult,
                                         op1=ALU.subtract).then_inc(xt_done, 1)

            power_of_two(pow_q, inv_q, slice(0, 4), redq, invq_done)
            off = 0
            for i, n in enumerate(QUANT):
                w = QUANT_COLS[n]
                dve.tensor_scalar(scn[:, off:off + w], scn[:, off:off + w], inv_q[:, i:i + 1], None,
                                  ALU.mult).then_inc(scn_done, 1)
                off += w
            dve.wait_ge(d_x[0], 16)
            for t in range(3):
                ln_stats(0, t)
            dve.wait_ge(d_const, 16 * N_CONST)
            dve.tensor_copy(ident_h[:], ident[:]).then_inc(chain, 1)
            dve.tensor_copy(ident_b[:], ident[:]).then_inc(chain, 1)
            dve.tensor_copy(mask_b[:], mask_f[:]).then_inc(chain, 1)
            ln_norm(0, 0)
            ln_norm(0, 1)
            ln_stats(0, ST - 1)

            def first_q(i):
                g = 2 + i
                dve.wait_ge(q_code, 1)
                dve.wait_ge(d_wscale["q"], 16)
                dve.tensor_tensor(wq_hi[:, g], qcode_f[:, g], qscale[:, g], ALU.mult).then_inc(w_first, 1)
                dve.tensor_tensor(qcode_f[:, g], qcode_f[:, g], qscale[:, g], ALU.mult).then_inc(w_first, 1)
                dve.wait_ge(w_first, 2 * i + 2)
                dve.tensor_tensor(wq_lo[:, g], qcode_f[:, g], wq_hi[:, g], ALU.subtract).then_inc(q_w, 1)

            for t in range(ST):
                ln_lo(0, t)
                if t + 2 < ST:
                    ln_norm(0, t + 2)
            dve.wait_ge(d_x[1], 16)
            for t in range(ST, ST + 2):
                ln_stats(0, t)
            for t in range(ST, ST + 2):
                ln_norm(0, t)
            for t in range(ST, NT):
                if t + 2 < NT:
                    ln_stats(0, t + 2)
                ln_lo(0, t)
                if t == ST:
                    first_q(0)
                if t + 2 < NT:
                    ln_norm(0, t + 2)
            first_q(1)
            dve.tensor_tensor(c_score[:, 0:1], pow_q[:, 0:1], pow_q[:, 1:2], ALU.mult).then_inc(chain, 1)
            dve.tensor_tensor(c_out[:], pow_q[:, 2:3], pow_q[:, 3:4], ALU.mult).then_inc(chain, 1)
            dve.wait_ge(chain, 5)
            k_a = float(A_HD ** -0.5) / 16.0
            dve.tensor_scalar(c_score[:, 1:2], c_score[:, 0:1], -k_a, None, ALU.mult).then_inc(chain, 1)
            dve.tensor_scalar(c_out[:], c_out[:], 1.0 / (4.0 * W_UP), None, ALU.mult).then_inc(chain, 1)
            dve.wait_ge(chain, 7)
            dve.tensor_scalar(c_score[:, 0:1], c_score[:, 0:1], k_a, None, ALU.mult).then_inc(chain, 1)

            def rope(j, u, idx):
                dve.wait_ge(proj_ps, 12 * j + idx + 1)
                if u >= 2:
                    dve.wait_ge(rot_done, 10 * j + u - 1)
                h = P // 2
                ps = bank[PROJ_BANK[idx]]
                dve.tensor_tensor(rt2[0:h, u % 2], ps[h:P], sin_a[h:P], ALU.mult)
                dve.tensor_tensor(rt2[h:P, u % 2], ps[0:h], sin_a[0:h], ALU.mult)
                dve.tensor_tensor(rt1[:, u % 2], ps[:], cos_a[:], ALU.mult).then_inc(proj_read, 1)

            def v_low(j, b):
                dve.wait_ge(vhi_done, 2 * j + b + 1)
                dve.scalar_tensor_tensor(out=v_lo[:, b], in0=bank[PROJ_BANK[V_AT[b]]][:], scalar=PROJ_DN,
                                         in1=v_hi[:, b], op0=ALU.mult, op1=ALU.subtract).then_inc(proj_read, 1)

            def row_max(n, i2, ps, own, shifted):
                for bk, (c0, c1) in enumerate(BANK_PLACES):
                    dve.wait_ge(ps, 3 * n + bk + 1)
                    for c in range(c0, c1):
                        i = S_ORDER[c]
                        o = S_BANK[i][1]
                        dve.tensor_reduce(smax[:, i2, c:c + 1], bank[bk][:, o:o + (i + 1) * P], AX,
                                          ALU.max).then_inc(own, 1)
                    shifted(c0, c1)

            def a_row_max(n, i2):
                def shifted(c0, c1):
                    dve.wait_ge(smax_done, 4 * n + c1)
                    dve.tensor_scalar(shift[:, i2, c0:c1], smax[:, i2, c0:c1], c_score[:, 1:2], None,
                                      ALU.mult).then_inc(shift_done, 1)

                row_max(n, i2, s_ps, smax_done, shifted)

            def pt_low(count, piece, hi_done, done, scale, hi, lo, banks=PT_BANK):
                w = S if piece < 2 else 2 * P
                c = slice(piece * S, piece * S + w)
                dve.wait_ge(hi_done, count)
                dve.scalar_tensor_tensor(out=lo[:, c], in0=bank[banks[piece]][:, 0:w], scalar=scale, in1=hi[:, c],
                                         op0=ALU.mult, op1=ALU.subtract).then_inc(done, 1)

            def normalise(j, s):
                n = 8 * j + s
                dve.wait_ge(exp_done, 4 * n + 4)
                dve.reciprocal(rden[:, s % 2], rsum[:, s % 2]).then_inc(rden_done, 1)
                dve.wait_ge(rden_done, n + 1)
                for i in range(ST - 1):
                    w = (i + 1) * P
                    pr = prob[:, s % 2, S_OFF[i]:S_OFF[i] + w]
                    c = S_PLACE[i]
                    dve.tensor_scalar(pr, pr, rden[:, s % 2, c:c + 1], None, ALU.mult).then_inc(prob_done, 1)

            def ctx_low(j, s):
                dve.wait_ge(ctxhi_done, 8 * j + s + 1)
                dve.scalar_tensor_tensor(out=ctx_lo[:, s], in0=bank[5][:], scalar=1.0 / P_UP, in1=ctx_hi[:, s],
                                         op0=ALU.mult, op1=ALU.subtract).then_inc(ctx_done, 1)

            def o_add(j, t):
                dve.wait_ge(o_ps, NT * j + t + 1)
                dve.scalar_tensor_tensor(out=x[:, t], in0=bank[O_BANK[t]][:], scalar=c_out[:, 0:1], in1=x[:, t],
                                         op0=ALU.mult, op1=ALU.add).then_inc(o_added, 1)

            def read(j, idx):
                if PROJ[idx][0] == "v":
                    v_low(j, PROJ[idx][1])
                else:
                    rope(j, ROT_AT.index(idx), idx)

            def w_largest(n):
                i = WEIGHTS.index(n)
                dve.wait_ge(d_raw[i // 3], 48)
                dve.tensor_reduce(amax_w[:, i:i + 1], raw[n], AX, ALU.max,
                                  apply_absolute_value=True).then_inc(amaxw_done[i // 3], 1)

            def w_factors(lot):
                power_of_two(pow_w, inv_w, slice(3 * lot, 3 * lot + 3), redw[lot], invw_done[lot])
                p = {n: pow_w[:, i:i + 1] for i, n in enumerate(WEIGHTS)}
                if lot == 0:
                    dve.tensor_tensor(c_ffn[:], p["lora_a"], p["lora_b"], ALU.mult).then_inc(chain, 1)
                    dve.tensor_scalar(c_gate[:], p["gate"], 1.0 / (X_UP * W_UP), None, ALU.mult).then_inc(chain, 1)
                    dve.wait_ge(chain, 10)
                    dve.tensor_scalar(c_ffn[:], c_ffn[:], 1.0 / (32.0 * W_UP), None, ALU.mult).then_inc(chain, 1)
                    return
                k_b = float(B_HD ** -0.5) / 1024.0
                dve.tensor_tensor(c_score_b[:, 0:1], p["b_q"], p["b_kv"], ALU.mult).then_inc(chain, 1)
                dve.tensor_tensor(c_out_b[:], p["b_kv"], p["b_o"], ALU.mult).then_inc(chain, 1)
                dve.wait_ge(chain, 13)
                dve.tensor_scalar(c_out_b[:], c_out_b[:], 1.0 / (32.0 * W_UP), None, ALU.mult).then_inc(chain, 1)
                dve.tensor_scalar(c_score_b[:, 1:2], c_score_b[:, 0:1], -k_b, None, ALU.mult).then_inc(chain, 1)
                dve.wait_ge(chain, 15)
                dve.tensor_scalar(c_score_b[:, 0:1], c_score_b[:, 0:1], k_b, None, ALU.mult).then_inc(chain, 1)

            def group(j, last):
                def o_add_stats(t):
                    o_add(j, t)
                    if last:
                        dve.wait_ge(o_added, NT * j + t + 1)
                        ln_stats(1, t)

                for idx in range(HEAD):
                    read(j, idx)
                for s in range(8):
                    a_row_max(8 * j + s, s % 2)
                    if s:
                        for piece in range(3):
                            pt_low(24 * j + 3 * (s - 1) + piece + 1, piece, pthi_done, pt_done, P_UP, pt_hi, pt_lo)
                    if s in MID:
                        read(j, MID[s])
                    if s in O_MID and s < 7:
                        o_add_stats(O_MID[s])
                    normalise(j, s)
                    if s == 7:
                        o_add_stats(O_MID[s])
                    if s:
                        ctx_low(j, s - 1)
                    if s in LATE:
                        read(j, LATE[s])
                    if s in O_LATE:
                        o_add_stats(O_LATE[s])
                    if last and s == 3:
                        w_largest("lora_a")
                        w_largest("gate")
                    if last and s == 4:
                        w_largest("lora_b")
                for piece in range(3):
                    pt_low(24 * j + 21 + piece + 1, piece, pthi_done, pt_done, P_UP, pt_hi, pt_lo)
                o_add_stats(3)
                ctx_low(j, 7)
                if last:
                    w_factors(0)
                for t in range(ST, NT):
                    if last and t == NT - 2:
                        ln_norm(1, 0)
                        ln_norm(1, 1)
                    o_add_stats(t)

            with dve.Fori(0, KV_HEADS - 1) as j:
                group(j, False)
            group(KV_HEADS - 1, True)

            steps = [0]

            def step(ins):
                ins.then_inc(gate_step, 1)
                steps[0] += 1
                dve.wait_ge(gate_step, steps[0])

            pair = [P, HALF, TOP_K]
            all_e = [P, HALF, TOP_K, EXPERTS]

            def gate_choice(ph, h):
                ts = slice(h * HALF, (h + 1) * HALF)
                tiles = range(h * HALF, (h + 1) * HALF)
                dve.wait_ge(g_ps, NT * ph + (h + 1) * HALF)
                step(dve.tensor_copy(lg[:, ts], bank[GATE_BANK[h]][:, 0:HALF * EXPERTS].rearrange(
                    "p (t e) -> p t e", t=HALF)))
                for t in tiles:
                    last = dve.max(top[:, t], lg[:, t])
                step(last)
                dve.tensor_tensor(dif[:, ts], top[:, ts, 0:TOP_K], top[:, ts, 0:1].broadcast_to(pair),
                                  ALU.subtract).then_inc(dif_done, 1)
                for t in tiles:
                    last = dve.max_index(topi[:, t], top[:, t], lg[:, t])
                step(last)
                step(dve.tensor_copy(topf[:, ts], topi[:, ts, 0:TOP_K]))
                step(dve.tensor_tensor(chosen[:, ts], iota_e[:].unsqueeze(1).unsqueeze(1).broadcast_to(all_e),
                                       topf[:, ts].unsqueeze(3).broadcast_to(all_e), ALU.is_equal))

            def gate_weights(ph, h):
                ts = slice(h * HALF, (h + 1) * HALF)
                dve.wait_ge(ex_done, 2 * ph + h + 1)
                step(dve.tensor_tensor(exs[:, ts], ex[:, ts, 0:1], ex[:, ts, 1:2], ALU.add))
                step(dve.reciprocal(exr[:, ts], exs[:, ts]))
                step(dve.tensor_tensor(wgt[:, ts], ex[:, ts], exr[:, ts].broadcast_to(pair), ALU.mult))
                step(dve.tensor_tensor(chosen[:, ts], chosen[:, ts], wgt[:, ts].unsqueeze(3).broadcast_to(all_e),
                                       ALU.mult))
                dve.tensor_tensor(wfull[:, ts], chosen[:, ts, 0], chosen[:, ts, 1], ALU.add).then_inc(wfull_done, 1)

            def m_low(m, scale):
                dve.wait_ge(mthi_done, m + 1)
                dve.scalar_tensor_tensor(out=mt_lo[:, m % 2],
                                         in0=bank[MT_BANK[m % 2]][:], scalar=scale, in1=mt_hi[:, m % 2],
                                         op0=ALU.mult, op1=ALU.subtract).then_inc(mt_done, 1)

            def y_add(m, t, factor):
                dve.wait_ge(y_ps, m + 1)
                dve.scalar_tensor_tensor(out=x[:, t], in0=bank[6 + m % 2][:], scalar=factor[:, 0:1], in1=x[:, t],
                                         op0=ALU.mult, op1=ALU.add).then_inc(y_added, 1)

            def y_adds(m0, scale, factor, after):
                for t in range(NT):
                    if t + 1 < NT:
                        m_low(m0 + t + 1, scale)
                    y_add(m0 + t, t, factor)
                    if after is not None:
                        dve.wait_ge(y_added, m0 + t + 1)
                        ln_stats(after, t)
                        if t == NT - 3:
                            ln_norm(after, 0)
                            ln_norm(after, 1)
                        if t == NT - 2:
                            ln_lo(after, 0)
                            ln_lo(after, 1)

            def experts(ph, after):
                c = 1 + 2 * ph
                if ph == 0:
                    ln_lo(c, 0)
                for t in range(NT):
                    if t + 1 < NT and (ph == 0 or t):
                        ln_lo(c, t + 1)
                    if t + 2 < NT:
                        ln_norm(c, t + 2)
                    if ph == 0 and 1 <= t < 4:
                        w_largest(LOTS[1][t - 1])
                    if t == HALF:
                        gate_choice(ph, 0)
                    if t == HALF + 1:
                        gate_weights(ph, 0)
                        if ph == 0:
                            w_factors(1)
                m_low(ph * 2 * NT, PROJ_DN_B)
                gate_choice(ph, 1)
                gate_weights(ph, 1)
                y_adds(ph * 2 * NT, PROJ_DN_B, c_ffn, after)

            experts(0, 2)

            H2 = B_HD // 2

            def rope_products(src, o1, o2, t):
                heads = src.shape[1] // B_HD
                cs = cos_b[:, t % ST].unsqueeze(1)
                s4 = src.rearrange("p (h a d) -> p h a d", a=2, d=H2)
                v2 = o2.rearrange("p (h a d) -> p h a d", a=2, d=H2)
                for a in range(2):
                    sn = sin_b[:, t % ST, a].unsqueeze(1)
                    dve.tensor_tensor(v2[:, :, a], s4[:, :, 1 - a], sn.broadcast_to([P, heads, H2]), ALU.mult)
                return dve.tensor_tensor(o1.rearrange("p (h d) -> p h d", d=H2),
                                         src.rearrange("p (h d) -> p h d", d=H2),
                                         cs.broadcast_to([P, 2 * heads, H2]), ALU.mult)

            def kv_low(t):
                dve.wait_ge(bk_hi, t + 1)
                st = k_stack[:, t % 2].rearrange("p (h e a d) -> p h e a d", h=KV_HEADS, e=2, a=2)
                rk = rk1[:, t % 2].rearrange("p (h d) -> p h d", d=B_HD).unsqueeze(2)
                dve.tensor_tensor(st[:, :, 1], rk.broadcast_to([P, KV_HEADS, 2, B_HD]), st[:, :, 0],
                                  ALU.subtract).then_inc(bk_lo, 1)
                dve.wait_ge(bv_hi_done, t + 1)
                dve.scalar_tensor_tensor(out=heads_v(bv_lo, t),
                                         in0=bank[5 + t % 2][:, P:2 * P].rearrange("p (h d) -> p h d", d=B_HD),
                                         scalar=PROJ_DN_B, in1=heads_v(bv_hi, t), op0=ALU.mult,
                                         op1=ALU.subtract).then_inc(bv_lo_done, 1)

            def stack_out(t):
                for w in range(2, 4):
                    dve.wait_ge(bt_ps, 5 * t + w + 1)
                    dve.tensor_copy(qt_b[:, 4 * w:4 * w + 4, t * P:(t + 1) * P],
                                    bank[t_bank(5 * t + w)][:].rearrange("p (c n) -> p c n", c=4)).then_inc(bt_dve, 1)

            ln_norm(2, 2)
            for t in range(NT):
                if t:
                    kv_low(t - 1)
                dve.wait_ge(bq_ps, t + 1)
                if t >= 2:
                    dve.wait_ge(bq_lo, t - 1)
                rope_products(bank[t % 2][:], rq1[:, t % 2], rq2[:, t % 2], t).then_inc(bq_mul, 1)
                dve.wait_ge(bkv_ps, t + 1)
                rope_products(bank[5 + t % 2][:, 0:P], rk1[:, t % 2], rk2[:, t % 2], t).then_inc(bk_mul, 1)
                if t:
                    stack_out(t - 1)
                if t + 2 < NT:
                    ln_lo(2, t + 2)
                if t + 3 < NT:
                    ln_norm(2, t + 3)
            dve.wait_ge(bq_hi, NT)
            st = q_stack[:, (NT - 1) % 2].rearrange("p (h e a d) -> p h e a d", h=B_HEADS, e=2, a=2)
            rq = rq1[:, (NT - 1) % 2].rearrange("p (h d) -> p h d", d=B_HD).unsqueeze(2)
            dve.tensor_tensor(st[:, :, :, 1], rq.broadcast_to([P, B_HEADS, 2, B_HD]), st[:, :, :, 0],
                              ALU.subtract).then_inc(bq_lo, 1)
            kv_low(NT - 1)
            stack_out(NT - 1)

            def b_rden(n, i2, first):
                if not first:
                    dve.wait_ge(bctx, n - 1)
                dve.wait_ge(bctx_ps, n + 1)
                dve.reciprocal(rden[:, i2],
                               bank[CTX_BANK][:, 0:ST * B_VD].rearrange("p (i d) -> p i d", d=B_VD)[:, :, B_HD]
                               ).then_inc(brden, 1)

            def b_ctx(j, s):
                hh, b = s // B, s % B
                n = 8 * j + s
                ps = bank[CTX_BANK][:, 0:ST * B_VD].rearrange("p (i d) -> p i d", d=B_VD)
                dve.wait_ge(brden, n + 1)
                dve.tensor_tensor(ctx_b[:, b * ST:(b + 1) * ST, bass.ds(j * (GROUP * B_HD) + hh * B_HD, B_HD)],
                                  ps[:, :, 0:B_HD], rden[:, s % 2].unsqueeze(2).broadcast_to([P, ST, B_HD]),
                                  ALU.mult).then_inc(bctx, 1)

            def b_low_piece(n, i2, piece):
                pt_low(2 * n + piece + 1, piece, bpthi, bpt, P_UP, ptb_hi[:, i2], ptb_lo[:, i2], B_PT_BANK[i2])

            def b_low(n, i2, first):
                if not first:
                    dve.wait_ge(bpt_last, n - 1)
                dve.wait_ge(bpt_ps, 3 * n + 3)
                dve.tensor_scalar(ptb_32[:, i2], bank[B_PT_BANK[i2][2]][:, 0:TRI - 2 * S], P_UP, None, ALU.mult
                                  ).then_inc(bpt, 1)
                b_low_piece(n, i2, 0)

            def b_group(j, first):
                for s in range(8):
                    n = 8 * j + s
                    row_max(n, s % 2, bs_ps, bsmax, lambda c0, c1: None)
                    if not (first and s < 1):
                        b_low(n - 1, (s - 1) % 2, first and s < 3)
                    if not (first and s < 2):
                        b_rden(n - 2, s % 2, first and s < 4)
                    if not (first and s < 1):
                        b_low_piece(n - 1, (s - 1) % 2, 1)
                    if s >= 2:
                        b_ctx(j, s - 2)
                    elif not first:
                        b_ctx(j - 1, s + 6)

            b_group(0, True)
            with dve.Fori(1, KV_HEADS) as j:
                b_group(j, False)
            last = 8 * KV_HEADS - 1
            b_low(last, 1, False)
            b_low_piece(last, 1, 1)
            for s in (6, 7):
                b_rden(last - 7 + s, s % 2, False)
                b_ctx(KV_HEADS - 1, s)
            m_low(NT, 1.0)
            y_adds(NT, 1.0, c_out_b, 3)
            experts(1, None)


def constants():
    pos = np.arange(S, dtype=np.float32)
    inv = (np.float32(1.0) / np.float32(10000.0) ** (np.arange(0, A_HD, 2, dtype=np.float32) / np.float32(A_HD)))
    f = pos[:, None] * inv.astype(np.float32)[None, :]
    cos, sin = np.cos(f).T.astype(np.float32), np.sin(f).T.astype(np.float32)
    cos_a = np.concatenate([cos, cos]) * np.float32(PROJ_DN)
    sin_a = np.concatenate([sin, -sin]) * np.float32(PROJ_DN)

    theta, factor, hi, lo, ctx_len = 500000.0, 32.0, 4.0, 1.0, 1024
    idx = np.arange(0, B_HD, 2, dtype=np.float32) / np.float32(B_HD)
    freq = np.float32(1.0 / (2.0 * np.pi)) * (np.float32(theta) ** (-idx)).astype(np.float32)
    scaled = np.where(freq < lo / ctx_len, freq / np.float32(factor), freq)
    smooth = np.clip((ctx_len * freq - np.float32(lo)) / np.float32(hi - lo), 0.0, 1.0).astype(np.float32)
    mid = (1 - smooth) * (freq / np.float32(factor)) + smooth * freq
    freq = np.where((freq >= lo / ctx_len) & (freq <= hi / ctx_len), mid, scaled).astype(np.float32)
    phase = (np.float32(2.0 * np.pi) * pos)[:, None] * freq[None, :]
    table = lambda a: np.ascontiguousarray(
        (a.astype(np.float32) * np.float32(PROJ_DN_B)).reshape(ST, P, -1).transpose(1, 0, 2))
    sin_b = table(np.concatenate([-np.sin(phase), np.sin(phase)], axis=1)).reshape(P, ST, 2, B_HD // 2)
    i = np.arange(P)
    mask = np.where(i[None, :] <= i[:, None], 0.0, MASKED).astype(np.float32)
    return {"ident": np.eye(P, dtype=np.float32), "mask": mask, "cos_a": cos_a.astype(np.float32),
            "sin_a": sin_a.astype(np.float32), "cos_b": table(np.cos(phase)), "sin_b": sin_b}


def kernel(**inputs):
    import concourse.bacc as bacc
    from concourse.bass_utils import run_bass_kernel_spmd

    a = {n: np.asarray(v) for n, v in inputs.items()}
    pre = "L0_attn_a_"
    tiles = lambda w: w.reshape(KT, P, -1).transpose(1, 0, 2).reshape(P, -1)

    def even_odd(w, heads):
        return w.reshape(-1, heads, A_HD // 2, 2).swapaxes(2, 3).reshape(w.shape)

    def by_group(w):
        return w.reshape(KT, P, KV_HEADS, -1).transpose(2, 1, 0, 3)

    def scales_by_group(w):
        return w.reshape(KT, KV_HEADS, -1).transpose(1, 0, 2).reshape(-1)

    q, k = even_odd(a[pre + "q_codes"], A_HEADS), even_odd(a[pre + "k_codes"], KV_HEADS)
    qs, ks = even_odd(a[pre + "q_scales"], A_HEADS), even_odd(a[pre + "k_scales"], KV_HEADS)
    lora_a, lora_b = a["L0_ffn_lora_A"], a["L0_ffn_lora_B"]
    arrays = {
        "x": a[pre + "hidden_states"],
        "q_codes": by_group(q), "k_codes": by_group(k), "v_codes": by_group(a[pre + "v_codes"]),
        "o_codes": a[pre + "o_codes"].reshape(KV_HEADS, GROUP, P, D).transpose(0, 2, 1, 3),
        "q_scales": scales_by_group(qs), "k_scales": scales_by_group(ks),
        "v_scales": scales_by_group(a[pre + "v_scales"]), "o_scales": a[pre + "o_scales"].reshape(-1),
        "lora_a": tiles(lora_a.reshape(EXPERTS * RANK, D).T),
        "lora_b": tiles(lora_b.transpose(0, 2, 1).reshape(EXPERTS * RANK, D)),
        "b_q": tiles(a["L0_attn_b_Wq"]), "b_o": tiles(a["L0_attn_b_Wo"]),
        "b_kv": tiles(np.concatenate([a["L0_attn_b_Wk"], a["L0_attn_b_Wv"]], axis=1)),
        "gate": tiles(a["L0_ffn_gate_w"].T),
        **constants(),
    }
    nc = bacc.Bacc("TRN2", target_bir_lowering=False, num_devices=1)
    arrays = {f"in_{n}": np.ascontiguousarray(v) for n, v in arrays.items()}
    t_in = {n[3:]: nc.dram_tensor(n, v.shape, mybir.dt.from_np(v.dtype), kind="ExternalInput").ap()
            for n, v in arrays.items()}
    out = nc.dram_tensor("out", (B, S, D), F32, kind="ExternalOutput").ap()
    build(nc, t_in, out)
    r = run_bass_kernel_spmd(nc, [arrays], core_ids=[0])
    return r.results[0]["out"]
```
